# Optimizing a Trainium2 kernel written in Bass

```python
import numpy as np
import jax
import jax.numpy as jnp

def _softmax(x, axis=-1):
    return jax.nn.softmax(x, axis=axis)

def _gelu(x):
    return jax.nn.gelu(x, approximate=True)

def _silu(x):
    return jax.nn.silu(x)

def _sigmoid(x):
    return jax.nn.sigmoid(x)

def _layernorm(x, axis=-1, eps=1e-05):
    m = jnp.mean(x, axis=axis, keepdims=True)
    v = jnp.var(x, axis=axis, keepdims=True)
    return (x - m) / jnp.sqrt(v + eps)

def _scatter_add(tgt, idx, src, axis=0):
    return tgt.at[idx].add(src)

def _segment_sum(src, seg, n):
    return jax.ops.segment_sum(src, seg, n)
kernel_name = 'mk_xattn_ffn_d2_seqx_r8_354c93'

def setup_inputs(seed: int=0):
    np.random.seed(seed)
    _w = jnp.asarray

    def _rec_inputs():
        import jax
        import jax.numpy as jnp
        _rk = jax.random.key(seed)
        x = 7.22e-05 + 1 * jax.random.normal(jax.random.fold_in(_rk, 1), (8, 256, 128), jnp.float32)
        _lenS = 256 - jax.random.randint(jax.random.fold_in(_rk, 7), (8,), 0, max(1, 256 // 4) + 1, jnp.int32)
        _lenS2 = 512 - jax.random.randint(jax.random.fold_in(_rk, 8), (8,), 0, max(1, 512 // 4) + 1, jnp.int32)
        _ctx_1024P = jax.random.normal(jax.random.fold_in(_rk, 11), (8, 16, 128), jnp.float32)
        _ctx_1024c = jax.random.dirichlet(jax.random.fold_in(_rk, 511), 0.3 * jnp.ones((16,), jnp.float32), (8, 512))
        _ctx_1024t = jnp.einsum('bsk,bkd->bsd', _ctx_1024c, _ctx_1024P)
        _ctx_1024t = _ctx_1024t * jax.lax.rsqrt(jnp.mean(jnp.square(_ctx_1024t)) + 1e-12) * 0.953939
        ctx_1024 = 4.13588e-05 + 0.999923 * (_ctx_1024t + 0.3 * jax.random.normal(jax.random.fold_in(_rk, 611), (8, 512, 128), jnp.float32))
        _validS = jnp.arange(256)[None, :] < _lenS[:, None]
        _validS2 = jnp.arange(512)[None, :] < _lenS2[:, None]
        _causal = jnp.tril(jnp.ones((256, 256), dtype=bool))
        mask_Bx1x1xS2_ff0 = jnp.where(jnp.ones((8, 1, 1, 512), dtype=bool), 0.0, -1000000000.0).astype(jnp.float32)
        return (x, ctx_1024, mask_Bx1x1xS2_ff0)
    x, ctx_1024, mask_Bx1x1xS2_ff0 = _rec_inputs()

    def _L0_xattn_setup():
        import jax, jax.numpy as jnp
        import numpy as np
        B, S, D, H = (4, 256, 128, 16)
        DEPTH = D // H

        def _split_heads(x):
            b, s, _ = x.shape
            return x.reshape(b, s, H, DEPTH).transpose(0, 2, 1, 3)
        key = jax.random.key(seed)
        ks = jax.random.split(key, 12)
        s = 1.0 / np.sqrt(D)
        return {'q': jax.random.normal(ks[0], (B, S, D), jnp.float32), 'k': jax.random.normal(ks[1], (B, S, D), jnp.float32), 'v': jax.random.normal(ks[2], (B, S, D), jnp.float32), 'mask': jnp.zeros((B, 1, 1, S), jnp.float32), 'wq': jax.random.normal(ks[3], (D, D), jnp.float32) * s, 'bq': jnp.zeros((D,), jnp.float32), 'wk': jax.random.normal(ks[4], (D, D), jnp.float32) * s, 'bk': jnp.zeros((D,), jnp.float32), 'wv': jax.random.normal(ks[5], (D, D), jnp.float32) * s, 'bv': jnp.zeros((D,), jnp.float32), 'wo': jax.random.normal(ks[6], (D, D), jnp.float32) * s, 'bo': jnp.zeros((D,), jnp.float32)}
    _L0_xattn_all = _L0_xattn_setup()
    _L0_xattn_in = {k: v for k, v in _L0_xattn_all.items() if k in ('wq', 'bq', 'wk', 'bk', 'wv', 'bv', 'wo', 'bo')}
    del _L0_xattn_all

    def _L0_ffn_setup():
        import jax, jax.numpy as jnp
        import numpy as np
        N_EXPERTS = 32
        TOP_K = 8
        N_GROUP = 4
        TOPK_GROUP = 2
        ROUTED_SCALING = 2.5

        def _gate(x, gate_w, gate_bias):
            T, E = (x.shape[0], gate_w.shape[0])
            logits = jnp.einsum('th,eh->te', x, gate_w)
            scores = jax.nn.sigmoid(logits)
            scores_choice = scores + gate_bias[None, :]
            grp = scores_choice.reshape(T, N_GROUP, E // N_GROUP)
            top2, _ = jax.lax.top_k(grp, 2)
            group_scores = top2.sum(-1)
            _, grp_idx = jax.lax.top_k(group_scores, TOPK_GROUP)
            group_mask = jax.nn.one_hot(grp_idx, N_GROUP, dtype=scores.dtype).sum(1)
            expert_mask = jnp.repeat(group_mask, E // N_GROUP, axis=1)
            masked = jnp.where(expert_mask > 0, scores_choice, 0.0)
            _, topk_idx = jax.lax.top_k(masked, TOP_K)
            topk_w = jnp.take_along_axis(scores, topk_idx, axis=1)
            topk_w = topk_w / (topk_w.sum(-1, keepdims=True) + 1e-20)
            topk_w = topk_w * ROUTED_SCALING
            return (topk_idx, topk_w)

        def _mlp(x, wg, wu, wd):
            return jnp.einsum('...i,hi->...h', jax.nn.silu(jnp.einsum('...h,ih->...i', x, wg)) * jnp.einsum('...h,ih->...i', x, wu), wd)
        key = jax.random.key(seed)
        ks = jax.random.split(key, 9)
        B, S, H, I = (2, 64, 128, 64)
        w = 0.02
        return {'hidden_states': jax.random.normal(ks[0], (B, S, H), jnp.float32), 'gate_w': jax.random.normal(ks[1], (N_EXPERTS, H), jnp.float32) * w, 'gate_bias': jax.random.normal(ks[2], (N_EXPERTS,), jnp.float32) * w, 'expert_gate': jax.random.normal(ks[3], (N_EXPERTS, I, H), jnp.float32) * w, 'expert_up': jax.random.normal(ks[4], (N_EXPERTS, I, H), jnp.float32) * w, 'expert_down': jax.random.normal(ks[5], (N_EXPERTS, H, I), jnp.float32) * w, 'shared_gate': jax.random.normal(ks[6], (2 * I, H), jnp.float32) * w, 'shared_up': jax.random.normal(ks[7], (2 * I, H), jnp.float32) * w, 'shared_down': jax.random.normal(ks[8], (H, 2 * I), jnp.float32) * w}
    _L0_ffn_all = _L0_ffn_setup()
    _L0_ffn_in = {k: v for k, v in _L0_ffn_all.items() if k in ('gate_w', 'gate_bias', 'expert_gate', 'expert_up', 'expert_down', 'shared_gate', 'shared_up', 'shared_down')}
    del _L0_ffn_all

    def _L1_xattn_setup():
        import jax, jax.numpy as jnp
        import numpy as np
        D_MODEL = 128
        NUM_HEADS = 16
        HEAD_DIM = D_MODEL // NUM_HEADS
        SEQ = 512
        BATCH = 1
        ROPE_BASE = 10000.0

        def _rope_cos_sin(seq_len, head_dim, dtype):
            inv_freq = 1.0 / ROPE_BASE ** (jnp.arange(0, head_dim, 2, dtype=jnp.float32) / head_dim)
            pos = jnp.arange(seq_len, dtype=jnp.float32)
            freqs = pos[:, None] * inv_freq[None, :]
            emb = jnp.concatenate([freqs, freqs], axis=-1)
            return (jnp.cos(emb).astype(dtype), jnp.sin(emb).astype(dtype))

        def _rotate_half(x):
            d = x.shape[-1] // 2
            return jnp.concatenate([-x[..., d:], x[..., :d]], axis=-1)
        key = jax.random.key(seed)
        ks = jax.random.split(key, 11)
        s = 1.0 / np.sqrt(D_MODEL)
        return {'query': jax.random.normal(ks[0], (BATCH, SEQ, D_MODEL), jnp.float32), 'key': jax.random.normal(ks[1], (BATCH, SEQ, D_MODEL), jnp.float32), 'value': jax.random.normal(ks[2], (BATCH, SEQ, D_MODEL), jnp.float32), 'Wq': jax.random.normal(ks[3], (D_MODEL, D_MODEL), jnp.float32) * s, 'bq': jnp.zeros((D_MODEL,), jnp.float32), 'Wk': jax.random.normal(ks[4], (D_MODEL, D_MODEL), jnp.float32) * s, 'bk': jnp.zeros((D_MODEL,), jnp.float32), 'Wv': jax.random.normal(ks[5], (D_MODEL, D_MODEL), jnp.float32) * s, 'bv': jnp.zeros((D_MODEL,), jnp.float32), 'Wo': jax.random.normal(ks[6], (D_MODEL, D_MODEL), jnp.float32) * s, 'bo': jnp.zeros((D_MODEL,), jnp.float32)}
    _L1_xattn_all = _L1_xattn_setup()
    _L1_xattn_in = {k: v for k, v in _L1_xattn_all.items() if k in ('Wq', 'bq', 'Wk', 'bk', 'Wv', 'bv', 'Wo', 'bo')}
    del _L1_xattn_all

    def _L1_ffn_setup():
        import jax, jax.numpy as jnp
        import numpy as np
        B, S, D, E, F, K = (4, 128, 128, 8, 352, 1)
        key = jax.random.key(seed)
        ks = jax.random.split(key, 8)
        sc = 0.02
        return {'x_bsD': jax.random.normal(ks[0], (B, S, D), jnp.float32), 'router_DE': jax.random.normal(ks[1], (D, E), jnp.float32) * sc, 'w1_eDF': jax.random.normal(ks[2], (E, D, F), jnp.float32) * sc, 'w3_eDF': jax.random.normal(ks[3], (E, D, F), jnp.float32) * sc, 'w2_eFD': jax.random.normal(ks[4], (E, F, D), jnp.float32) * sc, 'ws1_DF': jax.random.normal(ks[5], (D, F), jnp.float32) * sc, 'ws3_DF': jax.random.normal(ks[6], (D, F), jnp.float32) * sc, 'ws2_FD': jax.random.normal(ks[7], (F, D), jnp.float32) * sc}
    _L1_ffn_all = _L1_ffn_setup()
    _L1_ffn_in = {k: v for k, v in _L1_ffn_all.items() if k in ('router_DE', 'w1_eDF', 'w3_eDF', 'w2_eFD', 'ws1_DF', 'ws3_DF', 'ws2_FD')}
    del _L1_ffn_all
    return {'x': x, 'ctx_1024': ctx_1024, 'mask_Bx1x1xS2_ff0': mask_Bx1x1xS2_ff0, 'L0_xattn_wq': _L0_xattn_in['wq'], 'L0_xattn_bq': _L0_xattn_in['bq'], 'L0_xattn_wk': _L0_xattn_in['wk'], 'L0_xattn_bk': _L0_xattn_in['bk'], 'L0_xattn_wv': _L0_xattn_in['wv'], 'L0_xattn_bv': _L0_xattn_in['bv'], 'L0_xattn_wo': _L0_xattn_in['wo'], 'L0_xattn_bo': _L0_xattn_in['bo'], 'L0_ffn_gate_w': _L0_ffn_in['gate_w'], 'L0_ffn_gate_bias': _L0_ffn_in['gate_bias'], 'L0_ffn_expert_gate': _L0_ffn_in['expert_gate'], 'L0_ffn_expert_up': _L0_ffn_in['expert_up'], 'L0_ffn_expert_down': _L0_ffn_in['expert_down'], 'L0_ffn_shared_gate': _L0_ffn_in['shared_gate'], 'L0_ffn_shared_up': _L0_ffn_in['shared_up'], 'L0_ffn_shared_down': _L0_ffn_in['shared_down'], 'L1_xattn_Wq': _L1_xattn_in['Wq'], 'L1_xattn_bq': _L1_xattn_in['bq'], 'L1_xattn_Wk': _L1_xattn_in['Wk'], 'L1_xattn_bk': _L1_xattn_in['bk'], 'L1_xattn_Wv': _L1_xattn_in['Wv'], 'L1_xattn_bv': _L1_xattn_in['bv'], 'L1_xattn_Wo': _L1_xattn_in['Wo'], 'L1_xattn_bo': _L1_xattn_in['bo'], 'L1_ffn_router_DE': _L1_ffn_in['router_DE'], 'L1_ffn_w1_eDF': _L1_ffn_in['w1_eDF'], 'L1_ffn_w3_eDF': _L1_ffn_in['w3_eDF'], 'L1_ffn_w2_eFD': _L1_ffn_in['w2_eFD'], 'L1_ffn_ws1_DF': _L1_ffn_in['ws1_DF'], 'L1_ffn_ws3_DF': _L1_ffn_in['ws3_DF'], 'L1_ffn_ws2_FD': _L1_ffn_in['ws2_FD']}

def reference(x, ctx_1024, mask_Bx1x1xS2_ff0, L0_xattn_wq, L0_xattn_bq, L0_xattn_wk, L0_xattn_bk, L0_xattn_wv, L0_xattn_bv, L0_xattn_wo, L0_xattn_bo, L0_ffn_gate_w, L0_ffn_gate_bias, L0_ffn_expert_gate, L0_ffn_expert_up, L0_ffn_expert_down, L0_ffn_shared_gate, L0_ffn_shared_up, L0_ffn_shared_down, L1_xattn_Wq, L1_xattn_bq, L1_xattn_Wk, L1_xattn_bk, L1_xattn_Wv, L1_xattn_bv, L1_xattn_Wo, L1_xattn_bo, L1_ffn_router_DE, L1_ffn_w1_eDF, L1_ffn_w3_eDF, L1_ffn_w2_eFD, L1_ffn_ws1_DF, L1_ffn_ws3_DF, L1_ffn_ws2_FD):
    import jax
    import jax.numpy as jnp

    def _L0_xattn_ref(q, k, v, mask, wq, bq, wk, bk, wv, bv, wo, bo):
        import jax, jax.numpy as jnp
        import numpy as np
        B, S, D, H = (4, 256, 128, 16)
        DEPTH = D // H

        def _split_heads(x):
            b, s, _ = x.shape
            return x.reshape(b, s, H, DEPTH).transpose(0, 2, 1, 3)
        qh = _split_heads(q @ wq + bq)
        kh = _split_heads(k @ wk + bk)
        vh = _split_heads(v @ wv + bv)
        scale = 1.0 / jnp.sqrt(jnp.asarray(DEPTH, jnp.float32))
        logits = jnp.einsum('bhqd,bhkd->bhqk', qh, kh) * scale
        logits = logits + mask * -1000000000.0
        attn = jax.nn.softmax(logits, axis=-1)
        out = jnp.einsum('bhqk,bhkd->bhqd', attn, vh)
        out = out.transpose(0, 2, 1, 3).reshape(q.shape[0], -1, D)
        return out @ wo + bo

    def _L0_ffn_ref(hidden_states, gate_w, gate_bias, expert_gate, expert_up, expert_down, shared_gate, shared_up, shared_down):
        import jax, jax.numpy as jnp
        import numpy as np
        N_EXPERTS = 32
        TOP_K = 8
        N_GROUP = 4
        TOPK_GROUP = 2
        ROUTED_SCALING = 2.5

        def _gate(x, gate_w, gate_bias):
            T, E = (x.shape[0], gate_w.shape[0])
            logits = jnp.einsum('th,eh->te', x, gate_w)
            scores = jax.nn.sigmoid(logits)
            scores_choice = scores + gate_bias[None, :]
            grp = scores_choice.reshape(T, N_GROUP, E // N_GROUP)
            top2, _ = jax.lax.top_k(grp, 2)
            group_scores = top2.sum(-1)
            _, grp_idx = jax.lax.top_k(group_scores, TOPK_GROUP)
            group_mask = jax.nn.one_hot(grp_idx, N_GROUP, dtype=scores.dtype).sum(1)
            expert_mask = jnp.repeat(group_mask, E // N_GROUP, axis=1)
            masked = jnp.where(expert_mask > 0, scores_choice, 0.0)
            _, topk_idx = jax.lax.top_k(masked, TOP_K)
            topk_w = jnp.take_along_axis(scores, topk_idx, axis=1)
            topk_w = topk_w / (topk_w.sum(-1, keepdims=True) + 1e-20)
            topk_w = topk_w * ROUTED_SCALING
            return (topk_idx, topk_w)

        def _mlp(x, wg, wu, wd):
            return jnp.einsum('...i,hi->...h', jax.nn.silu(jnp.einsum('...h,ih->...i', x, wg)) * jnp.einsum('...h,ih->...i', x, wu), wd)
        orig_shape = hidden_states.shape
        H = orig_shape[-1]
        residuals = hidden_states
        x = hidden_states.reshape(-1, H)
        topk_idx, topk_w = _gate(x, gate_w, gate_bias)
        g = jnp.einsum('th,eih->eti', x, expert_gate)
        u = jnp.einsum('th,eih->eti', x, expert_up)
        outs = jnp.einsum('eti,ehi->eth', jax.nn.silu(g) * u, expert_down)
        outs_t = jnp.transpose(outs, (1, 0, 2))
        gathered = jnp.take_along_axis(outs_t, topk_idx[:, :, None], axis=1)
        final = (gathered * topk_w[:, :, None]).sum(1)
        shared = _mlp(residuals, shared_gate, shared_up, shared_down)
        return final.reshape(orig_shape) + shared

    def _L1_xattn_ref(query, key, value, Wq, bq, Wk, bk, Wv, bv, Wo, bo):
        import jax, jax.numpy as jnp
        import numpy as np
        D_MODEL = 128
        NUM_HEADS = 16
        HEAD_DIM = D_MODEL // NUM_HEADS
        SEQ = 512
        BATCH = 1
        ROPE_BASE = 10000.0

        def _rope_cos_sin(seq_len, head_dim, dtype):
            inv_freq = 1.0 / ROPE_BASE ** (jnp.arange(0, head_dim, 2, dtype=jnp.float32) / head_dim)
            pos = jnp.arange(seq_len, dtype=jnp.float32)
            freqs = pos[:, None] * inv_freq[None, :]
            emb = jnp.concatenate([freqs, freqs], axis=-1)
            return (jnp.cos(emb).astype(dtype), jnp.sin(emb).astype(dtype))

        def _rotate_half(x):
            d = x.shape[-1] // 2
            return jnp.concatenate([-x[..., d:], x[..., :d]], axis=-1)
        B, Sq, _ = query.shape
        Skv = key.shape[1]
        H, Dh = (NUM_HEADS, HEAD_DIM)
        q = (query @ Wq.T + bq).reshape(B, Sq, H, Dh)
        k = (key @ Wk.T + bk).reshape(B, Skv, H, Dh)
        v = (value @ Wv.T + bv).reshape(B, Skv, H, Dh)
        cos, sin = _rope_cos_sin(max(Sq, Skv), Dh, query.dtype)
        cq, sq_ = (cos[None, :Sq, None, :], sin[None, :Sq, None, :])
        ck, sk_ = (cos[None, :Skv, None, :], sin[None, :Skv, None, :])
        q = q * cq + _rotate_half(q) * sq_
        k = k * ck + _rotate_half(k) * sk_
        scale = 1.0 / np.sqrt(Dh)
        scores = jnp.einsum('bqhd,bkhd->bhqk', q, k) * scale
        probs = jax.nn.softmax(scores, axis=-1)
        ctx = jnp.einsum('bhqk,bkhd->bqhd', probs, v).reshape(B, Sq, H * Dh)
        return ctx @ Wo.T + bo

    def _L1_ffn_ref(x_bsD, router_DE, w1_eDF, w3_eDF, w2_eFD, ws1_DF, ws3_DF, ws2_FD):
        import jax, jax.numpy as jnp
        import numpy as np
        B, S, D, E, F, K = (4, 128, 128, 8, 352, 1)
        b, s, d = x_bsD.shape
        a = b * s
        x_aD = x_bsD.reshape(a, d)
        scores_aE = x_aD @ router_DE
        vals_aK, idx_aK = jax.lax.top_k(scores_aE, K)
        masked_aE = jnp.full_like(scores_aE, -jnp.inf).at[jnp.arange(a)[:, None], idx_aK].set(vals_aK)
        gates_Ea = jax.nn.sigmoid(masked_aE).T
        routed_in_EaD = jax.lax.stop_gradient(gates_Ea[:, :, None] * x_aD[None, :, :])
        mid_EaF = jax.nn.silu(jnp.einsum('ead,edf->eaf', routed_in_EaD, w1_eDF)) * jnp.einsum('ead,edf->eaf', routed_in_EaD, w3_eDF)
        routed_out_EaD = jnp.einsum('eaf,efd->ead', mid_EaF, w2_eFD)
        shared_aD = jax.nn.silu(x_aD @ ws1_DF) * (x_aD @ ws3_DF) @ ws2_FD
        out_aD = shared_aD + routed_out_EaD.sum(axis=0)
        return out_aD.reshape(b, s, d)
    x = x + _L0_xattn_ref(_layernorm(x, axis=-1), ctx_1024, ctx_1024, mask_Bx1x1xS2_ff0, L0_xattn_wq, L0_xattn_bq, L0_xattn_wk, L0_xattn_bk, L0_xattn_wv, L0_xattn_bv, L0_xattn_wo, L0_xattn_bo)
    x = x + _L0_ffn_ref(_layernorm(x, axis=-1), L0_ffn_gate_w, L0_ffn_gate_bias, L0_ffn_expert_gate, L0_ffn_expert_up, L0_ffn_expert_down, L0_ffn_shared_gate, L0_ffn_shared_up, L0_ffn_shared_down)
    x = x + _L1_xattn_ref(_layernorm(x, axis=-1), ctx_1024, ctx_1024, L1_xattn_Wq, L1_xattn_bq, L1_xattn_Wk, L1_xattn_bk, L1_xattn_Wv, L1_xattn_bv, L1_xattn_Wo, L1_xattn_bo)
    x = x + _L1_ffn_ref(_layernorm(x, axis=-1), L1_ffn_router_DE, L1_ffn_w1_eDF, L1_ffn_w3_eDF, L1_ffn_w2_eFD, L1_ffn_ws1_DF, L1_ffn_ws3_DF, L1_ffn_ws2_FD)
    return x

_drawn_inputs = setup_inputs


def setup_inputs(seed=0):
    import zlib

    import numpy as np

    out = dict(_drawn_inputs(seed))
    spreads = {'L0_xattn_bq': (0.0, 0.395),
     'L0_xattn_bk': (0.0, 0.8),
     'L0_xattn_bv': (0.0, 0.1),
     'L0_xattn_bo': (0.0, 0.1),
     'L1_xattn_bq': (0.0, 0.608),
     'L1_xattn_bk': (0.0, 0.8),
     'L1_xattn_bv': (0.0, 0.1),
     'L1_xattn_bo': (0.0, 0.1)}
    factors = {'L0_ffn_gate_w': 8.0,
     'L0_ffn_gate_bias': 8.0,
     'L0_ffn_expert_gate': 8.0,
     'L0_ffn_expert_up': 8.0,
     'L0_ffn_expert_down': 8.0,
     'L0_ffn_shared_gate': 8.0,
     'L0_ffn_shared_up': 8.0,
     'L0_ffn_shared_down': 8.0,
     'L1_ffn_router_DE': 8.0,
     'L1_ffn_w1_eDF': 8.0,
     'L1_ffn_w3_eDF': 8.0,
     'L1_ffn_w2_eFD': 8.0,
     'L1_ffn_ws1_DF': 7.263,
     'L1_ffn_ws3_DF': 7.228,
     'L1_ffn_ws2_FD': 7.265}
    for name, (base, spread) in spreads.items():
        noise = np.random.default_rng([zlib.crc32(name.encode()), seed]).standard_normal(out[name].shape)
        drawn = base * np.exp(spread * noise) if base else spread * noise
        out[name] = jnp.asarray(drawn.astype(out[name].dtype))
    for name, factor in factors.items():
        out[name] = (out[name] * factor).astype(out[name].dtype)
    return out
```

```python
import math
from contextlib import ExitStack

import concourse.bass as bass
from concourse import mybir

FP32 = mybir.dt.float32
F32R = mybir.dt.float32r
BF16 = mybir.dt.bfloat16
ALU = mybir.AluOpType
ACT = mybir.ActivationFunctionType
AX = mybir.AxisListType

P = 128
B, SQ, SK, D, H = 8, 256, 512, 128, 16
HD = D // H
PAIRS = H // 2
T = B * SQ
TT = T // P
QT = SQ // P
KC = SK // P
CT = B * KC
EPS = 1e-5
SCALE = 1.0 / math.sqrt(HD)
TERMS = [(0, 0), (0, 1), (1, 0), (0, 2), (2, 0), (1, 1)]
HROWS = HD * len(TERMS)
MASK_ROW = 2 * HROWS
MAX_ROW = MASK_ROW + 3
STACK = MAX_ROW + 3
VC = HD + 1
E0, I0, GROUPS = 32, 64, 4
EP = E0 // 2
E1, F1 = 8, 352
FC = [(0, 128), (128, 128), (256, 96)]
BLK = 512
NB = T // BLK
BIG = 1e30


class Queue:

    def __init__(self, engine, sem):
        self.engine, self.sem, self.count, self.seen = engine, sem, 0, {}

    def after(self, *events):
        for event in events:
            if event is None:
                continue
            if isinstance(event, list):
                self.after(*event)
                continue
            sem, value = event
            if self.seen.get(sem.name, 0) < value:
                self.engine.wait_ge(sem, value)
                self.seen[sem.name] = value

    def run(self, instruction):
        instruction.then_inc(self.sem, 1)
        self.count += 1
        return self.sem, self.count


class Transfers:

    def __init__(self, sem):
        self.sem, self.count = sem, 0

    def start(self, queue, out, in_):
        queue.engine.dma_start(out, in_).then_inc(self.sem, 16)
        self.count += 16
        return self.sem, self.count


def build(nc, A, out):
    stack = ExitStack()
    with stack:
        def sem(name):
            return stack.enter_context(nc.semaphore(name))

        def sbuf(name, shape, dt, scope=stack):
            return scope.enter_context(nc.sbuf_tensor(name, shape, dt))

        pe = Queue(nc.tensor, sem("pe_done"))
        act = Queue(nc.scalar, sem("act_done"))
        dve = Queue(nc.vector, sem("dve_done"))
        pool = Queue(nc.gpsimd, sem("pool_done"))
        sp = Queue(nc.sync, sem("sp_done"))
        engines = (pe, act, dve, pool, sp)

        def transfers(name):
            return Transfers(sem(name))

        x = sbuf("x", [P, TT, D], FP32)
        ident = sbuf("ident", [P, P], FP32)
        ident16 = sbuf("ident16", [P, P], BF16)
        order = sbuf("order", [P, 16 + E1], FP32)
        actT = sbuf("actT", [P, 2, CT * P], F32R)
        aw = sbuf("aw", [P, 5, 2, D], F32R)
        wo = sbuf("wo", [P, D], FP32)
        col = sbuf("col", [P, 4], FP32)
        bv = sbuf("bv", [P, D], FP32)
        bo = sbuf("bo", [P, D], FP32)
        stats = sbuf("stats", [P, TT, 6], FP32)
        mv = sbuf("mv", [P, TT, 2], FP32)
        rstd = sbuf("rstd", [P, 3, TT], FP32)
        xn = sbuf("xn", [P, 4, D], FP32)

        scope = ExitStack()
        kparts = sbuf("kparts", [P, 3, B * SK], BF16, scope)
        qparts = sbuf("qparts", [P, 3, T], BF16, scope)
        vaug = sbuf("vaug", [P, CT, H * VC + 23], FP32, scope)
        kstack = [sbuf(f"kstack{i}", [P, PAIRS, SK], BF16, scope) for i in range(3)]
        qstack = [sbuf(f"qstack{i}", [P, H, SQ], BF16, scope) for i in range(3)]
        prep = ExitStack()
        ctx_nat = sbuf("ctx_nat", [P, 4, 1024], FP32, prep)
        wnat = sbuf("wnat", [P, 5, D], FP32, prep)
        rope = sbuf("rope", [P, 2, SK], FP32, prep)
        work = sbuf("work", [P, 4, SK], FP32, prep)
        mask8 = sbuf("mask8", [B, 2, SK], FP32, prep)
        prep.close()
        prob = sbuf("prob", [P, 2, 2, KC, 2 * SQ], FP32, scope)
        oT = sbuf("oT", [P, 2, 2, 2 * SQ], FP32, scope)
        o_norm = sbuf("o_norm", [P, 2, D], FP32, scope)
        o_normT = sbuf("o_normT", [P, 2, D], FP32, scope)
        rsum = sbuf("rsum", [P, 2, H], FP32, scope)
        negmax = sbuf("negmax", [P, 2, H, QT], FP32, scope)
        mrest = sbuf("mrest", [P, QT, H // 2], FP32, scope)
        mparts = sbuf("mparts", [P, 2, QT, 3, H // 2], BF16, scope)
        mT = sbuf("mT", [24, 2, SQ], BF16, scope)
        maskp = sbuf("maskp", [B, 3, SK], BF16, scope)
        scope.close()

        ffn0 = ExitStack()
        e_nat = sbuf("e_nat", [P, EP + 1, 2, D], FP32, ffn0)
        gu0 = sbuf("gu0", [P, EP + 1, 2, 2, D], F32R, ffn0)
        down0 = sbuf("down0", [P, EP + 1, D], FP32, ffn0)
        gw_nat = sbuf("gw_nat", [P, E0], FP32, ffn0)
        gate_bias = sbuf("gate_bias", [P, E0], FP32, ffn0)
        sel0f = sbuf("sel0f", [96, EP, P], FP32, ffn0)
        sel0 = sbuf("sel0", [96, EP, P], BF16, ffn0)
        ffn0.close()
        ffn1 = ExitStack()
        w_nat = sbuf("w_nat", [P, E1 + 1, 2, F1], FP32, ffn1)
        gu1 = sbuf("gu1", [P, E1 + 1, 2, 2, F1], F32R, ffn1)
        down1 = sbuf("down1", [P, E1 + 1, 3, D], FP32, ffn1)
        sel1f = sbuf("sel1f", [96, E1, P], FP32, ffn1)
        sel1 = sbuf("sel1", [96, E1, P], BF16, ffn1)
        gated = sbuf("gated", [P, 2, 2, BLK], F32R, ffn1)
        gatedf = sbuf("gatedf", [P, BLK], FP32, ffn1)
        route = sbuf("route", [P, 8, TT, E0], FP32, ffn1)
        small = sbuf("small", [P, 6, TT, 16], FP32, ffn1)
        wparts = sbuf("wparts", [P, TT, 3, E0], BF16, ffn1)
        wT = sbuf("wT", [96, T], BF16, ffn1)
        rt_w = sbuf("rt_w", [P, 2, E0], F32R, ffn1)
        silu = sbuf("silu", [P, 2, BLK], FP32, ffn1)
        prod = sbuf("prod", [P, 2, BLK], FP32, ffn1)
        hid = sbuf("hid", [P, 3, BLK], FP32, ffn1)
        yT = sbuf("yT", [P, 2, BLK], FP32, ffn1)
        ffn1.close()

        def psum(name, banks):
            return stack.enter_context(nc.psum_tensor(name, [P, 512 * banks], FP32))

        s_bank = [psum("s_bank0", 1), psum("s_bank1", 1)]
        t_bank = [psum("t_bank0", 2), psum("t_bank1", 2)]
        o_bank = psum("o_bank", 1)
        m_bank = psum("m_bank", 1)
        bank = [s_bank[0][:, :], s_bank[1][:, :], t_bank[0][:, 0:512], t_bank[0][:, 512:1024],
                t_bank[1][:, 0:512], t_bank[1][:, 512:1024], o_bank[:, :], m_bank[:, :]]
        free = [None] * 8

        def everybody():
            ends = [(q.sem, q.count) for q in engines if q.count]
            for q in engines:
                q.after(*ends)

        def parts3(hi, whi, wlo, xhi, xlo):
            nc.tensor.matmul(hi, whi, xhi, start=True, stop=False)
            nc.tensor.matmul(hi, whi, xlo, start=False, stop=False)
            return pe.run(nc.tensor.matmul(hi, wlo, xhi, start=False, stop=True))

        def split(src, hi, lo, ready):
            act.after(ready)
            a = act.run(nc.scalar.activation(hi, src, ACT.Copy))
            dve.after(ready, a)
            return dve.run(nc.vector.tensor_tensor(lo, src, hi.bitcast(FP32), ALU.subtract))

        ld_x, ld_const, ld_w = transfers("ld_x"), transfers("ld_const"), transfers("ld_w")
        ld_ctx = [transfers(f"ld_ctx{i}") for i in range(4)]
        x_ready = ld_x.start(sp, x[:, :, :], A["x"])
        ld_const.start(act, ident[:, :], A["c_ident"])
        const_ready = ld_const.start(act, order[:, :], A["c_order"])
        dve.after(const_ready)
        ident_ready = dve.run(nc.vector.tensor_copy(ident16[:, :], ident[:, :]))
        exponent = dve.run(nc.vector.memset(rstd[:, 1, :], -0.5))

        ld_k = [transfers(f"ld_k{i}") for i in range(3)]
        ld_q = [transfers(f"ld_q{i}") for i in range(3)]
        ld_m = [transfers(f"ld_m{i}") for i in range(2)]
        ld_mask = transfers("ld_mask")

        def layernorm(done_x):
            steps = []
            for g in range(NB):
                dve.after(done_x)
                tiles = range(4 * g, 4 * g + 4)
                for t in tiles:
                    e = dve.run(nc.vector.bn_stats(stats[:, t, :], x[:, t, :]))
                dve.after(e)
                for t in tiles:
                    e = dve.run(nc.vector.bn_aggr(mv[:, t, :], stats[:, t, :]))
                dve.after(e)
                e = dve.run(nc.vector.tensor_scalar(rstd[:, 0, 4 * g:4 * g + 4], mv[:, 4 * g:4 * g + 4, 1],
                                                    EPS, None, ALU.add))
                pool.after(e, exponent)
                steps.append(pool.run(nc.gpsimd.tensor_tensor(
                    rstd[:, 2, 4 * g:4 * g + 4], rstd[:, 0, 4 * g:4 * g + 4], rstd[:, 1, 4 * g:4 * g + 4], ALU.pow)))
            out_events, was_read = [], None
            for g in range(NB):
                dve.after(steps[g], was_read)
                for i in range(4):
                    t = 4 * g + i
                    e = dve.run(nc.vector.tensor_scalar(xn[:, i, :], x[:, t, :], mv[:, t, 0:1],
                                                        rstd[:, 2, t:t + 1], ALU.subtract, ALU.mult))
                n = g % 2
                pe.after(e, free[n], ident_ready, const_ready)
                for i in range(4):
                    was_read = pe.run(nc.tensor.transpose(bank[n][:, i * P:(i + 1) * P], xn[:, i, :], ident[:, :]))
                free[n] = split(bank[n], actT[:, 0, g * BLK:(g + 1) * BLK], actT[:, 1, g * BLK:(g + 1) * BLK], was_read)
                out_events.append(free[n])
            return out_events, e

        def xattn(layer, x_done):
            pre = f"L{layer}_"
            rope_on = layer == 1
            kinds = 4 if rope_on else 2
            w_ready = ld_w.start(sp, wnat[:, :, :], A[pre + "w"])
            w_ready = ld_w.start(sp, wo[:, :], A[pre + "wo"])
            w_ready = ld_w.start(sp, col[:, :], A[pre + "b"])
            w_ready = ld_w.start(sp, bv[:, :], A[pre + "bv"].partition_broadcast(P))
            w_ready = ld_w.start(sp, bo[:, :], A[pre + "bo"].partition_broadcast(P))
            if rope_on:
                w_ready = ld_w.start(sp, rope[:, :, :], A["c_rope"])
            else:
                w_ready = ld_w.start(sp, mask8[:, 0, :], A["mask"])
            ctx_ready = [ld_ctx[h].start(sp, ctx_nat[:, h, :], A["ctxT"][:, h * 1024:(h + 1) * 1024]) for h in range(4)]

            dve.after(w_ready)
            act.after(w_ready)
            e = dve.run(nc.vector.tensor_scalar(wnat[:, 0:kinds:2, :], wnat[:, 0:kinds:2, :], SCALE, None, ALU.mult))
            e2 = dve.run(nc.vector.tensor_scalar(col[:, 0:kinds:2], col[:, 0:kinds:2], SCALE, None, ALU.mult))
            dve.after(e2)
            aw_ready = split(wnat[:, :, :], aw[:, :, 0, :], aw[:, :, 1, :], e)

            e = None
            for i in range(3):
                for rows in (qstack[i][0:96, :, :], qstack[i][96:128, :, :], kstack[i][96:128, :, :]):
                    pool.after(e)
                    e = pool.run(nc.gpsimd.memset(rows, 0.0 if rows.shape[0] == 96 else 1.0))
            pool.after(e)
            stacks_set = e
            v_set = pool.run(nc.gpsimd.memset(vaug[:, :, :], 1.0))
            pool.after(v_set)

            if layer == 0:
                e = dve.run(nc.vector.tensor_scalar(mask8[:, 0, :], mask8[:, 0, :], -1e9, None, ALU.mult))
                for i in range(3):
                    dve.after(e)
                    e = dve.run(nc.vector.tensor_copy(maskp[:, i, :], mask8[:, i % 2, :]))
                    if i < 2:
                        dve.after(e)
                        e = dve.run(nc.vector.tensor_tensor(mask8[:, 1 - i % 2, :], mask8[:, i % 2, :], maskp[:, i, :], ALU.subtract))
            else:
                e = dve.run(nc.vector.memset(maskp[:, :, :], 0.0))
            mask_ready = e

            ctxT_ready = [split(ctx_nat[:, g // 2, g % 2 * SK:(g % 2 + 1) * SK], actT[:, 0, g * SK:(g + 1) * SK],
                                actT[:, 1, g * SK:(g + 1) * SK], ctx_ready[g // 2]) for g in range(B)]

            def project(which, block, parts, ready, work_read):
                n = 2 + 2 * (block % 2)
                cols = slice(block * 512, (block + 1) * 512)
                wk_ = work[:, 2 * (block % 2), :]
                wk2 = work[:, 2 * (block % 2) + 1, :]
                pe.after(ready, aw_ready, free[n], free[n + 1])
                e = parts3(bank[n], aw[:, which, 0, :], aw[:, which, 1, :], actT[:, 0, cols], actT[:, 1, cols])
                if not rope_on:
                    act.after(e)
                    a = act.run(nc.scalar.activation(parts[:, 0, cols], bank[n], ACT.Identity, bias=col[:, which:which + 1]))
                    dve.after(a, work_read)
                    r = dve.run(nc.vector.scalar_tensor_tensor(wk_, bank[n], col[:, which:which + 1], parts[:, 0, cols],
                                                               ALU.add, ALU.subtract))
                    free[n] = r
                else:
                    e2 = parts3(bank[n + 1], aw[:, 2 + which, 0, :], aw[:, 2 + which, 1, :], actT[:, 0, cols], actT[:, 1, cols])
                    dve.after(e, work_read)
                    if which == 0:
                        shape = [P, 2, SQ]
                        cos = rope[:, 0:1, 0:SQ].to_broadcast(shape)
                        sin = rope[:, 1:2, 0:SQ].to_broadcast(shape)
                        v = lambda ap: ap.rearrange("p (a n) -> p a n", a=2)
                    else:
                        cos, sin, v = rope[:, 0, :], rope[:, 1, :], lambda ap: ap
                    t1 = dve.run(nc.vector.scalar_tensor_tensor(v(wk_), v(bank[n]), col[:, which:which + 1], cos, ALU.add, ALU.mult))
                    dve.after(e2)
                    t2 = dve.run(nc.vector.scalar_tensor_tensor(v(wk2), v(bank[n + 1]), col[:, 2 + which:3 + which], sin, ALU.add, ALU.mult))
                    free[n], free[n + 1] = t1, t2
                    dve.after(t2)
                    e = dve.run(nc.vector.tensor_tensor(wk2, wk_, wk2, ALU.add))
                    act.after(e)
                    a = act.run(nc.scalar.activation(parts[:, 0, cols], wk2, ACT.Copy))
                    pool.after(a)
                    r = pool.run(nc.gpsimd.tensor_tensor(wk_, wk2, parts[:, 0, cols], ALU.subtract))
                act.after(r)
                a = act.run(nc.scalar.activation(parts[:, 1, cols], wk_, ACT.Copy))
                pool.after(a, r)
                return pool.run(nc.gpsimd.tensor_tensor(parts[:, 2, cols], wk_, parts[:, 1, cols], ALU.subtract))

            last = [None, None]
            k_ready = []
            for g in range(B):
                last[g % 2] = project(1, g, kparts, ctxT_ready[g], last[g % 2])
                k_ready.append(last[g % 2])
                n = 6 + g % 2
                pe.after(free[n])
                for c in range(KC):
                    tok = slice((KC * g + c) * P, (KC * g + c + 1) * P)
                    e = parts3(bank[n][:, c * P:(c + 1) * P], actT[:, 0, tok], actT[:, 1, tok], aw[:, 4, 0, :], aw[:, 4, 1, :])
                dve.after(e, v_set, w_ready)
                free[n] = dve.run(nc.vector.tensor_tensor(
                    vaug[:, KC * g:KC * (g + 1), 0:H * VC].rearrange("p c (h v) -> p c h v", v=VC)[:, :, :, 0:HD],
                    bank[n].rearrange("p (c h v) -> p c h v", c=KC, v=HD),
                    bv[:, :].rearrange("p (h v) -> p h v", v=HD).unsqueeze(1).to_broadcast([P, KC, H, HD]), ALU.add))
                v_ready = free[n]
            dve.after((pe.sem, pe.count))
            act.after((pe.sem, pe.count))
            xT_ready, x_read = layernorm(x_done)
            q_ready = []
            for blk in range(NB):
                last[blk % 2] = project(0, blk, qparts, xT_ready[blk], last[blk % 2])
                q_ready += [last[blk % 2]] * (BLK // SQ)
            pool.after(x_read, w_ready)
            x_plus = pool.run(nc.gpsimd.tensor_tensor(x[:, :, :], x[:, :, :], bo[:, :].unsqueeze(1).to_broadcast([P, TT, D]), ALU.add))
            everybody()

            mask_rows = MAX_ROW if layer == 0 else MASK_ROW
            k_loaded, q_loaded, m_loaded, stack_read = {}, {}, {}, {}

            def load_stacks(b):
                i = b % 3
                sp.after(k_ready[b], q_ready[b], stacks_set, mask_ready, stack_read.get(b - 3))
                for n, (qp, kp) in enumerate(TERMS):
                    for r in range(2):
                        row = HROWS * r + HD * n
                        k_loaded[b] = ld_k[i].start(sp, kstack[i][row:row + HD, :, :],
                                                    kparts[64 * r:64 * r + 64, kp, b * SK:(b + 1) * SK])
                        q_loaded[b] = ld_q[i].start(sp, qstack[i][row:row + HD, r::2, :],
                                                    qparts[64 * r:64 * r + 64, qp, b * SQ:(b + 1) * SQ])
                for m in range(3):
                    k_loaded[b] = ld_k[i].start(sp, kstack[i][MASK_ROW + m:MASK_ROW + m + 1, :, :],
                                                maskp[b:b + 1, m:m + 1, :].to_broadcast([1, PAIRS, SK]))

            s_free, s_count = [None, None], 0
            s_last = {}

            def scores_max(b, h, qt):
                nonlocal s_count
                n = s_count % 2
                s_count += 1
                i = b % 3
                pe.after(k_loaded[b], q_loaded[b], free[n])
                e = pe.run(nc.tensor.matmul(bank[n], qstack[i][0:mask_rows, h, qt * P:(qt + 1) * P],
                                            kstack[i][0:mask_rows, h // 2, :], start=True, stop=True))
                dve.after(e)
                free[n] = dve.run(nc.vector.tensor_reduce(negmax[:, b % 2, h, qt:qt + 1], bank[n], AX.X, ALU.max, negate=True))
                s_last[b, h // 8] = free[n]

            mT_event = {}

            def max_parts(b, half):
                hs = slice(8 * half, 8 * half + 8)
                nm = negmax[:, b % 2, hs, :].rearrange("p h q -> p q h")
                mp = mparts[:, half]
                dve.after(s_last[b, half])
                e = dve.run(nc.vector.tensor_copy(mp[:, :, 0, :], nm))
                dve.after(e)
                e = dve.run(nc.vector.tensor_tensor(mrest[:, :, :], nm, mp[:, :, 0, :], ALU.subtract))
                dve.after(e)
                e = dve.run(nc.vector.tensor_copy(mp[:, :, 1, :], mrest[:, :, :]))
                dve.after(e)
                mT_event[b, half] = dve.run(nc.vector.tensor_tensor(mp[:, :, 2, :], mrest[:, :, :], mp[:, :, 1, :], ALU.subtract))

            def max_rows(b, half):
                m16 = m_bank[:, :].bitcast(BF16)
                pe.after(mT_event[b, half], free[7])
                for qt in range(QT):
                    e = pe.run(nc.tensor.transpose(m16[0:24, qt * P:(qt + 1) * P],
                                                   mparts[:, half, qt].rearrange("p j h -> p (j h)"), ident16[:, :]))
                dve.after(e, m_loaded.get((b - 1, half)))
                free[7] = e = dve.run(nc.vector.tensor_copy(mT[:, half, :], m16[0:24, 0:SQ]))
                sp.after(e)
                m_loaded[b, half] = ld_m[half].start(sp, qstack[b % 3][MAX_ROW:MAX_ROW + 3, 8 * half:8 * half + 8, :], mT[:, half, :])

            t_count = 0
            exp_done, pv_done, o_free, o_copied = {}, {}, [None], {}
            t_free = [None, None]

            def scores_exp(b, quad, tile):
                nonlocal t_count
                g, cc = 2 * quad + tile % 2, tile // 2
                n = t_count % 2
                t_count += 1
                i = b % 3
                pe.after(m_loaded[b, quad // 2], t_free[n])
                for j in range(2):
                    c = 2 * cc + j
                    e = nc.tensor.matmul(t_bank[n][:, j * 512:(j + 1) * 512], kstack[i][0:STACK, g, c * P:(c + 1) * P],
                                         qstack[i][0:STACK, 2 * g:2 * g + 2, :].rearrange("p h q -> p (h q)"), start=True, stop=True)
                    if j == 1:
                        e = pe.run(e)
                stack_read[b] = e
                turn = (KC * b + quad) % 2
                act.after(e, pv_done.get(KC * b + quad - 2))
                t_free[n] = act.run(nc.scalar.activation(
                    prob[:, turn, tile % 2, 2 * cc:2 * cc + 2, :].rearrange("p c n -> p (c n)"), t_bank[n][:, :], ACT.Exp))
                exp_done[b, quad, tile] = t_free[n]

            def values(b, quad, c):
                turn = (KC * b + quad) % 2
                pe.after(exp_done[b, quad, 2 * (c // 2)], exp_done[b, quad, 2 * (c // 2) + 1], v_ready)
                if c == 0 and quad % 2 == 0:
                    pe.after(free[6])
                for j in range(4):
                    h = 4 * quad + j
                    e = nc.tensor.matmul(o_bank[32 * j:32 * j + 32, (quad % 2) * SQ:(quad % 2 + 1) * SQ],
                                         vaug[:, KC * b + c, h * VC:h * VC + 32],
                                         prob[:, turn, j // 2, c, (j % 2) * SQ:(j % 2 + 1) * SQ],
                                         start=c == 0, stop=c == KC - 1)
                    if j == 3:
                        pv_done[KC * b + quad] = e = pe.run(e)
                if c == KC - 1 and quad % 2 == 1:
                    half = quad // 2
                    act.after(e, o_read.get((b - 2, QT - 1)))
                    free[6] = o_copied[b, half] = act.run(nc.scalar.activation(oT[:, b % 2, half, :], o_bank[:, :], ACT.Copy))

            o_read, o_step = {}, {}

            def out_gather(b, qt):
                pe.after(o_copied[b, 0], o_copied[b, 1], free[7])
                for k in range(4):
                    o_read[b, qt] = e = pe.run(nc.tensor.transpose(
                        m_bank[:, k * P:(k + 1) * P], oT[:, b % 2, k // 2, (k % 2) * SQ + qt * P:(k % 2) * SQ + (qt + 1) * P], ident[:, :]))
                m = m_bank[:, :].rearrange("p (h v) -> p h v", v=32)
                dve.after(e)
                e = dve.run(nc.vector.reciprocal(rsum[:, qt, :], m[:, :, HD]))
                dve.after(e, o_step.get((b - 1, qt, "transposed")))
                free[7] = o_step[b, qt, "norm"] = dve.run(nc.vector.tensor_tensor(
                    o_norm[:, qt, :].rearrange("p (h v) -> p h v", v=HD), m[:, :, 0:HD],
                    rsum[:, qt, :].unsqueeze(2).to_broadcast([P, H, HD]), ALU.mult))

            def out_transpose(b, qt):
                pe.after(o_step[b, qt, "norm"], free[7])
                e = o_step[b, qt, "transposed"] = pe.run(nc.tensor.transpose(m_bank[:, 0:P], o_norm[:, qt, :], ident[:, :]))
                act.after(e, o_step.get((b - 1, qt, "product")))
                free[7] = o_step[b, qt, "copied"] = act.run(nc.scalar.activation(o_normT[:, qt, :], m_bank[:, 0:P], ACT.Copy))

            def out_project(b, qt):
                pe.after(o_step[b, qt, "copied"], free[7])
                e = o_step[b, qt, "product"] = pe.run(nc.tensor.matmul(m_bank[:, 0:D], o_normT[:, qt, :], wo[:, :], start=True, stop=True))
                dve.after(e, x_plus)
                free[7] = o_step[b, qt, "added"] = dve.run(nc.vector.tensor_tensor(
                    x[:, QT * b + qt, :], m_bank[:, 0:D], x[:, QT * b + qt, :], ALU.add))

            load_stacks(0)
            load_stacks(1)
            units = [(h, qt) for h in range(H) for qt in range(QT)]
            for b in range(-1, B + 1):
                if b + 3 < B + 1 and b + 2 >= 2 and b + 2 < B:
                    load_stacks(b + 2)
                for slot in range(16):
                    if b + 1 < B:
                        for h, qt in units[2 * slot:2 * slot + 2]:
                            scores_max(b + 1, h, qt)
                    if slot == 0 and 0 <= b < B:
                        max_parts(b, 1)
                    if 0 <= b < B:
                        if slot == 1:
                            max_rows(b, 1)
                        scores_exp(b, slot // 4, slot % 4)
                    if slot < 4 and b >= 1:
                        values(b - 1, 3, slot)
                    elif slot >= 4 and 0 <= b < B:
                        values(b, slot // 4 - 1, slot % 4)
                    if b >= 1:
                        if slot in (5, 10):
                            out_gather(b - 1, slot // 10)
                        if slot in (6, 11):
                            out_transpose(b - 1, slot // 10)
                        if slot in (7, 12):
                            out_project(b - 1, slot // 10)
                    if b + 1 < B:
                        if slot == 8:
                            max_parts(b + 1, 0)
                        if slot == 9:
                            max_rows(b + 1, 0)
            return (dve.sem, dve.count)

        def cast_parts(ready, columns):
            w, r = route[:, 0, :, 0:columns], route[:, 1, :, 0:columns]
            if columns < E0:
                ready = dve.run(nc.vector.memset(wparts[:, :, :, :], 0.0))
            dve.after(ready)
            e = dve.run(nc.vector.tensor_copy(wparts[:, :, 0, 0:columns], w))
            dve.after(e)
            e = dve.run(nc.vector.tensor_tensor(r, w, wparts[:, :, 0, 0:columns], ALU.subtract))
            dve.after(e)
            e = dve.run(nc.vector.tensor_copy(wparts[:, :, 1, 0:columns], r))
            dve.after(e)
            e = dve.run(nc.vector.tensor_tensor(wparts[:, :, 2, 0:columns], r, wparts[:, :, 1, 0:columns], ALU.subtract))
            for g in range(NB):
                n = 6 + g % 2
                b16 = bank[n].bitcast(BF16)
                pe.after(e, free[n])
                for i in range(4):
                    f = pe.run(nc.tensor.transpose(b16[0:96, i * P:(i + 1) * P],
                                                   wparts[:, 4 * g + i].rearrange("p j h -> p (j h)"), ident16[:, :]))
                act.after(f)
                free[n] = act.run(nc.scalar.activation(wT[:, g * BLK:(g + 1) * BLK], b16[0:96, 0:BLK], ACT.Copy))
            return free[n]

        def router_logits(xT_ready, experts, w_ready):
            pe.after(free[5], w_ready)
            for t in range(TT):
                pe.after(xT_ready[t // 4])
                tok = slice(t * P, (t + 1) * P)
                e = parts3(bank[5][:, t * experts:(t + 1) * experts], actT[:, 0, tok], actT[:, 1, tok],
                           rt_w[:, 0, 0:experts], rt_w[:, 1, 0:experts])
            return e

        class Blocks:

            def __init__(self):
                self.n, self.waiting = 0, None
                self.silu_read, self.prod_read = [None, None], [None, None]
                self.hid_read = [None] * 3

            def unit(self, rows, gu, xhi, xlo, x_ready, weight, down, acc, first, last):
                i, h = self.n % 2, self.n % 3
                self.n += 1
                pe.after(x_ready, free[i])
                g = parts3(bank[i][0:rows, :], gu[0][0], gu[0][1], xhi, xlo)
                pe.after(free[2 + i])
                u = parts3(bank[2 + i][0:rows, :], gu[1][0], gu[1][1], xhi, xlo)
                if weight is not None:
                    pe.after(free[4])
                    w = pe.run(nc.tensor.matmul(bank[4], weight[0], weight[1], start=True, stop=True))
                self.flush()
                act.after(g, self.silu_read[i])
                free[i] = s = act.run(nc.scalar.activation(silu[0:rows, i, :], bank[i][0:rows, :], ACT.Silu))
                dve.after(s, u)
                if weight is not None:
                    dve.after(self.prod_read[i])
                    free[2 + i] = self.silu_read[i] = e = dve.run(nc.vector.tensor_tensor(
                        prod[:, i, :], bank[2 + i], silu[:, i, :], ALU.mult))
                    dve.after(e, w, self.hid_read[h])
                    free[4] = e = self.prod_read[i] = dve.run(nc.vector.tensor_tensor(
                        hid[:, h, :], bank[4], prod[:, i, :], ALU.mult))
                else:
                    dve.after(self.hid_read[h])
                    free[2 + i] = self.silu_read[i] = e = dve.run(nc.vector.tensor_tensor(
                        hid[0:rows, h, :], bank[2 + i][0:rows, :], silu[0:rows, i, :], ALU.mult))
                self.waiting = (rows, h, e, down, acc, first, last)

            def flush(self):
                if self.waiting is None:
                    return
                rows, h, ready, down, acc, first, last = self.waiting
                self.waiting = None
                pe.after(ready)
                if first:
                    pe.after(free[acc])
                self.hid_read[h] = self.done = pe.run(nc.tensor.matmul(bank[acc], down, hid[0:rows, h, :], start=first, stop=last))

            def finish(self, blk, acc, x_free):
                self.flush()
                i = blk % 2
                act.after(self.done, self.y_read[i])
                free[acc] = e = act.run(nc.scalar.activation(yT[:, i, :], bank[acc], ACT.Copy))
                pe.after(e, free[5])
                for k in range(4):
                    e = pe.run(nc.tensor.transpose(bank[5][:, k * P:(k + 1) * P], yT[:, i, k * P:(k + 1) * P], ident[:, :]))
                self.y_read[i] = e
                dve.after(e, x_free)
                xs = x[:, 4 * blk:4 * blk + 4, :].rearrange("p t d -> p (t d)")
                free[5] = dve.run(nc.vector.tensor_tensor(xs, bank[5], xs, ALU.add))
                return free[5]

            y_read = [None, None]

        def ffn_0(x_done):
            pre = "L0_ffn_"
            e = ld_w.start(sp, e_nat[:, :, :, :], A["L0_gu"])
            e = ld_w.start(sp, down0[:, :, :], A["L0_down"])
            e = ld_w.start(sp, gw_nat[:, :], A["L0_router"])
            e = ld_w.start(sp, gate_bias[:, :], A[pre + "gate_bias"].partition_broadcast(P))
            w_loaded = ld_w.start(sp, sel0f[:, :, :], A["c_sel0"])

            xT_ready, x_read = layernorm(x_done)
            rw = split(gw_nat[:, :], rt_w[:, 0, :], rt_w[:, 1, :], w_loaded)
            pool.after(w_loaded)
            sel_ready = pool.run(nc.gpsimd.tensor_copy(sel0[:, :, :], sel0f[:, :, :]))
            logits = router_logits(xT_ready, E0, rw)
            act.after(logits)
            scores, choice, masked, found, sel = (route[:, i, :, :] for i in range(2, 7))
            free[5] = e = act.run(nc.scalar.activation(scores, bank[5].rearrange("p (t e) -> p t e", e=E0), ACT.Sigmoid))
            for g in range(0, EP + 1, 4):
                m = min(4, EP + 1 - g)
                w_ready = split(e_nat[:, g:g + m, :, :], gu0[:, g:g + m, :, 0, :], gu0[:, g:g + m, :, 1, :], w_loaded)
            dve.after(e, w_loaded)
            e = dve.run(nc.vector.tensor_tensor(choice, scores, gate_bias[:, :].unsqueeze(1).to_broadcast([P, TT, E0]), ALU.add))
            dve.after(e)
            for t in range(TT):
                for g in range(GROUPS):
                    e = dve.run(nc.vector.max(found[:, t, 8 * g:8 * g + 8], choice[:, t, 8 * g:8 * g + 8]))
            dve.after(e)
            gs = small[:, 0, :, 0:4]
            f4 = found.rearrange("p t (g k) -> p t g k", k=8)
            e = dve.run(nc.vector.tensor_tensor(gs, f4[:, :, :, 0], f4[:, :, :, 1], ALU.add))
            dve.after(e)
            sh = [P, TT, 4, 4]
            mine = gs.unsqueeze(3).to_broadcast(sh)
            other = gs.unsqueeze(2).to_broadcast(sh)
            c4 = [small[:, i, :, :].rearrange("p t (a b) -> p t a b", b=4) for i in range(1, 4)]
            e1 = dve.run(nc.vector.tensor_tensor(c4[0], other, mine, ALU.is_gt))
            e2 = dve.run(nc.vector.tensor_tensor(c4[1], other, mine, ALU.is_equal))
            dve.after(e2)
            e = dve.run(nc.vector.tensor_tensor(small[:, 2, :, :], small[:, 2, :, :],
                                                order[:, 0:16].unsqueeze(1).to_broadcast([P, TT, 16]), ALU.mult))
            dve.after(e)
            e = dve.run(nc.vector.tensor_tensor(small[:, 3, :, :], small[:, 1, :, :], small[:, 2, :, :], ALU.add))
            dve.after(e)
            e = dve.run(nc.vector.tensor_reduce(small[:, 4, :, 0:4], c4[2], AX.X, ALU.add))
            dve.after(e)
            e = dve.run(nc.vector.tensor_scalar(small[:, 5, :, 0:4], small[:, 4, :, 0:4], 2.0, None, ALU.is_lt))
            dve.after(e)
            e = dve.run(nc.vector.tensor_tensor(masked.rearrange("p t (g k) -> p t g k", k=8), choice.rearrange("p t (g k) -> p t g k", k=8),
                                                small[:, 5, :, 0:4].unsqueeze(3).to_broadcast([P, TT, 4, 8]), ALU.mult))
            dve.after(e)
            e = dve.run(nc.vector.tensor_scalar(masked, masked, 0.0, None, ALU.add))
            dve.after(e)
            for t in range(TT):
                e = dve.run(nc.vector.max(small[:, 0, t, 8:16], masked[:, t, :]))
            dve.after(e)
            for t in range(TT):
                e = dve.run(nc.vector.match_replace(sel[:, t, :], small[:, 0, t, 8:16], masked[:, t, :], -BIG))
            dve.after(e)
            e = dve.run(nc.vector.scalar_tensor_tensor(sel, sel, -BIG, scores, ALU.is_equal, ALU.mult))
            dve.after(e)
            tot = small[:, 1, :, 0]
            e = dve.run(nc.vector.tensor_reduce(tot, sel, AX.X, ALU.add))
            dve.after(e)
            e = dve.run(nc.vector.tensor_scalar(tot, tot, 1e-20, None, ALU.add))
            dve.after(e)
            e = dve.run(nc.vector.reciprocal(tot, tot))
            dve.after(e)
            e = dve.run(nc.vector.tensor_scalar(tot, tot, 2.5, None, ALU.mult))
            dve.after(e)
            e = dve.run(nc.vector.tensor_tensor(route[:, 0, :, :], sel, small[:, 1, :, 0:1].to_broadcast([P, TT, E0]), ALU.mult))
            wT_ready = cast_parts(e, E0)

            blocks = Blocks()
            pe.after(w_loaded, w_ready, wT_ready, sel_ready)
            done = []
            for blk in range(NB):
                cols = slice(blk * BLK, (blk + 1) * BLK)
                acc = 6 + blk % 2
                for u in range(EP + 1):
                    gu = [[gu0[:, u, i, j, :] for j in range(2)] for i in range(2)]
                    weight = (sel0[:, u, :], wT[:, cols]) if u < EP else None
                    blocks.unit(P, gu, actT[:, 0, cols], actT[:, 1, cols], xT_ready[blk], weight,
                                down0[:, u, :], acc, u == 0, u == EP)
                    if u == 1 and blk:
                        done.append(pending(blocks, blk - 1))
                blocks.flush()
                pending = lambda bl, k, d=blocks.done: finish(bl, k, d, x_read)
            done.append(pending(blocks, NB - 1))
            return done[-1]

        def finish(blocks, blk, done, x_read):
            keep, blocks.done = (blocks.done, blocks.waiting), done
            blocks.waiting = None
            e = blocks.finish(blk, 6 + blk % 2, x_read)
            blocks.done, blocks.waiting = keep
            return e

        def ffn_1(x_done):
            pre = "L1_ffn_"
            ld_w.start(sp, w_nat[:, :, :, :], A["L1_gu"])
            for c, (f0, fn) in enumerate(FC):
                ld_w.start(sp, down1[0:fn, 0:E1, c, :], A[pre + "w2_eFD"][:, f0:f0 + fn, :].rearrange("e f d -> f e d"))
                ld_w.start(sp, down1[0:fn, E1, c, :], A[pre + "ws2_FD"][f0:f0 + fn, :])
            ld_w.start(sp, sel1f[:, :, :], A["c_sel1"])
            w_loaded = ld_w.start(sp, gatedf[:, 0:E1], A[pre + "router_DE"])

            xT_ready, x_read = layernorm(x_done)
            act.after(w_loaded)
            rw = split(gatedf[:, 0:E1], rt_w[:, 0, 0:E1], rt_w[:, 1, 0:E1], w_loaded)
            pool.after(w_loaded)
            sel_ready = pool.run(nc.gpsimd.tensor_copy(sel1[:, :, :], sel1f[:, :, :]))
            logits = router_logits(xT_ready, E1, rw)
            act.after(logits)
            scores, eq, sel = (route[:, i, :, 0:E1] for i in range(2, 5))
            free[5] = e = act.run(nc.scalar.activation(scores, bank[5][:, 0:TT * E1].rearrange("p (t e) -> p t e", e=E1), ACT.Copy))
            gate = route[:, 5, :, 0:E1]
            act.after(e)
            e2 = act.run(nc.scalar.activation(gate, scores, ACT.Sigmoid))
            dve.after(e, e2)
            best = small[:, 0, :, 0:1]
            e = dve.run(nc.vector.tensor_reduce(best.rearrange("p t o -> p (t o)"), scores, AX.X, ALU.max))
            dve.after(e)
            e = dve.run(nc.vector.tensor_tensor(eq, scores, best.to_broadcast([P, TT, E1]), ALU.is_equal))
            dve.after(e)
            e = dve.run(nc.vector.tensor_tensor(eq, eq, order[:, 16:16 + E1].unsqueeze(1).to_broadcast([P, TT, E1]), ALU.mult))
            dve.after(e)
            e = dve.run(nc.vector.tensor_reduce(best.rearrange("p t o -> p (t o)"), eq, AX.X, ALU.max))
            dve.after(e)
            e = dve.run(nc.vector.tensor_tensor(sel, eq, best.to_broadcast([P, TT, E1]), ALU.is_equal))
            dve.after(e)
            e = dve.run(nc.vector.tensor_tensor(route[:, 0, :, 0:E1], sel, gate, ALU.mult))
            wT_ready = cast_parts(e, E1)
            for u in range(E1 + 1):
                w_ready = split(w_nat[:, u, :, :], gu1[:, u, :, 0, :], gu1[:, u, :, 1, :], w_loaded)

            blocks = Blocks()
            pe.after(w_ready, wT_ready, sel_ready)
            g_ready, g_read = {}, {}
            order_u = [(blk, u) for blk in range(NB) for u in [E1] + list(range(E1))]

            def gate_inputs(k):
                blk, u = order_u[k]
                if u == E1:
                    return
                cols = slice(blk * BLK, (blk + 1) * BLK)
                pe.after(free[4])
                e = pe.run(nc.tensor.matmul(bank[4], sel1[:, u, :], wT[:, cols], start=True, stop=True))
                dve.after(e, g_read.get("f"))
                full = xfull[:, cols]
                free[4] = e = dve.run(nc.vector.tensor_tensor(gatedf[:, :], bank[4], full, ALU.mult))
                act.after(e, g_read.get(k - 2))
                a = act.run(nc.scalar.activation(gated[:, k % 2, 0, :], gatedf[:, :], ACT.Copy))
                dve.after(a)
                g_ready[k] = g_read["f"] = dve.run(nc.vector.tensor_tensor(
                    gated[:, k % 2, 1, :], gatedf[:, :], gated[:, k % 2, 0, :].bitcast(FP32), ALU.subtract))

            xfull = w_nat[:, :, :, :].rearrange("p a b c -> p (a b c)")[:, 0:T]
            dve.after(w_ready)
            e = dve.run(nc.vector.tensor_tensor(xfull, actT[:, 0, 0:T].bitcast(FP32), actT[:, 1, 0:T].bitcast(FP32), ALU.add))
            dve.after(e)
            done, pending = [], None
            gate_inputs(1)
            for k, (blk, u) in enumerate(order_u):
                cols = slice(blk * BLK, (blk + 1) * BLK)
                acc = 6 + blk % 2
                if u == E1:
                    xs, ready = (actT[:, 0, cols], actT[:, 1, cols]), xT_ready[blk]
                else:
                    xs, ready = (gated[:, k % 2, 0, :], gated[:, k % 2, 1, :]), g_ready[k]
                for c, (f0, fn) in enumerate(FC):
                    gu = [[gu1[:, u, i, j, f0:f0 + fn] for j in range(2)] for i in range(2)]
                    blocks.unit(fn, gu, xs[0], xs[1], ready, None, down1[0:fn, u, c, :], acc,
                                u == E1 and c == 0, u == E1 - 1 and c == 2)
                    if c == 1 and u == E1 and blk:
                        done.append(pending(blocks, blk - 1))
                g_read[k] = (pe.sem, pe.count)
                if k + 2 < len(order_u):
                    gate_inputs(k + 2)
                if u == E1 - 1:
                    blocks.flush()
                    pending = lambda bl, kk, d=blocks.done: finish(bl, kk, d, x_read)
            done.append(pending(blocks, NB - 1))
            return done

        x_done = xattn(0, x_ready)
        everybody()
        x_done = ffn_0(x_done)
        everybody()
        x_done = xattn(1, x_done)
        everybody()
        done = ffn_1(x_done)
        st = transfers("store")
        for blk in range(NB):
            sp.after(done[blk])
            stored = st.start(sp, out[:, 4 * blk:4 * blk + 4, :], x[:, 4 * blk:4 * blk + 4, :])
        sp.after(stored)


def constants():
    import numpy as np
    ident = np.eye(P, dtype=np.float32)
    order = np.zeros((P, 16 + E1), np.float32)
    order[:, 0:16] = (np.arange(4)[None, :] < np.arange(4)[:, None]).astype(np.float32).reshape(1, 16)
    order[:, 16:] = E1 - np.arange(E1)
    sel0 = np.zeros((96, EP, P), np.float32)
    sel1 = np.zeros((96, E1, P), np.float32)
    for part in range(3):
        for e in range(E0):
            sel0[32 * part + e, e // 2, 64 * (e % 2):64 * (e % 2) + 64] = 1.0
        for e in range(E1):
            sel1[32 * part + e, e, :] = 1.0
    half = np.arange(0, HD, 2, dtype=np.float32) / np.float32(HD)
    inv = (np.float32(1.0) / np.power(np.float32(10000.0), half)).astype(np.float32)
    angle = (np.arange(SK, dtype=np.float32)[:, None] * inv[None, :]).astype(np.float32)
    rope = np.zeros((P, 2, SK), np.float32)
    for row in range(P):
        d = row % 64 // PAIRS
        a = angle[:, d % (HD // 2)].astype(np.float64)
        rope[row, 0] = np.cos(a)
        rope[row, 1] = np.sin(a) * (-1.0 if d < HD // 2 else 1.0)
    return {"c_ident": ident, "c_order": order, "c_sel0": sel0, "c_sel1": sel1, "c_rope": rope}


def laid_out(a):
    import numpy as np
    a = {k: np.asarray(v) for k, v in a.items()}

    def tiles(v):
        return v.reshape(TT, P, D).transpose(1, 0, 2)

    def stacked(w):
        return w.reshape(*w.shape[:-1], PAIRS, 2, HD).swapaxes(-3, -2).swapaxes(-2, -1).reshape(w.shape)

    def half(w):
        return np.roll(w.reshape(*w.shape[:-1], H, HD), HD // 2, axis=-1).reshape(w.shape)

    r = {"x": tiles(a["x"]), "ctxT": a["ctx_1024"].reshape(-1, D).T, "mask": a["mask_Bx1x1xS2_ff0"].reshape(B, SK)}
    for layer, names in ((0, ["wq", "wk", "wv", "wo"]), (1, ["Wq", "Wk", "Wv", "Wo"])):
        pre = f"L{layer}_xattn_"
        wq, wk, wv, wo = (a[pre + n] if layer == 0 else a[pre + n].T for n in names)
        bq, bk = a[pre + "bq"], a[pre + "bk"]
        r[f"L{layer}_w"] = np.stack([stacked(wq), stacked(wk), stacked(half(wq)), stacked(half(wk)), wv], 1)
        r[f"L{layer}_b"] = np.stack([stacked(bq), stacked(bk), stacked(half(bq)), stacked(half(bk))], 1)
        r[f"L{layer}_wo"], r[f"L{layer}_bv"], r[f"L{layer}_bo"] = wo, a[pre + "bv"], a[pre + "bo"]
    pre = "L0_ffn_"
    gu = [np.concatenate([a[pre + "expert_" + n].reshape(EP, P, D), a[pre + "shared_" + n][None]]) for n in ("gate", "up")]
    r["L0_gu"] = np.stack(gu, 1).transpose(3, 0, 1, 2)
    down = a[pre + "expert_down"].transpose(0, 2, 1).reshape(EP, P, D)
    r["L0_down"] = np.concatenate([down, a[pre + "shared_down"].T[None]]).transpose(1, 0, 2)
    r["L0_router"], r[pre + "gate_bias"] = a[pre + "gate_w"].T, a[pre + "gate_bias"]
    pre = "L1_ffn_"
    gu = [np.concatenate([a[pre + f"w{n}_eDF"], a[pre + f"ws{n}_DF"][None]]) for n in (1, 3)]
    r["L1_gu"] = np.stack(gu, 1).transpose(2, 0, 1, 3)
    for n in ("w2_eFD", "ws2_FD", "router_DE"):
        r[pre + n] = a[pre + n]
    return r


def kernel(**inputs):
    import numpy as np
    import concourse.bacc as bacc
    from concourse.bass_utils import run_bass_kernel_spmd

    nc = bacc.Bacc("TRN2", target_bir_lowering=False, num_devices=1)
    arrays, aps = {}, {}
    for name, value in {**laid_out(inputs), **constants()}.items():
        a = np.ascontiguousarray(value)
        arrays[f"in_{name}"] = a
        aps[name] = nc.dram_tensor(f"in_{name}", a.shape, mybir.dt.from_np(a.dtype), kind="ExternalInput").ap()
    out = nc.dram_tensor("out_x", (P, TT, D), FP32, kind="ExternalOutput").ap()
    build(nc, aps, out)
    r = run_bass_kernel_spmd(nc, [arrays], core_ids=[0])
    return r.results[0]["out_x"].transpose(1, 0, 2).reshape(B, SQ, D)
```

```python
import itertools
import math
from contextlib import ExitStack

import concourse.bass as bass
from concourse import mybir

FP32 = mybir.dt.float32
F32R = mybir.dt.float32r
BF16 = mybir.dt.bfloat16
I32 = mybir.dt.int32
ALU = mybir.AluOpType
ACT = mybir.ActivationFunctionType
AX = mybir.AxisListType

P = 128
B, SQ, SK, D, H = 8, 256, 512, 128, 16
HD = D // H
PAIRS = H // 2
T = B * SQ
TT = T // P
QT = SQ // P
KC = SK // P
CT = B * KC
EPS = 1e-5
SCALE = 1.0 / math.sqrt(HD)
TERMS = [(0, 0), (0, 1), (1, 0), (0, 2), (2, 0), (1, 1)]
HROWS = HD * len(TERMS)
MASK_ROW = 2 * HROWS
MAX_ROW = MASK_ROW + 3
STACK = MAX_ROW + 3
VC = HD + 1
E0, I0, GROUPS = 32, 64, 4
EP = E0 // 2
E1, F1 = 8, 352
FC = [(0, 128), (128, 128), (256, 96)]
BLK = 512
NB = T // BLK
START1 = 26
FAST = lambda tick: tick % 2
BT = BLK // P
TILES = T // P + E1 - 1
ORDER = 16 + E1 + TT + E1 * E1 + TILES + TT
BIG = 1e30


class Queue:

    def __init__(self, engine, sem):
        self.engine, self.sem, self.count, self.seen = engine, sem, 0, {}

    def after(self, *events):
        for event in events:
            if event is None:
                continue
            if isinstance(event, list):
                self.after(*event)
                continue
            sem, value = event
            if self.seen.get(sem.name, 0) < value:
                self.engine.wait_ge(sem, value)
                self.seen[sem.name] = value

    def run(self, instruction):
        instruction.then_inc(self.sem, 1)
        self.count += 1
        return self.sem, self.count


class Transfers:

    def __init__(self, sem):
        self.sem, self.count = sem, 0

    def start(self, queue, out, in_):
        queue.engine.dma_start(out, in_).then_inc(self.sem, 16)
        self.count += 16
        return self.sem, self.count

    def scatter(self, queue, out, rows, in_):
        queue.engine.indirect_dma_start(out, bass.IndirectOffsetOnAxis(ap=rows, axis=0), in_, None).then_inc(self.sem, 16)
        self.count += 16
        return self.sem, self.count


def build(nc, A, out):
    stack = ExitStack()
    with stack:
        def sem(name):
            return stack.enter_context(nc.semaphore(name))

        def sbuf(name, shape, dt, scope=stack):
            return scope.enter_context(nc.sbuf_tensor(name, shape, dt))

        pe = Queue(nc.tensor, sem("pe_done"))
        act = Queue(nc.scalar, sem("act_done"))
        dve = Queue(nc.vector, sem("dve_done"))
        pool = Queue(nc.gpsimd, sem("pool_done"))
        sp = Queue(nc.sync, sem("sp_done"))
        engines = (pe, act, dve, pool, sp)

        def transfers(name):
            return Transfers(sem(name))

        x = sbuf("x", [P, TT, D], FP32)
        ident = sbuf("ident", [P, P], FP32)
        ident16 = sbuf("ident16", [P, P], BF16)
        order = sbuf("order", [P, ORDER], FP32)
        before16 = sbuf("before16", [P, 2, P], BF16)
        xT = sbuf("xT", [P, 2, T], F32R)
        stats = sbuf("stats", [P, TT, 6], FP32)
        mv = sbuf("mv", [P, TT, 2], FP32)
        rstd = sbuf("rstd", [P, 3, TT], FP32)
        wnat = sbuf("wnat", [P, 5, D], FP32)
        col = sbuf("col", [P, 4], FP32)
        wo = sbuf("wo", [P, D], FP32)
        rt_nat = sbuf("rt_nat", [P, E0], FP32)
        rt_w = sbuf("rt_w", [P, 2, E0], F32R)
        gate_bias = sbuf("gate_bias", [P, E0], FP32)
        bv = sbuf("bv", [P, D], FP32)
        bo = sbuf("bo", [P, D], FP32)
        wscope = ExitStack()
        e_nat = sbuf("e_nat", [P, EP + 1, 2, D], FP32, wscope)
        wscope.close()
        e_lo = sbuf("e_lo", [P, EP + 1, 2, D], F32R, wscope)
        down0 = sbuf("down0", [P, EP + 1, D], FP32, wscope)
        route = sbuf("route", [P, 6, BT, E0], FP32, wscope)
        small = sbuf("small", [P, 6, BT, 16], FP32, wscope)
        wparts = sbuf("wparts", [P, BT, 3, E0], BF16, wscope)
        wT = sbuf("wT", [96, T], BF16, wscope)
        yT0 = sbuf("yT0", [P, BLK], FP32, wscope)
        wscope.close()
        w_nat = sbuf("w_nat", [P, E1 + 1, 2, F1], FP32)
        down1 = sbuf("down1", [P, E1 + 1, 3, D], FP32)

        gscope = ExitStack()
        gu1 = sbuf("gu1", [P, E1 + 1, 2, 2, F1], F32R, gscope)
        gscope.close()
        ctx_nat = sbuf("ctx_nat", [P, SK], FP32)
        kstack = [sbuf(f"kstack{i}", [P, PAIRS, SK], BF16) for i in range(3)]
        qstack = [sbuf(f"qstack{i}", [P, H, SQ], BF16) for i in range(3)]

        scope = ExitStack()
        aw = sbuf("aw", [P, 5, 2, D], F32R, scope)
        ctxT = sbuf("ctxT", [P, 2, SK], F32R, scope)
        xqT = sbuf("xqT", [P, 2, SQ], F32R, scope)
        kparts = sbuf("kparts", [P, 3, 2, SK], BF16, scope)
        qparts = sbuf("qparts", [P, 3, SQ], BF16, scope)
        vaug = sbuf("vaug", [P, 3 * KC, H * VC + 23], FP32, scope)
        rscope = ExitStack()
        maskp = sbuf("maskp", [B, 3, SK], BF16, rscope)
        rscope.close()
        rope = sbuf("rope", [P, 2, SK], FP32, scope)
        work = sbuf("work", [P, 3, SK], FP32, scope)
        xn = sbuf("xn", [P, 4, D], FP32, scope)
        negmax = sbuf("negmax", [P, 2, H, QT], FP32, scope)
        mrest = sbuf("mrest", [P, QT, H // 2], FP32, scope)
        mparts = sbuf("mparts", [P, 2, QT, 3, H // 2], BF16, scope)
        mT = sbuf("mT", [24, 2, SQ], BF16, scope)
        ffn0 = ExitStack()
        eh = sbuf("eh", [P, EP + 1, 2, D], F32R, ffn0)
        sel0 = sbuf("sel0", [96, EP, P], BF16, ffn0)
        silu0 = sbuf("silu0", [P, 2, BLK], FP32, ffn0)
        hid0 = sbuf("hid0", [P, 3, BLK], FP32, ffn0)
        ffn0.close()
        mscope = ExitStack()
        mask8 = sbuf("mask8", [B, 2, SK], FP32, mscope)
        mscope.close()
        prob = sbuf("prob", [P, 2, 2, KC, 2 * SQ], FP32, scope)
        oT = sbuf("oT", [P, 2, 2, 2 * SQ], FP32, scope)
        o_norm = sbuf("o_norm", [P, 2, D], FP32, scope)
        o_normT = sbuf("o_normT", [P, 2, D], FP32, scope)
        rsum = sbuf("rsum", [P, 2, H], FP32, scope)
        scope.close()

        ffn1 = ExitStack()
        choice1 = sbuf("choice1", [P, 5, TT, E1], FP32, ffn1)
        per_token = sbuf("per_token", [P, 3, TT], FP32, ffn1)
        silu1 = sbuf("silu1", [P, 2, BLK], FP32, ffn1)
        hid1 = sbuf("hid1", [P, 3, BLK], FP32, ffn1)
        mid = sbuf("mid", [P, 2, F1], FP32, ffn1)
        yT1 = sbuf("yT1", [P, BLK], FP32, ffn1)
        sel16 = sbuf("sel16", [P, TT, E1], BF16, ffn1)
        plan = sbuf("plan", [P, 6, 84], FP32, ffn1)
        row_of = sbuf("row_of", [P, TT], I32, ffn1)
        expert_of = sbuf("expert_of", [P, TILES], I32, ffn1)
        token_of = sbuf("token_of", [P, TILES], I32, ffn1)
        gx = sbuf("gx", [P, TT, D + 1], FP32, ffn1)
        rows = sbuf("rows", [P, TILES, D + 1], FP32, ffn1)
        gxT = sbuf("gxT", [P, 2, 2, 4 * P], F32R, ffn1)
        ffn1.close()

        def psum(name, banks):
            return stack.enter_context(nc.psum_tensor(name, [P, 512 * banks], FP32))

        bank = [psum(f"bank{i}", 1)[:, :] for i in range(8)]
        NS, NT = 3, 2
        S0, T0, O, M0, M1 = 0, NS, NS + NT, 6, 7
        SIDE = 5
        free = [None] * 8

        def advance(jobs):
            for job in list(jobs):
                if next(job, "end") == "end":
                    jobs.remove(job)

        def to_the_end(steps):
            while True:
                try:
                    next(steps)
                except StopIteration as end:
                    return end.value

        def everybody():
            ends = [(q.sem, q.count) for q in engines if q.count]
            for q in engines:
                q.after(*ends)

        def parts3(hi, whi, wlo, xhi, xlo):
            nc.tensor.matmul(hi, whi, xhi, start=True, stop=False)
            nc.tensor.matmul(hi, whi, xlo, start=False, stop=False)
            return pe.run(nc.tensor.matmul(hi, wlo, xhi, start=False, stop=True))

        def split(src, hi, lo, ready):
            act.after(ready)
            a = act.run(nc.scalar.activation(hi, src, ACT.Copy))
            dve.after(ready, a)
            return dve.run(nc.vector.tensor_tensor(lo, src, hi.bitcast(FP32), ALU.subtract))

        ld_x, ld_const, ld_w = transfers("ld_x"), transfers("ld_const"), transfers("ld_w")
        ld_ctx = [transfers(f"ld_ctx{i}") for i in range(2)]
        x_ready = ld_x.start(sp, x[:, :, :], A["x"])
        ld_const.start(act, ident[:, :], A["c_ident"])
        ld_const.start(act, before16[:, :, :], A["c_before"].bitcast(BF16))
        const_ready = ld_const.start(act, order[:, :], A["c_order"])
        dve.after(const_ready)
        ident_ready = dve.run(nc.vector.tensor_copy(ident16[:, :], ident[:, :]))
        exponent = dve.run(nc.vector.memset(rstd[:, 1, :], -0.5))

        ld_k = [transfers(f"ld_k{i}") for i in range(3)]
        ld_q = [transfers(f"ld_q{i}") for i in range(3)]
        ld_m = [transfers(f"ld_m{i}") for i in range(2)]
        ld_mask, ld_zero = transfers("ld_mask"), transfers("ld_zero")
        ld_ffn, ld_ones = transfers("ld_ffn"), transfers("ld_ones")

        for i in range(3):
            q = dve if i == 0 else pool
            zeros_set = q.run(q.engine.memset(qstack[i][:, :, :].bitcast(FP32)[0:MASK_ROW], 0.0))
            ld_ones.start(act, qstack[i][MASK_ROW:STACK, :, :], A["c_ones"].bitcast(BF16).rearrange("r (h n) -> r h n", h=H))
            ones_set = ld_ones.start(act, kstack[i][MASK_ROW:STACK, :, :], A["c_ones"].bitcast(BF16).rearrange("r (g n) -> r g n", g=PAIRS))
        rows_in = nc.dram_tensor("rows_in", (TILES * P, D + 1), FP32, kind="Internal").ap()
        rows_out = nc.dram_tensor("rows_out", (T + TILES * P, D), FP32, kind="Internal").ap()
        ld_rows = [transfers(f"ld_rows{i}") for i in range(-(-TILES // 4))]
        ld_back = [transfers(f"ld_back{i}") for i in range(NB)]
        ld_empty = transfers("ld_empty")
        stacks_set = [(dve.sem, dve.count), zeros_set, ones_set]

        def ln_statistics(tiles, x_done):
            dve.after(x_done)
            for t in tiles:
                e = dve.run(nc.vector.bn_stats(stats[:, t, :], x[:, t, :]))
            dve.after(e)
            for t in tiles:
                e = dve.run(nc.vector.bn_aggr(mv[:, t, :], stats[:, t, :]))
            ts = slice(tiles[0], tiles[-1] + 1)
            pool.after(e, exponent)
            e = pool.run(nc.gpsimd.tensor_scalar(rstd[:, 0, ts], mv[:, ts, 1], EPS, None, ALU.add))
            pool.after(e)
            return pool.run(nc.gpsimd.tensor_tensor(rstd[:, 2, ts], rstd[:, 0, ts], rstd[:, 1, ts], ALU.pow))

        def ln_apply(tiles, slot, ready, xn_read):
            pool.after(ready, xn_read)
            for i, t in enumerate(tiles):
                e = pool.run(nc.gpsimd.tensor_scalar(xn[:, slot + i, :], x[:, t, :], mv[:, t, 0:1],
                                                    rstd[:, 2, t:t + 1], ALU.subtract, ALU.mult))
            return e

        def xattn(layer, x_ready):
            pre = f"L{layer}_"
            rope_on = layer == 1
            kinds = 4 if rope_on else 2
            ctx_loaded = ld_ctx[0].start(sp, ctx_nat[:, :], A["ctxT"][:, 0:SK])
            ld_w.start(sp, wnat[:, :, :], A[pre + "w"])
            ld_w.start(sp, wo[:, :], A[pre + "wo"])
            ld_w.start(sp, col[:, :], A[pre + "b"])
            ld_w.start(sp, bv[:, :], A[pre + "bv"].partition_broadcast(P))
            w_ready = ld_w.start(sp, bo[:, :], A[pre + "bo"].partition_broadcast(P))
            if rope_on:
                w_ready = ld_w.start(sp, rope[:, :, :], A["c_rope"])
            else:
                w_ready = ld_w.start(sp, mask8[:, 0, :], A["mask"])

            yield

            pool.run(nc.gpsimd.memset(vaug[:, :, HD:H * VC:VC], 1.0))
            v_set = pool.run(nc.gpsimd.memset(vaug[:, :, H * VC:], 1.0))
            yield from itertools.repeat(None, 4 * layer)
            dve.after(w_ready)
            act.after(w_ready)
            e = dve.run(nc.vector.tensor_scalar(wnat[:, 0:kinds:2, :], wnat[:, 0:kinds:2, :], SCALE, None, ALU.mult))
            e2 = dve.run(nc.vector.tensor_scalar(col[:, 0:kinds:2], col[:, 0:kinds:2], SCALE, None, ALU.mult))
            dve.after(e2)
            aw_ready = split(wnat[:, :, :], aw[:, :, 0, :], aw[:, :, 1, :], e)

            if layer == 0:
                e = dve.run(nc.vector.tensor_scalar(mask8[:, 0, :], mask8[:, 0, :], -1e9, None, ALU.mult))
                for i in range(3):
                    dve.after(e)
                    e = dve.run(nc.vector.tensor_copy(maskp[:, i, :], mask8[:, i % 2, :]))
                    if i < 2:
                        dve.after(e)
                        e = dve.run(nc.vector.tensor_tensor(mask8[:, 1 - i % 2, :], mask8[:, i % 2, :], maskp[:, i, :], ALU.subtract))
                mask_ready = e
            else:
                dve.after(w_ready)
                sp.after(dve.run(nc.vector.memset(work[0:3, 0, :].bitcast(BF16)[:, 0:SK], 0.0)))
                for i in range(3):
                    mask_ready = ld_zero.start(sp, kstack[i][MASK_ROW:MASK_ROW + 3, :, :],
                                               work[0:3, 0, :].bitcast(BF16)[:, 0:SK].unsqueeze(1).to_broadcast([3, PAIRS, SK]))

            mask_rows = MAX_ROW if layer == 0 else MASK_ROW
            k_loaded, q_loaded, m_loaded, stack_read = {}, {}, {}, {}
            o_read, o_step, mT_event = {}, {}, {}
            exp_done, pv_done, o_copied, s_last = {}, {}, {}, {}
            k_parts, q_parts, v_ready, x_ln, x_free = {}, {}, {}, {}, {}
            work_read = [mask_ready if layer else None, None]
            ctx_state = {"loaded": {0: ctx_loaded}, "kv_read": None, "xq_read": None}
            xn_read = [None, None]

            def stack_loads(b, which):
                i = b % 3
                if which == "k":
                    sp.after(k_parts[b], stacks_set, mask_ready, stack_read.get(b - 3))
                    for n, (_, part) in enumerate(TERMS):
                        for r in range(2):
                            row = HROWS * r + HD * n
                            k_loaded[b] = ld_k[i].start(sp, kstack[i][row:row + HD, :, :], kparts[64 * r:64 * r + 64, part, b % 2, :])
                    if layer == 0:
                        for m in range(3):
                            k_loaded[b] = ld_k[i].start(sp, kstack[i][MASK_ROW + m:MASK_ROW + m + 1, :, :],
                                                        maskp[b:b + 1, m:m + 1, :].to_broadcast([1, PAIRS, SK]))
                else:
                    sp.after(q_parts[b], stacks_set, stack_read.get(b - 3))
                    for n, (part, _) in enumerate(TERMS):
                        for r in range(2):
                            row = HROWS * r + HD * n
                            q_loaded[b] = ld_q[i].start(sp, qstack[i][row:row + HD, r::2, :], qparts[64 * r:64 * r + 64, part, :])

            def prep_context(b):
                e = ctx_state["loaded"][b]
                act.after(e, ctx_state["kv_read"], aw_ready)
                a = act.run(nc.scalar.activation(ctxT[:, 0, :], ctx_nat[:, :], ACT.Copy))
                yield
                pool.after(e, a, v_set)
                e = ctx_state["split"] = pool.run(nc.gpsimd.tensor_tensor(ctxT[:, 1, :], ctx_nat[:, :], ctxT[:, 0, :].bitcast(FP32), ALU.subtract))
                yield
                if b + 1 < B:
                    sp.after(e)
                    ctx_state["loaded"][b + 1] = ld_ctx[(b + 1) % 2].start(sp, ctx_nat[:, :], A["ctxT"][:, (b + 1) * SK:(b + 2) * SK])

            def prep_ln(b):
                while b * SQ // BLK not in x_ready:
                    yield
                x_ln[b] = ln_statistics([QT * b, QT * b + 1], x_ready[b * SQ // BLK])
                yield
                yield
                e = ln_apply([QT * b, QT * b + 1], 0, x_ln[b], xn_read[0])
                x_ln[b] = e
                pool.after(e, w_ready)
                xs = x[:, QT * b:QT * b + QT, :]
                x_free[b] = pool.run(nc.gpsimd.tensor_tensor(xs, xs, bo[:, :].unsqueeze(1).to_broadcast([P, QT, D]), ALU.add))
                yield

            def prep_k(b):
                hi, mid, lo = (kparts[:, i, b % 2, :] for i in range(3))
                pe.after(ctx_state["split"], aw_ready, free[M1])
                e = parts3(bank[M1], aw[:, 1, 0, :], aw[:, 1, 1, :], ctxT[:, 0, :], ctxT[:, 1, :])
                yield
                if rope_on:
                    dve.after(e, work_read[0])
                    free[M1] = dve.run(nc.vector.scalar_tensor_tensor(work[:, 0, :], bank[M1], col[:, 1:2], rope[:, 0, :], ALU.add, ALU.mult))
                    yield
                    pe.after(free[M1])
                    e = parts3(bank[M1], aw[:, 3, 0, :], aw[:, 3, 1, :], ctxT[:, 0, :], ctxT[:, 1, :])
                    yield
                    dve.after(e, free[M1])
                    free[M1] = e = dve.run(nc.vector.scalar_tensor_tensor(work[:, 1, :], bank[M1], col[:, 3:4], rope[:, 1, :], ALU.add, ALU.mult))
                    side.append(k_rotated_parts(b, e))
                else:
                    act.after(e, k_loaded.get(b - 2))
                    a = act.run(nc.scalar.activation(hi, bank[M1], ACT.Identity, bias=col[:, 1:2]))
                    yield
                    dve.after(a, work_read[0])
                    free[M1] = r = dve.run(nc.vector.scalar_tensor_tensor(work[:, 0, :], bank[M1], col[:, 1:2], hi, ALU.add, ALU.subtract))
                    side.append(k_low_parts(b, r, work[:, 0, :]))

            def k_low_parts(b, ready, rest):
                hi, mid, lo = (kparts[:, i, b % 2, :] for i in range(3))
                yield
                act.after(ready)
                a = act.run(nc.scalar.activation(mid, rest, ACT.Copy))
                yield
                pool.after(a)
                k_parts[b] = work_read[0] = pool.run(nc.gpsimd.tensor_tensor(lo, rest, mid, ALU.subtract))
                yield
                stack_loads(b, "k")

            def k_rotated_parts(b, ready):
                hi, mid, lo = (kparts[:, i, b % 2, :] for i in range(3))
                pool.after(ready)
                e = pool.run(nc.gpsimd.tensor_tensor(work[:, 0, :], work[:, 0, :], work[:, 1, :], ALU.add))
                yield
                yield
                act.after(e, k_loaded.get(b - 2))
                a = act.run(nc.scalar.activation(hi, work[:, 0, :], ACT.Copy))
                yield
                pool.after(a)
                r = pool.run(nc.gpsimd.tensor_tensor(work[:, 1, :], work[:, 0, :], hi, ALU.subtract))
                yield
                yield from k_low_parts(b, r, work[:, 1, :])

            def prep_v(b):
                pe.after(free[M1])
                for c in range(KC):
                    tok = slice(c * P, (c + 1) * P)
                    e = parts3(bank[M1][:, tok], ctxT[:, 0, tok], ctxT[:, 1, tok], aw[:, 4, 0, :], aw[:, 4, 1, :])
                ctx_state["kv_read"] = e
                yield
                dve.after(e, v_set, pv_done.get(KC * (b - 3) + 3))
                free[M1] = v_ready[b] = dve.run(nc.vector.tensor_tensor(
                    vaug[:, KC * (b % 3):KC * (b % 3 + 1), 0:H * VC].rearrange("p c (h v) -> p c h v", v=VC)[:, :, :, 0:HD],
                    bank[M1].rearrange("p (c h v) -> p c h v", c=KC, v=HD),
                    bv[:, :].rearrange("p (h v) -> p h v", v=HD).unsqueeze(1).to_broadcast([P, KC, H, HD]), ALU.add))

            def prep_x_transpose(b):
                pe.after(x_ln[b], free[M1], ident_ready)
                for i in range(QT):
                    e = pe.run(nc.tensor.transpose(bank[M1][:, i * P:(i + 1) * P], xn[:, i, :], ident[:, :]))
                xn_read[0] = e
                yield
                act.after(e, ctx_state["xq_read"])
                a = act.run(nc.scalar.activation(xqT[:, 0, :], bank[M1][:, 0:SQ], ACT.Copy))
                yield
                dve.after(e, a)
                free[M1] = ctx_state["xq"] = dve.run(nc.vector.tensor_tensor(xqT[:, 1, :], bank[M1][:, 0:SQ], xqT[:, 0, :].bitcast(FP32), ALU.subtract))

            def prep_q(b):
                pe.after(ctx_state["xq"], free[M1])
                q, qr = bank[M1][:, 0:SQ], bank[M1][:, SQ:2 * SQ]
                e = parts3(q, aw[:, 0, 0, :], aw[:, 0, 1, :], xqT[:, 0, :], xqT[:, 1, :])
                if rope_on:
                    e = parts3(qr, aw[:, 2, 0, :], aw[:, 2, 1, :], xqT[:, 0, :], xqT[:, 1, :])
                ctx_state["xq_read"] = e
                hi, mid, lo = (qparts[:, i, :] for i in range(3))
                w0, w1 = work[:, 2, 0:SQ], work[:, 2, SQ:2 * SQ]
                yield
                if rope_on:
                    dve.after(e, work_read[1])
                    dve.run(nc.vector.scalar_tensor_tensor(w0, q, col[:, 0:1], rope[:, 0, 0:SQ], ALU.add, ALU.mult))
                    free[M1] = e = dve.run(nc.vector.scalar_tensor_tensor(w1, qr, col[:, 2:3], rope[:, 1, 0:SQ], ALU.add, ALU.mult))
                    pool.after(e)
                    e = pool.run(nc.gpsimd.tensor_tensor(w0, w0, w1, ALU.add))
                    yield
                    act.after(e, q_loaded.get(b - 1))
                    a = act.run(nc.scalar.activation(hi, w0, ACT.Copy))
                    yield
                    pool.after(a)
                    r = pool.run(nc.gpsimd.tensor_tensor(w1, w0, hi, ALU.subtract))
                else:
                    act.after(e, q_loaded.get(b - 1))
                    a = act.run(nc.scalar.activation(hi, q, ACT.Identity, bias=col[:, 0:1]))
                    yield
                    dve.after(a, work_read[1])
                    free[M1] = r = dve.run(nc.vector.scalar_tensor_tensor(w1, q, col[:, 0:1], hi, ALU.add, ALU.subtract))
                yield
                act.after(r)
                a = act.run(nc.scalar.activation(mid, w1, ACT.Copy))
                yield
                pool.after(a)
                q_parts[b] = work_read[1] = pool.run(nc.gpsimd.tensor_tensor(lo, w1, mid, ALU.subtract))
                yield
                stack_loads(b, "q")

            side = []

            def prep(b):
                for job in (prep_context, prep_ln, prep_k, prep_v, prep_x_transpose, prep_q):
                    yield from job(b)
                    yield

            s_count = 0
            s_banks = [S0 + i for i in range(NS)]

            def scores_max(b, h, qt, banks=s_banks):
                nonlocal s_count
                n = banks[s_count % len(banks)]
                s_count += 1
                i = b % 3
                pe.after(k_loaded[b], q_loaded[b], free[n])
                e = pe.run(nc.tensor.matmul(bank[n], qstack[i][0:mask_rows, h, qt * P:(qt + 1) * P],
                                            kstack[i][0:mask_rows, h // 2, :], start=True, stop=True))
                dve.after(e)
                free[n] = dve.run(nc.vector.tensor_reduce(negmax[:, b % 2, h, qt:qt + 1], bank[n], AX.X, ALU.max, negate=True))
                s_last[b, h // 8] = free[n]

            def max_parts(b, half):
                hs = slice(8 * half, 8 * half + 8)
                nm = negmax[:, b % 2, hs, :].rearrange("p h q -> p q h")
                mp = mparts[:, half]
                pool.after(s_last[b, half])
                e = pool.run(nc.gpsimd.tensor_copy(mp[:, :, 0, :], nm))
                pool.after(e)
                e = pool.run(nc.gpsimd.tensor_tensor(mrest[:, :, :], nm, mp[:, :, 0, :], ALU.subtract))
                pool.after(e)
                e = pool.run(nc.gpsimd.tensor_copy(mp[:, :, 1, :], mrest[:, :, :]))
                pool.after(e)
                mT_event[b, half] = pool.run(nc.gpsimd.tensor_tensor(mp[:, :, 2, :], mrest[:, :, :], mp[:, :, 1, :], ALU.subtract))

            def max_rows(b, half, n=M0):
                m16 = bank[n].bitcast(BF16)
                pe.after(mT_event[b, half], free[n])
                for qt in range(QT):
                    e = pe.run(nc.tensor.transpose(m16[0:24, qt * P:(qt + 1) * P],
                                                   mparts[:, half, qt].rearrange("p j h -> p (j h)"), ident16[:, :]))
                if n == M0:
                    yield
                act.after(e, m_loaded.get((b - 1, half)))
                free[n] = e = act.run(nc.scalar.activation(mT[:, half, :], m16[0:24, 0:SQ], ACT.Copy))
                sp.after(e)
                m_loaded[b, half] = ld_m[half].start(sp, qstack[b % 3][MAX_ROW:MAX_ROW + 3, 8 * half:8 * half + 8, :], mT[:, half, :])

            t_count = 0

            def scores_exp(b, tick):
                nonlocal t_count
                quad, g, c = tick // 8, 2 * (tick // 8) + tick % 2, tick % 8 // 2
                i = b % 3
                turn = (KC * b + quad) % 2
                n = T0 + t_count % NT
                t_count += 1
                pe.after(m_loaded[b, quad // 2], free[n])
                stack_read[b] = e = pe.run(nc.tensor.matmul(
                    bank[n], kstack[i][0:STACK, g, c * P:(c + 1) * P],
                    qstack[i][0:STACK, 2 * g:2 * g + 2, :].rearrange("p h q -> p (h q)"), start=True, stop=True))
                act.after(e, pv_done.get(KC * b + quad - 2))
                free[n] = exp_done[b, quad, g % 2, c] = act.run(nc.scalar.activation(prob[:, turn, g % 2, c, :], bank[n], ACT.Exp))

            def values(b, quad, c):
                turn = (KC * b + quad) % 2
                pe.after(exp_done[b, quad, 0, c], exp_done[b, quad, 1, c], v_ready[b])
                if c == 0 and quad % 2 == 0:
                    pe.after(free[O])
                for j in range(4):
                    h = 4 * quad + j
                    e = nc.tensor.matmul(bank[O][32 * j:32 * j + 32, (quad % 2) * SQ:(quad % 2 + 1) * SQ],
                                         vaug[:, KC * (b % 3) + c, h * VC:h * VC + 32],
                                         prob[:, turn, j // 2, c, (j % 2) * SQ:(j % 2 + 1) * SQ],
                                         start=c == 0, stop=c == KC - 1)
                    if j == 3:
                        pv_done[KC * b + quad] = e = pe.run(e)
                if c == KC - 1 and quad % 2 == 1:
                    half = quad // 2
                    act.after(e, o_read.get((b - 2, QT - 1)))
                    free[O] = o_copied[b, half] = act.run(nc.scalar.activation(oT[:, b % 2, half, :], bank[O], ACT.Copy))

            def out_tile(b, qt, n=M0):
                pe.after(o_copied[b, 0], o_copied[b, 1], free[n])
                for k in range(4):
                    o_read[b, qt] = e = pe.run(nc.tensor.transpose(
                        bank[n][:, k * P:(k + 1) * P], oT[:, b % 2, k // 2, (k % 2) * SQ + qt * P:(k % 2) * SQ + (qt + 1) * P], ident[:, :]))
                yield
                m = bank[n].rearrange("p (h v) -> p h v", v=32)
                dve.after(e)
                e = dve.run(nc.vector.reciprocal(rsum[:, qt, :], m[:, :, HD]))
                dve.after(e, o_step.get((b - 1, qt, "transposed")))
                free[n] = e = dve.run(nc.vector.tensor_tensor(
                    o_norm[:, qt, :].rearrange("p (h v) -> p h v", v=HD), m[:, :, 0:HD],
                    rsum[:, qt, :].unsqueeze(2).to_broadcast([P, H, HD]), ALU.mult))
                yield
                pe.after(e, free[n])
                e = o_step[b, qt, "transposed"] = pe.run(nc.tensor.transpose(bank[n][:, 0:P], o_norm[:, qt, :], ident[:, :]))
                yield
                act.after(e, o_step.get((b - 1, qt, "product")))
                free[n] = e = act.run(nc.scalar.activation(o_normT[:, qt, :], bank[n][:, 0:P], ACT.Copy))
                yield
                pe.after(e, free[n])
                e = o_step[b, qt, "product"] = pe.run(nc.tensor.matmul(bank[n][:, 0:D], o_normT[:, qt, :], wo[:, :], start=True, stop=True))
                yield
                dve.after(e, x_free[b])
                free[n] = o_step[b, qt, "added"] = dve.run(nc.vector.tensor_tensor(
                    x[:, QT * b + qt, :], bank[n][:, 0:D], x[:, QT * b + qt, :], ALU.add))

            def next_ln(b, n=M0):
                e = ln_statistics([QT * b, QT * b + 1], o_step[b, 1, "added"])
                yield
                yield
                e = ln_apply([QT * b, QT * b + 1], 2, e, xn_read[1])
                yield
                yield
                pe.after(e, free[n])
                for i in range(QT):
                    e = pe.run(nc.tensor.transpose(bank[n][:, i * P:(i + 1) * P], xn[:, 2 + i, :], ident[:, :]))
                xn_read[1] = e
                cols = slice(b * SQ, (b + 1) * SQ)
                yield
                act.after(e)
                a = act.run(nc.scalar.activation(xT[:, 0, cols], bank[n][:, 0:SQ], ACT.Copy))
                yield
                dve.after(e, a)
                free[n] = next_ready[b] = dve.run(nc.vector.tensor_tensor(
                    xT[:, 1, cols], bank[n][:, 0:SQ], xT[:, 0, cols].bitcast(FP32), ALU.subtract))

            next_ready = {}

            def wait(n):
                for _ in range(n):
                    yield

            def m0_jobs(b):
                if 0 <= b < B:
                    yield
                    yield from max_rows(b, 1)
                elif b < 0:
                    yield
                if b == B:
                    for job in (out_tile(b - 1, 0, SIDE), out_tile(b - 1, 1, SIDE), next_ln(b - 1, SIDE)):
                        yield from job
                        yield
                    return
                if b >= 1:
                    yield from wait(7)
                    yield from out_tile(b - 1, 0)
                    yield
                if b + 1 < B:
                    yield from wait(0 if b >= 1 else 16)
                    while (b + 1, 0) not in mT_event:
                        yield
                    yield
                    yield from max_rows(b + 1, 0)
                    yield
                if b >= 1:
                    yield from out_tile(b - 1, 1)
                    yield
                    yield from next_ln(b - 1)

            units = [(h, qt) for h in range(H) for qt in range(QT)]

            def before_heads():
                jobs = [prep(0)]
                while jobs or side:
                    advance(jobs)
                    advance(side)
                    yield
                jobs = [prep(1)]
                for tick in range(8):
                    advance(jobs)
                    yield
                for tick in range(32):
                    scores_max(0, *units[tick], banks=[SIDE])
                    if tick == 17:
                        max_parts(0, 0)
                    if tick == 22:
                        list(max_rows(0, 0, SIDE))
                    advance(jobs)
                    advance(side)
                    yield
                while jobs or side:
                    advance(jobs)
                    advance(side)
                    yield

            def heads():
                for b in range(-1 if layer == 0 else 0, B):
                    jobs, fast = [m0_jobs(b)], []
                    if b == -1:
                        fast = [prep(0)]
                        while fast or side:
                            advance(fast)
                            advance(side)
                        fast = [prep(1)]
                    elif b + 2 < B:
                        fast = [prep(b + 2)]
                    if layer == 0 and b == B - 1:
                        router["parts"] = split(rt_nat[:, :], rt_w[:, 0, :], rt_w[:, 1, :], scratch["weights"])
                        jobs.append(itertools.chain(*(routing(blk, next_ready, S0, ACT.Exp) for blk in range(2))))
                    if b == 0:
                        load_ffn_weights(layer)
                    for tick in range(32):
                        if b + 1 < B:
                            scores_max(b + 1, *units[tick])
                        if tick == 0 and 0 <= b < B:
                            max_parts(b, 1)
                        if 0 <= b < B:
                            scores_exp(b, tick)
                        if tick % 2:
                            if tick < 8 and b >= 1:
                                values(b - 1, 3, tick // 2)
                            elif tick >= 8 and 0 <= b < B:
                                values(b, tick // 8 - 1, tick % 8 // 2)
                        if tick == 16 and b + 1 < B:
                            max_parts(b + 1, 0)
                        advance(jobs)
                        advance(side)
                        advance(fast)
                        if FAST(tick):
                            advance(side)
                            advance(fast)
                    while jobs or side or fast:
                        advance(jobs)
                        advance(fast)
                        advance(side)
                for c in range(KC):
                    values(B - 1, 3, c)
                return next_ready, m0_jobs(B), pv_done[KC * B - 1]

            if layer == 1:
                yield from before_heads()
            return heads

        scratch = {}

        def load_ffn_weights(layer):
            if layer == 0:
                ld_ffn.start(sp, rt_nat[:, :], A["L0_router"])
                ld_ffn.start(sp, gate_bias[:, :], A["L0_ffn_gate_bias"].partition_broadcast(P))
                ld_ffn.start(sp, e_nat[:, :, :, :], A["L0_gu"])
                scratch["weights"] = ld_ffn.start(sp, down0[:, :, :], A["L0_down"])
                return
            pre = "L1_ffn_"
            ld_ffn.start(sp, rt_nat[:, 0:E1], A["L1_ffn_router_DE"])
            ld_ffn.start(sp, w_nat[:, :, :, :], A["L1_gu"])
            for c, (f0, fn) in enumerate(FC):
                ld_ffn.start(sp, down1[0:fn, 0:E1, c, :], A[pre + "w2_eFD"][:, f0:f0 + fn, :].rearrange("e f d -> f e d"))
                scratch["weights"] = ld_ffn.start(sp, down1[0:fn, E1, c, :], A[pre + "ws2_FD"][f0:f0 + fn, :])
            scratch["set"] = ld_empty.start(sp, rows_in, A["c_rows"])

        def router_logits(n, tiles, xT_ready, experts, w_ready):
            pe.after(free[n], w_ready)
            for i, t in enumerate(tiles):
                pe.after(xT_ready[t // QT])
                tok = slice(t * P, (t + 1) * P)
                e = parts3(bank[n][:, i * experts:(i + 1) * experts], xT[:, 0, tok], xT[:, 1, tok],
                           rt_w[:, 0, 0:experts], rt_w[:, 1, 0:experts])
            return e

        class Blocks:

            def __init__(self, silu, hid, yT):
                self.silu, self.hid, self.yT = silu, hid, yT
                self.n, self.waiting, self.sums, self.y_read = 0, None, {}, None
                self.silu_read, self.hid_read = [None, None], [None] * 3

            def unit(self, blk, rows, gu, x_ready, weight, down, first, last, background=iter(())):
                i, h = self.n % 2, self.n % 3
                self.n += 1
                silu, hid = self.silu[0:rows, i, :], self.hid[0:rows, h, :]
                cols = slice(blk * BLK, (blk + 1) * BLK)
                pe.after([x_ready[b] for b in range(BLK * blk // SQ, BLK * (blk + 1) // SQ)], free[i])
                g = parts3(bank[i][0:rows, :], gu[0][0], gu[0][1], xT[:, 0, cols], xT[:, 1, cols])
                next(background, None)
                pe.after(free[2 + i])
                u = parts3(bank[2 + i][0:rows, :], gu[1][0], gu[1][1], xT[:, 0, cols], xT[:, 1, cols])
                if weight is not None:
                    pe.after(free[4])
                    w = pe.run(nc.tensor.matmul(bank[4], weight, wT[:, cols], start=True, stop=True))
                self.flush()
                act.after(g, self.silu_read[i])
                free[i] = s = act.run(nc.scalar.activation(silu, bank[i][0:rows, :], ACT.Silu))
                dve.after(s, u, self.hid_read[h])
                free[2 + i] = self.silu_read[i] = e = dve.run(nc.vector.tensor_tensor(hid, bank[2 + i][0:rows, :], silu, ALU.mult))
                if weight is not None:
                    dve.after(e, w)
                    free[4] = e = dve.run(nc.vector.tensor_tensor(hid, bank[4], hid, ALU.mult))
                self.waiting = (blk, rows, h, e, down, first, last)

            def flush(self):
                if self.waiting is None:
                    return
                blk, rows, h, ready, down, first, last = self.waiting
                self.waiting = None
                pe.after(ready)
                if first:
                    pe.after(free[6])
                self.hid_read[h] = e = pe.run(nc.tensor.matmul(bank[6], down, self.hid[0:rows, h, :], start=first, stop=last))
                if last:
                    act.after(e, self.y_read)
                    free[6] = self.sums[blk] = act.run(nc.scalar.activation(self.yT[:, :], bank[6], ACT.Copy))

            def finish(self, blk):
                pe.after(self.sums[blk], free[SIDE])
                for k in range(BT):
                    e = pe.run(nc.tensor.transpose(bank[SIDE][:, k * P:(k + 1) * P], self.yT[:, k * P:(k + 1) * P], ident[:, :]))
                self.y_read = e
                dve.after(e)
                xs = x[:, BT * blk:BT * blk + BT, :].rearrange("p t d -> p (t d)")
                free[SIDE] = dve.run(nc.vector.tensor_tensor(xs, bank[SIDE], xs, ALU.add))
                return free[SIDE]

        router, weights = {}, {}

        def routing(blk, xT_ready, n, function):
            w, r, scores, choice, masked, found = (route[:, i, :, :] for i in range(6))
            sel = found
            logits = bank[n][:, 0:BT * E0].rearrange("p (t e) -> p t e", e=E0)
            act.after(router_logits(n, range(BT * blk, BT * blk + BT), xT_ready, E0, router["parts"]), weights.get(blk - 1))
            if function == ACT.Sigmoid:
                free[n] = e = act.run(nc.scalar.activation(scores, logits, ACT.Sigmoid))
            else:
                free[n] = e = act.run(nc.scalar.activation(scores, logits, ACT.Exp, scale=-1.0))
                yield
                dve.after(e)
                e = dve.run(nc.vector.tensor_scalar(scores, scores, 1.0, None, ALU.add))
                dve.after(e)
                e = dve.run(nc.vector.reciprocal(scores, scores))
            yield
            dve.after(e)
            e = dve.run(nc.vector.tensor_tensor(choice, scores, gate_bias[:, :].unsqueeze(1).to_broadcast([P, BT, E0]), ALU.add))
            dve.after(e)
            for t in range(BT):
                for g in range(GROUPS):
                    e = dve.run(nc.vector.max(found[:, t, 8 * g:8 * g + 8], choice[:, t, 8 * g:8 * g + 8]))
                if t % 2:
                    yield
            dve.after(e)
            gs = small[:, 0, :, 0:4]
            f4 = found.rearrange("p t (g k) -> p t g k", k=8)
            e = dve.run(nc.vector.tensor_tensor(gs, f4[:, :, :, 0], f4[:, :, :, 1], ALU.add))
            dve.after(e)
            sh = [P, BT, 4, 4]
            mine = gs.unsqueeze(3).to_broadcast(sh)
            other = gs.unsqueeze(2).to_broadcast(sh)
            c4 = [small[:, i, :, :].rearrange("p t (a b) -> p t a b", b=4) for i in range(1, 4)]
            dve.run(nc.vector.tensor_tensor(c4[0], other, mine, ALU.is_gt))
            e = dve.run(nc.vector.tensor_tensor(c4[1], other, mine, ALU.is_equal))
            yield
            dve.after(e)
            e = dve.run(nc.vector.tensor_tensor(small[:, 2, :, :], small[:, 2, :, :],
                                                order[:, 0:16].unsqueeze(1).to_broadcast([P, BT, 16]), ALU.mult))
            dve.after(e)
            e = dve.run(nc.vector.tensor_tensor(small[:, 3, :, :], small[:, 1, :, :], small[:, 2, :, :], ALU.add))
            dve.after(e)
            e = dve.run(nc.vector.tensor_reduce(small[:, 4, :, 0:4], c4[2], AX.X, ALU.add))
            yield
            dve.after(e)
            e = dve.run(nc.vector.tensor_scalar(small[:, 5, :, 0:4], small[:, 4, :, 0:4], 2.0, None, ALU.is_lt))
            dve.after(e)
            e = dve.run(nc.vector.tensor_tensor(masked.rearrange("p t (g k) -> p t g k", k=8), choice.rearrange("p t (g k) -> p t g k", k=8),
                                                small[:, 5, :, 0:4].unsqueeze(3).to_broadcast([P, BT, 4, 8]), ALU.mult))
            dve.after(e)
            e = dve.run(nc.vector.tensor_scalar(masked, masked, 0.0, None, ALU.add))
            yield
            dve.after(e)
            for t in range(BT):
                e = dve.run(nc.vector.max(small[:, 0, t, 8:16], masked[:, t, :]))
            dve.after(e)
            for t in range(BT):
                e = dve.run(nc.vector.match_replace(sel[:, t, :], small[:, 0, t, 8:16], masked[:, t, :], -BIG))
            yield
            dve.after(e)
            e = dve.run(nc.vector.scalar_tensor_tensor(sel, sel, -BIG, scores, ALU.is_equal, ALU.mult))
            dve.after(e)
            tot = small[:, 1, :, 0]
            e = dve.run(nc.vector.tensor_reduce(tot, sel, AX.X, ALU.add))
            dve.after(e)
            e = dve.run(nc.vector.tensor_scalar(tot, tot, 1e-20, None, ALU.add))
            yield
            dve.after(e)
            e = dve.run(nc.vector.reciprocal(tot, tot))
            dve.after(e)
            e = dve.run(nc.vector.tensor_scalar(tot, tot, 2.5, None, ALU.mult))
            dve.after(e)
            e = dve.run(nc.vector.tensor_tensor(w, sel, small[:, 1, :, 0:1].to_broadcast([P, BT, E0]), ALU.mult))
            yield
            dve.after(e, weights.get(blk - 1))
            e = dve.run(nc.vector.tensor_copy(wparts[:, :, 0, :], w))
            dve.after(e)
            e = dve.run(nc.vector.tensor_tensor(r, w, wparts[:, :, 0, :], ALU.subtract))
            dve.after(e)
            e = dve.run(nc.vector.tensor_copy(wparts[:, :, 1, :], r))
            dve.after(e)
            e = dve.run(nc.vector.tensor_tensor(wparts[:, :, 2, :], r, wparts[:, :, 1, :], ALU.subtract))
            yield
            yield
            yield
            b16 = bank[n].bitcast(BF16)
            pe.after(e, free[n])
            for i in range(BT):
                e = pe.run(nc.tensor.transpose(b16[0:96, i * P:(i + 1) * P], wparts[:, i].rearrange("p j h -> p (j h)"), ident16[:, :]))
            act.after(e)
            free[n] = weights[blk] = act.run(nc.scalar.activation(wT[:, blk * BLK:(blk + 1) * BLK], b16[0:96, 0:BLK], ACT.Copy))

        def ffn_0(xT_ready, last_heads, prob_read, background, done):
            w_loaded = scratch["weights"]
            for q in (act, dve, sp):
                q.after(prob_read)
            sel_loaded = ld_w.start(sp, sel0[:, :, :], A["c_sel0"].bitcast(BF16))
            w_ready = {}

            def split_weights(u):
                nat, hi = e_nat[:, u, :, :], eh[:, u, :, :]
                act.after(w_loaded)
                a = act.run(nc.scalar.activation(hi, nat, ACT.Copy))
                dve.after(w_loaded, a)
                w_ready[u] = dve.run(nc.vector.tensor_tensor(e_lo[:, u, :, :], nat, hi.bitcast(FP32), ALU.subtract))

            blocks = Blocks(silu0, hid0, yT0)
            split_weights(EP)
            jobs = [itertools.chain(last_heads, *(routing(blk, xT_ready, SIDE, ACT.Sigmoid) for blk in range(2, NB)))]
            for blk in range(NB):
                for n, u in enumerate([EP] + list(range(EP))):
                    if blk == 0 and n < EP:
                        split_weights(n)
                    if n == 1:
                        pe.after(weights[blk], sel_loaded)
                    pe.after(w_ready[u])
                    gu = [[part[:, u, i, :] for part in (eh, e_lo)] for i in range(2)]
                    blocks.unit(blk, P, gu, xT_ready, sel0[:, u, :] if u < EP else None, down0[:, u, :], n == 0, n == EP, background)
                    if n == 2 and blk:
                        done[blk - 1] = blocks.finish(blk - 1)
                    advance(jobs)
                    if blk == 0:
                        advance(jobs)
                    next(background, None)
            blocks.flush()
            done[NB - 1] = blocks.finish(NB - 1)
            list(background)

        def ffn_1(xT_ready):
            w_loaded = scratch["weights"]
            rw = split(rt_nat[:, 0:E1], rt_w[:, 0, 0:E1], rt_w[:, 1, 0:E1], w_loaded)
            logits = router_logits(SIDE, range(TT), xT_ready, E1, rw)

            def split_weights(u):
                return split(w_nat[:, u, :, :], gu1[:, u, :, 0, :], gu1[:, u, :, 1, :], w_loaded)

            shared_ready = split_weights(E1)
            act.after(logits)
            scores, eq, sel = (choice1[:, i, :, :] for i in range(3))
            gates, rank = choice1[:, 3, :, :], choice1[:, 4, :, :]
            e = act.run(nc.scalar.activation(scores, bank[5][:, 0:TT * E1].rearrange("p (t e) -> p t e", e=E1), ACT.Copy))
            act.after(e)
            free[5] = g = act.run(nc.scalar.activation(gates, scores, ACT.Sigmoid))
            dve.after(e)
            best, gate, place = (per_token[:, i, :].unsqueeze(2) for i in range(3))

            def over_experts(out, in_, op, ready):
                dve.after(ready)
                return dve.run(nc.vector.tensor_reduce(out.rearrange("p t o -> p (t o)"), in_, AX.X, op))

            e = over_experts(best, scores, ALU.max, e)
            dve.after(e)
            e = dve.run(nc.vector.tensor_tensor(eq, scores, best.to_broadcast([P, TT, E1]), ALU.is_equal))
            dve.after(e)
            e = dve.run(nc.vector.tensor_tensor(eq, eq, order[:, 16:16 + E1].unsqueeze(1).to_broadcast([P, TT, E1]), ALU.mult))
            e = over_experts(best, eq, ALU.max, e)
            dve.after(e)
            chosen = dve.run(nc.vector.tensor_tensor(sel, eq, best.to_broadcast([P, TT, E1]), ALU.is_equal))
            dve.after(chosen, g)
            sel16_ready = dve.run(nc.vector.tensor_copy(sel16[:, :, :], sel))
            e = dve.run(nc.vector.tensor_tensor(gates, gates, sel, ALU.mult))
            e = over_experts(gate, gates, ALU.add, e)
            dve.after(e)
            gate_ready = dve.run(nc.vector.tensor_tensor(gate.rearrange("p t o -> p (t o)"), gate.rearrange("p t o -> p (t o)"), rstd[:, 2, :], ALU.mult))

            blocks = Blocks(silu1, hid1, yT1)
            pe.after(w_loaded, shared_ready)
            done = {}

            def shared_units(first, count):
                for n in range(first, first + count):
                    blk, c = n // len(FC), n % len(FC)
                    f0, fn = FC[c]
                    gu = [[gu1[:, E1, i, j, f0:f0 + fn] for j in range(2)] for i in range(2)]
                    blocks.unit(blk, fn, gu, xT_ready, None, down1[0:fn, E1, c, :], c == 0, c == len(FC) - 1)
                    if c == 1 and blk:
                        done[blk - 1] = blocks.finish(blk - 1)

            shared_units(0, 2)
            ranks = bank[4][:, 0:TT * E1].rearrange("p (t e) -> p t e", e=E1)
            totals = bank[4][:, TT * E1:(TT + 1) * E1]
            pe.after(sel16_ready, free[4], const_ready)
            nc.tensor.matmul(ranks, before16[:, 0, :], sel16[:, :, :], start=True, stop=False)
            for k in range(1, TT):
                nc.tensor.matmul(ranks[:, k:TT, :], before16[:, 1, :], sel16[:, 0:TT - k, :], start=False, stop=k == TT - 1)
            for t in range(TT):
                e = nc.tensor.matmul(totals, before16[:, 1, :], sel16[:, t, :], start=t == 0, stop=t == TT - 1)
            counted = pe.run(e)
            shared_units(2, 1)
            o = 16 + E1
            steps = order[:, o:o + TT].unsqueeze(1).to_broadcast([P, E1, TT])
            before = order[:, o + TT:o + TT + E1 * E1].rearrange("p (a b) -> p a b", b=E1)
            numbers = order[:, o + TT + E1 * E1:o + TT + E1 * E1 + TILES]
            tiles_of, first_tile, end_tile = (plan[:, i, 0:E1] for i in range(3))
            grid = plan[:, 3:5, :].rearrange("p a b -> p (a b)")
            dve.after(counted)
            g3 = grid[:, 0:E1 * TT].rearrange("p (e k) -> p e k", k=TT)
            e = dve.run(nc.vector.tensor_tensor(g3, totals.unsqueeze(2).to_broadcast([P, E1, TT]), steps, ALU.is_gt))
            dve.after(e)
            e = dve.run(nc.vector.tensor_reduce(tiles_of, g3, AX.X, ALU.add))
            dve.after(e)
            g3 = grid[:, 0:E1 * E1].rearrange("p (a b) -> p a b", b=E1)
            e = dve.run(nc.vector.tensor_tensor(g3, tiles_of.unsqueeze(1).to_broadcast([P, E1, E1]), before, ALU.mult))
            dve.after(e)
            e = dve.run(nc.vector.tensor_reduce(first_tile, g3, AX.X, ALU.add))
            dve.after(e)
            free[4] = r = dve.run(nc.vector.scalar_tensor_tensor(rank, first_tile.unsqueeze(1).to_broadcast([P, TT, E1]), float(P), ranks, ALU.mult, ALU.add))
            e = dve.run(nc.vector.tensor_tensor(end_tile, first_tile, tiles_of, ALU.add))
            dve.after(r)
            r = dve.run(nc.vector.tensor_tensor(rank, rank, sel, ALU.mult))
            r = over_experts(place, rank, ALU.add, r)
            dve.after(r)
            placed = dve.run(nc.vector.tensor_copy(row_of[:, :], place.rearrange("p t o -> p (t o)")))
            e2 = dve.run(nc.vector.tensor_copy(gx[:, :, D], order[:, ORDER - TT:ORDER]))
            dve.after(gate_ready)
            sc = transfers("sorted")
            pool.after(placed, e2, scratch["set"])
            for t in range(TT):
                pool.after(dve.run(nc.vector.tensor_scalar(gx[:, t, 0:D], x[:, t, :], mv[:, t, 0:1], per_token[:, 1, t:t + 1], ALU.subtract, ALU.mult)))
                sorted_ = sc.scatter(pool, rows_in, row_of[:, t:t + 1], gx[:, t, :])
                if t == 3:
                    dve.after(e)
                    g3 = grid[:, 0:TILES * (E1 - 1)].rearrange("p (j e) -> p j e", e=E1 - 1)
                    i = dve.run(nc.vector.tensor_tensor(g3, end_tile[:, 0:E1 - 1].unsqueeze(1).to_broadcast([P, TILES, E1 - 1]),
                                                        numbers.unsqueeze(2).to_broadcast([P, TILES, E1 - 1]), ALU.is_le))
                    dve.after(i)
                    i = dve.run(nc.vector.tensor_reduce(plan[:, 5, 0:TILES], g3, AX.X, ALU.add))
                    dve.after(i)
                    experts_known = dve.run(nc.vector.tensor_copy(expert_of[:, :], plan[:, 5, 0:TILES]))
            groups = [range(g, min(g + 4, TILES)) for g in range(0, TILES, 4)]
            sp.after(sorted_)
            loaded = []
            for i, g in enumerate(groups):
                loaded.append(ld_rows[i].start(sp, rows[:, g[0]:g[-1] + 1, :], rows_in.rearrange("(t p) d -> p t d", p=P)[:, g[0]:g[-1] + 1, :]))
            for n in range(3, 12):
                shared_units(n, 1)
                if n - 3 < E1:
                    w_ready = split_weights(n - 3)
            blocks.flush()
            done[NB - 1] = blocks.finish(NB - 1)

            turned, numbers_known = {}, {}
            pe.after(w_ready, experts_known)

            def turn(i):
                g = groups[i]
                n = len(g) * P
                pe.after(loaded[i], free[4])
                for k, j in enumerate(g):
                    e = pe.run(nc.tensor.transpose(bank[4][:, k * P:(k + 1) * P], rows[:, j, 0:D], ident[:, :]))
                act.after(e, gu_done.get(groups[i - 2][-1]) if i > 1 else None)
                a = act.run(nc.scalar.activation(gxT[:, i % 2, 0, 0:n], bank[4][:, 0:n], ACT.Copy))
                dve.after(e, a)
                free[4] = turned[i] = dve.run(nc.vector.tensor_tensor(gxT[:, i % 2, 1, 0:n], bank[4][:, 0:n], gxT[:, i % 2, 0, 0:n].bitcast(FP32), ALU.subtract))
                numbers_known[i] = dve.run(nc.vector.tensor_copy(token_of[:, g[0]:g[-1] + 1], rows[:, g[0]:g[-1] + 1, D]))

            gu_done, hid_ready, hidT_ready, hidT_read, hid_read, expert = {}, {}, {}, {}, {}, {}
            scattered = transfers("scattered")
            F = slice(0, F1)

            def gate_up(j):
                i, k, m = j // 4, j % 4, j % 2
                expert[j] = ev = nc.tensor.value_load(expert_of[0:1, j:j + 1], min_val=0, max_val=E1 - 1)
                pe.after(turned[i])
                xs = [gxT[:, i % 2, part, k * P:(k + 1) * P] for part in range(2)]
                for which, n in ((0, m), (1, 2 + m)):
                    w = [gu1[:, bass.ds(ev, 1), which, part, :].rearrange("p o f -> p (o f)") for part in range(2)]
                    pe.after(free[n])
                    e = parts3(bank[n][:, F], xs[0], xs[1], w[0], w[1])
                    if which == 0:
                        act.after(e, hid_ready.get(j - 2))
                        free[n] = s = act.run(nc.scalar.activation(silu1[:, m, F], bank[n][:, F], ACT.Silu))
                gu_done[j] = e
                dve.after(e, s, hid_read.get(j - 2))
                free[n] = hid_ready[j] = dve.run(nc.vector.tensor_tensor(mid[:, m, F], bank[n][:, F], silu1[:, m, F], ALU.mult))

            def turn_hidden(j):
                m = j % 2
                pe.after(hid_ready[j], free[5])
                for c, (f0, fn) in enumerate(FC):
                    e = pe.run(nc.tensor.transpose(bank[5][0:fn, c * P:(c + 1) * P], mid[:, m, f0:f0 + fn], ident[:, :]))
                hid_read[j] = e
                act.after(e, hidT_read.get(j - 2))
                a = act.run(nc.scalar.activation(hid1[:, m, 0:2 * P], bank[5][:, 0:2 * P], ACT.Copy))
                dve.after(e, a)
                d = dve.run(nc.vector.tensor_copy(hid1[0:FC[2][1], m, 2 * P:3 * P], bank[5][0:FC[2][1], 2 * P:3 * P]))
                free[5] = hidT_ready[j] = d

            def down(j):
                i, k = j // 4, j % 4
                n = 6 + i % 2
                pe.after(hidT_ready[j])
                if k == 0:
                    pe.after(free[n])
                for c, (f0, fn) in enumerate(FC):
                    w2 = down1[0:fn, bass.ds(expert[j], 1), c, :].rearrange("p o f -> p (o f)")
                    e = nc.tensor.matmul(bank[n][:, k * P:(k + 1) * P], hid1[0:fn, j % 2, c * P:(c + 1) * P], w2, start=c == 0, stop=c == 2)
                hidT_read[j] = e = pe.run(e)
                if j == groups[i][-1]:
                    g = groups[i]
                    act.after(e, turned[i])
                    free[n] = a = act.run(nc.scalar.activation(rows[:, g[0]:g[-1] + 1, 0:D], bank[n][:, 0:len(g) * P].rearrange("p (t d) -> p t d", d=P), ACT.Copy))
                    pool.after(a, numbers_known[i])
                    for t in g:
                        back = scattered.scatter(pool, rows_out, token_of[:, t:t + 1], rows[:, t, 0:D])
                    return back

            turn(0)
            for j in range(TILES + 2):
                if j < TILES:
                    gate_up(j)
                if j % 4 == 1 and j // 4 + 1 < len(groups):
                    turn(j // 4 + 1)
                if 0 <= j - 1 < TILES:
                    turn_hidden(j - 1)
                if j >= 2:
                    back = down(j - 2) or back if j > 2 else down(0)
            sp.after(back)
            for blk in range(NB):
                ts = slice(4 * blk, 4 * blk + 4)
                e = ld_back[blk].start(sp, gx[:, ts, 0:D], rows_out.rearrange("(t p) d -> p t d", p=P)[:, ts, :])
                dve.after(e, done[blk])
                done[blk] = dve.run(nc.vector.tensor_tensor(x[:, ts, :], gx[:, ts, 0:D], x[:, ts, :], ALU.add))
            return done

        x_loaded, layer0_done = {blk: x_ready for blk in range(NB)}, {}
        xT_ready, last_heads, prob_read = to_the_end(xattn(0, x_loaded))()
        start_1 = {}

        def layer1_start():
            yield from itertools.repeat(None, START1)
            attention_done = [(q.sem, q.count) for q in engines if q.count]
            sp.after(attention_done)
            pool.after(attention_done)
            start_1["heads"] = yield from xattn(1, layer0_done)

        ffn_0(xT_ready, last_heads, prob_read, layer1_start(), layer0_done)
        everybody()
        xT_ready, last_heads, _ = start_1["heads"]()
        list(last_heads)
        everybody()
        done = ffn_1(xT_ready)
        st = transfers("store")
        for blk in range(NB):
            sp.after(done[blk])
            stored = st.start(sp, out[:, 4 * blk:4 * blk + 4, :], x[:, 4 * blk:4 * blk + 4, :])
        sp.after(stored)


def constants():
    import numpy as np
    ident = np.eye(P, dtype=np.float32)
    experts = np.arange(E1)
    order = [(np.arange(4)[None, :] < np.arange(4)[:, None]).reshape(-1),
             E1 - experts,
             P * np.arange(TT),
             (experts[None, :] < experts[:, None]).reshape(-1),
             np.arange(TILES)]
    order = np.concatenate([np.tile(np.concatenate(order), (P, 1)),
                            np.arange(P)[:, None] + P * np.arange(TT)[None, :]], 1).astype(np.float32)
    rows = np.zeros((TILES * P, D + 1), np.float32)
    rows[:, D] = T + np.arange(TILES * P)
    before = np.stack([np.arange(P)[:, None] < np.arange(P)[None, :], np.ones((P, P), bool)], 1) * np.uint16(0x3F80)
    sel0 = np.zeros((96, EP, P), np.uint16)
    for part in range(3):
        for e in range(E0):
            sel0[32 * part + e, e // 2, 64 * (e % 2):64 * (e % 2) + 64] = 0x3F80
    half = np.arange(0, HD, 2, dtype=np.float32) / np.float32(HD)
    inv = (np.float32(1.0) / np.power(np.float32(10000.0), half)).astype(np.float32)
    angle = (np.arange(SK, dtype=np.float32)[:, None] * inv[None, :]).astype(np.float32)
    rope = np.zeros((P, 2, SK), np.float32)
    for row in range(P):
        d = row % 64 // PAIRS
        a = angle[:, d % (HD // 2)].astype(np.float64)
        rope[row, 0] = np.cos(a)
        rope[row, 1] = np.sin(a) * (-1.0 if d < HD // 2 else 1.0)
    return {"c_ones": np.full((STACK - MASK_ROW, H * SQ), 0x3F80, np.uint16), "c_ident": ident, "c_order": order, "c_sel0": sel0, "c_before": before, "c_rows": rows, "c_rope": rope}


def laid_out(a):
    import numpy as np
    a = {k: np.asarray(v) for k, v in a.items()}

    def tiles(v):
        return v.reshape(TT, P, D).transpose(1, 0, 2)

    def stacked(w):
        return w.reshape(*w.shape[:-1], PAIRS, 2, HD).swapaxes(-3, -2).swapaxes(-2, -1).reshape(w.shape)

    def half(w):
        return np.roll(w.reshape(*w.shape[:-1], H, HD), HD // 2, axis=-1).reshape(w.shape)

    r = {"x": tiles(a["x"]), "ctxT": a["ctx_1024"].reshape(-1, D).T, "mask": a["mask_Bx1x1xS2_ff0"].reshape(B, SK)}
    for layer, names in ((0, ["wq", "wk", "wv", "wo"]), (1, ["Wq", "Wk", "Wv", "Wo"])):
        pre = f"L{layer}_xattn_"
        wq, wk, wv, wo = (a[pre + n] if layer == 0 else a[pre + n].T for n in names)
        bq, bk = a[pre + "bq"], a[pre + "bk"]
        r[f"L{layer}_w"] = np.stack([stacked(wq), stacked(wk), stacked(half(wq)), stacked(half(wk)), wv], 1)
        r[f"L{layer}_b"] = np.stack([stacked(bq), stacked(bk), stacked(half(bq)), stacked(half(bk))], 1)
        r[f"L{layer}_wo"], r[f"L{layer}_bv"], r[f"L{layer}_bo"] = wo, a[pre + "bv"], a[pre + "bo"]
    pre = "L0_ffn_"
    gu = [np.concatenate([a[pre + "expert_" + n].reshape(EP, P, D), a[pre + "shared_" + n][None]]) for n in ("gate", "up")]
    r["L0_gu"] = np.stack(gu, 1).transpose(3, 0, 1, 2)
    down = a[pre + "expert_down"].transpose(0, 2, 1).reshape(EP, P, D)
    r["L0_down"] = np.concatenate([down, a[pre + "shared_down"].T[None]]).transpose(1, 0, 2)
    r["L0_router"], r[pre + "gate_bias"] = a[pre + "gate_w"].T, a[pre + "gate_bias"]
    pre = "L1_ffn_"
    gu = [np.concatenate([a[pre + f"w{n}_eDF"], a[pre + f"ws{n}_DF"][None]]) for n in (1, 3)]
    r["L1_gu"] = np.stack(gu, 1).transpose(2, 0, 1, 3)
    for n in ("w2_eFD", "ws2_FD", "router_DE"):
        r[pre + n] = a[pre + n]
    return r


def kernel(**inputs):
    import numpy as np
    import concourse.bacc as bacc
    from concourse.bass_utils import run_bass_kernel_spmd

    nc = bacc.Bacc("TRN2", target_bir_lowering=False, num_devices=1)
    arrays, aps = {}, {}
    for name, value in {**laid_out(inputs), **constants()}.items():
        a = np.ascontiguousarray(value)
        arrays[f"in_{name}"] = a
        aps[name] = nc.dram_tensor(f"in_{name}", a.shape, mybir.dt.from_np(a.dtype), kind="ExternalInput").ap()
    out = nc.dram_tensor("out_x", (P, TT, D), FP32, kind="ExternalOutput").ap()
    build(nc, aps, out)
    r = run_bass_kernel_spmd(nc, [arrays], core_ids=[0])
    return r.results[0]["out_x"].transpose(1, 0, 2).reshape(B, SQ, D)
```

```python
import itertools
import math
from contextlib import ExitStack

import concourse.bass as bass
from concourse import mybir

FP32 = mybir.dt.float32
F32R = mybir.dt.float32r
BF16 = mybir.dt.bfloat16
I32 = mybir.dt.int32
ALU = mybir.AluOpType
ACT = mybir.ActivationFunctionType
AX = mybir.AxisListType

P = 128
B, SQ, SK, D, H = 8, 256, 512, 128, 16
HD = D // H
PAIRS = H // 2
T = B * SQ
TT = T // P
QT = SQ // P
KC = SK // P
EPS = 1e-5
SCALE = 1.0 / math.sqrt(HD)
TERMS = [(0, 0), (0, 1), (1, 0), (0, 2), (2, 0), (1, 1)]
HROWS = HD * len(TERMS)
MASK_ROW = 2 * HROWS
MAX_ROW = MASK_ROW + 3
STACK = MAX_ROW + 3
VC = HD + 1
E0, GROUPS = 32, 4
EP = E0 // 2
E1, F1 = 8, 352
FC = [(0, 128), (128, 128), (256, 96)]
BLK = 512
NB = T // BLK
BT = BLK // P
TILES = T // P + E1 - 1
COLUMNS, ORDER = {}, 0
for _name, _width in (("groups_before", GROUPS * GROUPS), ("precedence", E1), ("full_tiles", TT),
                      ("experts_before", E1 * E1), ("tile", TILES), ("token", TT)):
    COLUMNS[_name] = slice(ORDER, ORDER + _width)
    ORDER += _width
BIG = 1e30

EXTRA_STEPS = [{*range(1, 32, 2)}, {*range(1, 32, 2), *range(0, 32, 4)}]
TRANSPOSE_AT = 3
ROUTED_EARLY = 2
LAYER1_AT = 18
SHARED_EARLY = 5


class Queue:

    def __init__(self, engine, sem):
        self.engine, self.sem, self.count, self.seen = engine, sem, 0, {}

    def after(self, *events):
        for event in events:
            if event is None:
                continue
            if isinstance(event, list):
                self.after(*event)
                continue
            sem, value = event
            if self.seen.get(sem.name, 0) < value:
                self.engine.wait_ge(sem, value)
                self.seen[sem.name] = value

    def run(self, instruction):
        instruction.then_inc(self.sem, 1)
        self.count += 1
        return self.sem, self.count


class Transfers:

    def __init__(self, sem):
        self.sem, self.count = sem, 0

    def start(self, queue, out, in_):
        queue.engine.dma_start(out, in_).then_inc(self.sem, 16)
        self.count += 16
        return self.sem, self.count

    def scatter(self, queue, out, rows, in_):
        queue.engine.indirect_dma_start(out, bass.IndirectOffsetOnAxis(ap=rows, axis=0), in_, None).then_inc(self.sem, 16)
        self.count += 16
        return self.sem, self.count


def build(nc, A, out):
    stack = ExitStack()
    with stack:
        def sem(name):
            return stack.enter_context(nc.semaphore(name))

        def sbuf(name, shape, dt, scope=stack):
            return scope.enter_context(nc.sbuf_tensor(name, shape, dt))

        pe = Queue(nc.tensor, sem("pe_done"))
        act = Queue(nc.scalar, sem("act_done"))
        dve = Queue(nc.vector, sem("dve_done"))
        pool = Queue(nc.gpsimd, sem("pool_done"))
        sp = Queue(nc.sync, sem("sp_done"))
        engines = (pe, act, dve, pool, sp)

        def transfers(name):
            return Transfers(sem(name))

        x = sbuf("x", [P, TT, D], FP32)
        ident = sbuf("ident", [P, P], FP32)
        ident16 = sbuf("ident16", [P, P], BF16)
        order = sbuf("order", [P, ORDER], FP32)
        before16 = sbuf("before16", [P, 2, P], BF16)
        xT = sbuf("xT", [P, 2, T], F32R)
        stats = sbuf("stats", [P, TT, 6], FP32)
        mv = sbuf("mv", [P, TT, 2], FP32)
        rstd = sbuf("rstd", [P, 3, TT], FP32)
        wnat = sbuf("wnat", [P, 5, D], FP32)
        col = sbuf("col", [P, 4], FP32)
        wo = sbuf("wo", [P, D], FP32)
        rt_nat = sbuf("rt_nat", [P, E0], FP32)
        rt_w = sbuf("rt_w", [P, 2, E0], F32R)
        gate_bias = sbuf("gate_bias", [P, E0], FP32)
        bv = sbuf("bv", [P, D], FP32)
        bo = sbuf("bo", [P, D], FP32)
        wscope = ExitStack()
        e_nat = sbuf("e_nat", [P, EP + 1, 2, D], FP32, wscope)
        wscope.close()
        e_lo = sbuf("e_lo", [P, EP + 1, 2, D], F32R, wscope)
        down0 = sbuf("down0", [P, EP + 1, D], FP32, wscope)
        route = sbuf("route", [P, 6, BT, E0], FP32, wscope)
        small = sbuf("small", [P, 6, BT, 16], FP32, wscope)
        wparts = sbuf("wparts", [P, BT, 3, E0], BF16, wscope)
        wT = sbuf("wT", [96, T], BF16, wscope)
        yT0 = sbuf("yT0", [P, 1, BLK], FP32, wscope)
        wscope.close()
        w_nat = sbuf("w_nat", [P, E1 + 1, 2, F1], FP32)
        down1 = sbuf("down1", [P, E1 + 1, 3, D], FP32)

        gscope = ExitStack()
        gu1 = sbuf("gu1", [P, E1 + 1, 2, 2, F1], F32R, gscope)
        gscope.close()
        ctx_nat = sbuf("ctx_nat", [P, SK], FP32)
        kstack = [sbuf(f"kstack{i}", [P, PAIRS, SK], BF16) for i in range(3)]
        qstack = [sbuf(f"qstack{i}", [P, H, SQ], BF16) for i in range(3)]

        scope = ExitStack()
        aw = sbuf("aw", [P, 4, 2, D], F32R, scope)
        ctxT = sbuf("ctxT", [P, 2, SK], F32R, scope)
        xqT = sbuf("xqT", [P, 2, SQ], F32R, scope)
        kparts = sbuf("kparts", [P, 3, 2, SK], BF16, scope)
        qparts = sbuf("qparts", [P, 3, SQ], BF16, scope)
        vaug = sbuf("vaug", [P, 3 * KC, H * VC + 23], FP32, scope)
        rscope = ExitStack()
        maskp = sbuf("maskp", [B, 3, SK], BF16, rscope)
        rscope.close()
        rope = sbuf("rope", [P, 2, SK], FP32, scope)
        work = sbuf("work", [P, 3, SK], FP32, scope)
        xn = sbuf("xn", [P, 4, D], FP32, scope)
        negmax = sbuf("negmax", [P, 2, H, QT], FP32, scope)
        mrest = sbuf("mrest", [P, QT, H // 2], FP32, scope)
        mparts = sbuf("mparts", [P, 2, QT, 3, H // 2], BF16, scope)
        mT = sbuf("mT", [24, 2, SQ], BF16, scope)
        ffn0 = ExitStack()
        eh = sbuf("eh", [P, EP + 1, 2, D], F32R, ffn0)
        sel0 = sbuf("sel0", [96, EP, P], BF16, ffn0)
        silu0 = sbuf("silu0", [P, 2, BLK], FP32, ffn0)
        hid0 = sbuf("hid0", [P, 3, BLK], FP32, ffn0)
        ffn0.close()
        mscope = ExitStack()
        mask8 = sbuf("mask8", [B, 2, SK], FP32, mscope)
        mscope.close()
        prob = sbuf("prob", [P, 2, 2, KC, 2 * SQ], FP32, scope)
        oT = sbuf("oT", [P, 2, 2, 2 * SQ], FP32, scope)
        o_norm = sbuf("o_norm", [P, 2, D], FP32, scope)
        o_normT = sbuf("o_normT", [P, 2, D], FP32, scope)
        rsum = sbuf("rsum", [P, 2, H], FP32, scope)
        scope.close()

        ffn1 = ExitStack()
        choice1 = sbuf("choice1", [P, 5, TT, E1], FP32, ffn1)
        per_token = sbuf("per_token", [P, 3, TT], FP32, ffn1)
        silu1 = sbuf("silu1", [P, 2, BLK], FP32, ffn1)
        hid1 = sbuf("hid1", [P, 3, BLK], FP32, ffn1)
        mid = sbuf("mid", [P, 2, F1], FP32, ffn1)
        yT1 = sbuf("yT1", [P, NB, BLK], FP32, ffn1)
        logitsT1 = sbuf("logitsT1", [E1, NB, BLK], FP32, ffn1)
        sel16 = sbuf("sel16", [P, TT, E1], BF16, ffn1)
        plan = sbuf("plan", [P, 6, 84], FP32, ffn1)
        row_of = sbuf("row_of", [P, TT], I32, ffn1)
        expert_of = sbuf("expert_of", [P, TILES], I32, ffn1)
        token_of = sbuf("token_of", [P, TILES], I32, ffn1)
        gx = sbuf("gx", [P, TT, D + 1], FP32, ffn1)
        rows = sbuf("rows", [P, TILES, D + 1], FP32, ffn1)
        gxT = sbuf("gxT", [P, 2, 2, 4 * P], F32R, ffn1)
        ffn1.close()

        def psum(name, banks):
            return stack.enter_context(nc.psum_tensor(name, [P, 512 * banks], FP32))

        bank = [psum(f"bank{i}", 1)[:, :] for i in range(8)]
        NS, NT = 3, 2
        S0, T0, O, M0, M1 = 0, NS, NS + NT, 6, 7
        WEIGHT, SIDE, SUM = 4, 5, 6
        free = [None] * 8

        def advance(jobs):
            for job in list(jobs):
                if next(job, "end") == "end":
                    jobs.remove(job)

        def to_the_end(steps):
            while True:
                try:
                    next(steps)
                except StopIteration as end:
                    return end.value

        def everybody():
            ends = [(q.sem, q.count) for q in engines if q.count]
            for q in engines:
                q.after(*ends)

        def parts3(hi, whi, wlo, xhi, xlo):
            nc.tensor.matmul(hi, whi, xhi, start=True, stop=False)
            nc.tensor.matmul(hi, whi, xlo, start=False, stop=False)
            return pe.run(nc.tensor.matmul(hi, wlo, xhi, start=False, stop=True))

        def split(src, hi, lo, ready):
            act.after(ready)
            a = act.run(nc.scalar.activation(hi, src, ACT.Copy))
            dve.after(ready, a)
            return dve.run(nc.vector.tensor_tensor(lo, src, hi.bitcast(FP32), ALU.subtract))

        ld_x, ld_ident, ld_w = transfers("ld_x"), transfers("ld_ident"), transfers("ld_w")
        ld_ctx = [transfers(f"ld_ctx{i}") for i in range(2)]
        ld_x0, ld_qkv = transfers("ld_x0"), transfers("ld_qkv")
        x0_ready = ld_x0.start(sp, x[:, 0:QT, :], A["x"][:, 0:QT, :])
        ident_loaded = ld_ident.start(act, ident[:, :], A["c_ident"])
        exponent = dve.run(nc.vector.memset(rstd[:, 1, :], -0.5))

        ld_k = [transfers(f"ld_k{i}") for i in range(3)]
        ld_q = [transfers(f"ld_q{i}") for i in range(3)]
        ld_q_first = transfers("ld_q_first")
        ld_m = [transfers(f"ld_m{i}") for i in range(2)]
        ld_zero = transfers("ld_zero")
        ld_ffn, ld_ones = transfers("ld_ffn"), transfers("ld_ones")

        for i in range(3):
            q = dve if i == 0 else pool
            zeros_set = q.run(q.engine.memset(qstack[i][:, :, :].bitcast(FP32)[0:MASK_ROW], 0.0))
            ld_ones.start(act, qstack[i][MASK_ROW:STACK, :, :], A["c_ones"].bitcast(BF16).rearrange("r (h n) -> r h n", h=H))
            ones_set = ld_ones.start(act, kstack[i][MASK_ROW:STACK, :, :], A["c_ones"].bitcast(BF16).rearrange("r (g n) -> r g n", g=PAIRS))
        rows_in = nc.dram_tensor("rows_in", (TILES * P, D + 1), FP32, kind="Internal").ap()
        rows_out = nc.dram_tensor("rows_out", (T + TILES * P, D), FP32, kind="Internal").ap()
        ld_rows = [transfers(f"ld_rows{i}") for i in range(-(-TILES // 4))]
        ld_back = [transfers(f"ld_back{i}") for i in range(NB)]
        ld_empty = transfers("ld_empty")
        stacks_set = [(dve.sem, dve.count), zeros_set, ones_set]
        ld_order = transfers("ld_order")
        ld_order.start(act, before16[:, :, :], A["c_before"].bitcast(BF16))
        order_ready = ld_order.start(act, order[:, :], A["c_order"])
        dve.after(ident_loaded)
        ident_ready = dve.run(nc.vector.tensor_copy(ident16[:, :], ident[:, :]))

        def ln_statistics(tiles, x_done):
            dve.after(x_done)
            for t in tiles:
                e = dve.run(nc.vector.bn_stats(stats[:, t, :], x[:, t, :]))
            dve.after(e)
            for t in tiles:
                e = dve.run(nc.vector.bn_aggr(mv[:, t, :], stats[:, t, :]))
            ts = slice(tiles[0], tiles[-1] + 1)
            pool.after(e, exponent)
            e = pool.run(nc.gpsimd.tensor_scalar(rstd[:, 0, ts], mv[:, ts, 1], EPS, None, ALU.add))
            pool.after(e)
            return pool.run(nc.gpsimd.tensor_tensor(rstd[:, 2, ts], rstd[:, 0, ts], rstd[:, 1, ts], ALU.pow))

        def ln_apply(q, tiles, slot, ready, xn_read):
            q.after(ready, xn_read)
            for i, t in enumerate(tiles):
                e = q.run(q.engine.tensor_scalar(xn[:, slot + i, :], x[:, t, :], mv[:, t, 0:1],
                                                    rstd[:, 2, t:t + 1], ALU.subtract, ALU.mult))
            return e

        def xattn(layer, x_ready):
            pre = f"L{layer}_"
            rope_on = layer == 1
            kinds = 4 if rope_on else 2
            ld_qkv.start(sp, wnat[:, :, :], A[pre + "w"])
            qkv_ready = ld_qkv.start(sp, col[:, :], A[pre + "b"])
            ctx_loaded = ld_ctx[0].start(sp, ctx_nat[:, :], A["ctxT"][:, 0:SK])
            ld_w.start(sp, wo[:, :], A[pre + "wo"])
            ld_w.start(sp, bv[:, :], A[pre + "bv"].partition_broadcast(P))
            w_ready = ld_w.start(sp, bo[:, :], A[pre + "bo"].partition_broadcast(P))
            if rope_on:
                w_ready = ld_w.start(sp, rope[:, :, :], A["c_rope"])
            else:
                w_ready = ld_w.start(sp, mask8[:, 0, :], A["mask"])
                x_ready["rest"] = ld_x.start(sp, x[:, QT:, :], A["x"][:, QT:, :])

            yield

            pool.run(nc.gpsimd.memset(vaug[:, :, HD:H * VC:VC], 1.0))
            v_set = pool.run(nc.gpsimd.memset(vaug[:, :, H * VC:], 1.0))
            yield from itertools.repeat(None, 4 * layer)
            dve.after(qkv_ready)
            act.after(qkv_ready)
            e = dve.run(nc.vector.tensor_scalar(wnat[:, 0:kinds:2, :], wnat[:, 0:kinds:2, :], SCALE, None, ALU.mult))
            e2 = dve.run(nc.vector.tensor_scalar(col[:, 0:kinds:2], col[:, 0:kinds:2], SCALE, None, ALU.mult))
            dve.after(e2)
            if layer == 0:
                aw_ready = split(wnat[:, 0:2, :], aw[:, 0:2, 0, :], aw[:, 0:2, 1, :], e)
            else:
                aw_ready = split(wnat[:, 0:4, :], aw[:, 0:4, 0, :], aw[:, 0:4, 1, :], e)

            mask = {}
            if layer == 0:
                def mask_parts():
                    dve.after(w_ready)
                    e = dve.run(nc.vector.tensor_scalar(mask8[:, 0, :], mask8[:, 0, :], -1e9, None, ALU.mult))
                    for i in range(3):
                        dve.after(e)
                        e = dve.run(nc.vector.tensor_copy(maskp[:, i, :], mask8[:, i % 2, :]))
                        if i < 2:
                            dve.after(e)
                            e = dve.run(nc.vector.tensor_tensor(mask8[:, 1 - i % 2, :], mask8[:, i % 2, :], maskp[:, i, :], ALU.subtract))
                    mask["ready"] = e
            else:
                dve.after(w_ready)
                sp.after(dve.run(nc.vector.memset(work[0:3, 0, :].bitcast(BF16)[:, 0:SK], 0.0)))
                for i in range(3):
                    mask["ready"] = ld_zero.start(sp, kstack[i][MASK_ROW:MASK_ROW + 3, :, :],
                                               work[0:3, 0, :].bitcast(BF16)[:, 0:SK].unsqueeze(1).to_broadcast([3, PAIRS, SK]))

            mask_rows = MAX_ROW if layer == 0 else MASK_ROW
            k_loaded, q_loaded, m_loaded, stack_read = {}, {}, {}, {}
            o_read, o_step, mT_event = {}, {}, {}
            exp_done, pv_done, o_copied, s_last = {}, {}, {}, {}
            k_parts, q_parts, v_ready, x_ln, x_free = {}, {}, {}, {}, {}
            work_read = [mask.get("ready"), None]
            ctx_state = {"loaded": {0: ctx_loaded}, "kv_read": None, "xq_read": None}
            xn_read = [None, None]

            def stack_loads(b, which):
                i = b % 3
                if which == "k":
                    sp.after(k_parts[b], stacks_set, mask["ready"], stack_read.get(b - 3))
                    for n, (_, part) in enumerate(TERMS):
                        for r in range(2):
                            row = HROWS * r + HD * n
                            k_loaded[b] = ld_k[i].start(sp, kstack[i][row:row + HD, :, :], kparts[64 * r:64 * r + 64, part, b % 2, :])
                    if layer == 0:
                        for m in range(3):
                            k_loaded[b] = ld_k[i].start(sp, kstack[i][MASK_ROW + m:MASK_ROW + m + 1, :, :],
                                                        maskp[b:b + 1, m:m + 1, :].to_broadcast([1, PAIRS, SK]))
                else:
                    queues = [(sp, ld_q[i]), (pool, ld_q_first) if layer == b == 0 else (sp, ld_q[i])]
                    loaded = {}
                    for n, (part, _) in enumerate(TERMS):
                        for r, (q, group) in enumerate(queues):
                            row = HROWS * r + HD * n
                            q.after(q_parts[b], stacks_set, stack_read.get(b - 3))
                            loaded[q] = group.start(q, qstack[i][row:row + HD, r::2, :], qparts[64 * r:64 * r + 64, part, :])
                    q_loaded[b] = list(loaded.values())

            def prep_context(b):
                e = ctx_state["loaded"][b]
                act.after(e, ctx_state["kv_read"], aw_ready)
                a = act.run(nc.scalar.activation(ctxT[:, 0, :], ctx_nat[:, :], ACT.Copy))
                yield
                pool.after(e, a, v_set)
                e = ctx_state["split"] = pool.run(nc.gpsimd.tensor_tensor(ctxT[:, 1, :], ctx_nat[:, :], ctxT[:, 0, :].bitcast(FP32), ALU.subtract))
                yield

            def prep_ln(b):
                source = b * SQ // BLK if layer else "rest" if b else "first"
                while source not in x_ready:
                    yield
                x_ln[b] = ln_statistics([QT * b, QT * b + 1], x_ready[source])
                yield
                yield
                e = ln_apply(dve if b == 0 else pool, [QT * b, QT * b + 1], 0, x_ln[b], xn_read[0])
                x_ln[b] = e
                pool.after(e, w_ready)
                xs = x[:, QT * b:QT * b + QT, :]
                x_free[b] = pool.run(nc.gpsimd.tensor_tensor(xs, xs, bo[:, :].unsqueeze(1).to_broadcast([P, QT, D]), ALU.add))
                yield

            def prep_k(b):
                hi, mid, lo = (kparts[:, i, b % 2, :] for i in range(3))
                pe.after(ctx_state["split"], aw_ready, free[M1])
                e = parts3(bank[M1], aw[:, 1, 0, :], aw[:, 1, 1, :], ctxT[:, 0, :], ctxT[:, 1, :])
                yield
                if rope_on:
                    dve.after(e, work_read[0])
                    free[M1] = dve.run(nc.vector.scalar_tensor_tensor(work[:, 0, :], bank[M1], col[:, 1:2], rope[:, 0, :], ALU.add, ALU.mult))
                    yield
                    pe.after(free[M1])
                    e = parts3(bank[M1], aw[:, 3, 0, :], aw[:, 3, 1, :], ctxT[:, 0, :], ctxT[:, 1, :])
                    yield
                    dve.after(e, free[M1])
                    free[M1] = e = dve.run(nc.vector.scalar_tensor_tensor(work[:, 1, :], bank[M1], col[:, 3:4], rope[:, 1, :], ALU.add, ALU.mult))
                    side.append(k_rotated_parts(b, e))
                else:
                    act.after(e, k_loaded.get(b - 2))
                    a = act.run(nc.scalar.activation(hi, bank[M1], ACT.Identity, bias=col[:, 1:2]))
                    yield
                    dve.after(a, work_read[0])
                    free[M1] = r = dve.run(nc.vector.scalar_tensor_tensor(work[:, 0, :], bank[M1], col[:, 1:2], hi, ALU.add, ALU.subtract))
                    side.append(k_low_parts(b, r, work[:, 0, :]))

            def k_low_parts(b, ready, rest):
                hi, mid, lo = (kparts[:, i, b % 2, :] for i in range(3))
                yield
                act.after(ready)
                a = act.run(nc.scalar.activation(mid, rest, ACT.Copy))
                yield
                pool.after(a)
                k_parts[b] = work_read[0] = pool.run(nc.gpsimd.tensor_tensor(lo, rest, mid, ALU.subtract))
                yield
                stack_loads(b, "k")

            def k_rotated_parts(b, ready):
                hi, mid, lo = (kparts[:, i, b % 2, :] for i in range(3))
                pool.after(ready)
                e = pool.run(nc.gpsimd.tensor_tensor(work[:, 0, :], work[:, 0, :], work[:, 1, :], ALU.add))
                yield
                yield
                act.after(e, k_loaded.get(b - 2))
                a = act.run(nc.scalar.activation(hi, work[:, 0, :], ACT.Copy))
                yield
                pool.after(a)
                r = pool.run(nc.gpsimd.tensor_tensor(work[:, 1, :], work[:, 0, :], hi, ALU.subtract))
                yield
                yield from k_low_parts(b, r, work[:, 1, :])

            def prep_v(b):
                yield
                pe.after(free[M1], ctx_state["loaded"][b], qkv_ready)
                for c in range(KC):
                    tok = slice(c * P, (c + 1) * P)
                    e = pe.run(nc.tensor.matmul(bank[M1][:, tok], ctx_nat[:, tok], wnat[:, 4, :], start=True, stop=True))
                ctx_state["kv_read"] = e
                if b + 1 < B:
                    sp.after(e, ctx_state["split"])
                    ctx_state["loaded"][b + 1] = ld_ctx[(b + 1) % 2].start(sp, ctx_nat[:, :], A["ctxT"][:, (b + 1) * SK:(b + 2) * SK])
                yield
                dve.after(e, v_set, pv_done.get(KC * (b - 3) + 3))
                free[M1] = v_ready[b] = dve.run(nc.vector.tensor_tensor(
                    vaug[:, KC * (b % 3):KC * (b % 3 + 1), 0:H * VC].rearrange("p c (h v) -> p c h v", v=VC)[:, :, :, 0:HD],
                    bank[M1].rearrange("p (c h v) -> p c h v", c=KC, v=HD),
                    bv[:, :].rearrange("p (h v) -> p h v", v=HD).unsqueeze(1).to_broadcast([P, KC, H, HD]), ALU.add))
                yield

            def prep_x_transpose(b, m=M1):
                pe.after(x_ln[b], free[m], ident_ready)
                for i in range(QT):
                    e = pe.run(nc.tensor.transpose(bank[m][:, i * P:(i + 1) * P], xn[:, i, :], ident[:, :]))
                xn_read[0] = e
                yield
                act.after(e, ctx_state["xq_read"])
                a = act.run(nc.scalar.activation(xqT[:, 0, :], bank[m][:, 0:SQ], ACT.Copy))
                yield
                dve.after(e, a)
                free[m] = ctx_state["xq"] = dve.run(nc.vector.tensor_tensor(xqT[:, 1, :], bank[m][:, 0:SQ], xqT[:, 0, :].bitcast(FP32), ALU.subtract))

            def prep_q(b, m=M1):
                yield
                pe.after(ctx_state["xq"], free[m])
                q, qr = bank[m][:, 0:SQ], bank[m][:, SQ:2 * SQ]
                e = parts3(q, aw[:, 0, 0, :], aw[:, 0, 1, :], xqT[:, 0, :], xqT[:, 1, :])
                if rope_on:
                    e = parts3(qr, aw[:, 2, 0, :], aw[:, 2, 1, :], xqT[:, 0, :], xqT[:, 1, :])
                ctx_state["xq_read"] = e
                hi, mid, lo = (qparts[:, i, :] for i in range(3))
                w0, w1 = work[:, 2, 0:SQ], work[:, 2, SQ:2 * SQ]
                yield
                if rope_on:
                    dve.after(e, work_read[1])
                    dve.run(nc.vector.scalar_tensor_tensor(w0, q, col[:, 0:1], rope[:, 0, 0:SQ], ALU.add, ALU.mult))
                    free[m] = e = dve.run(nc.vector.scalar_tensor_tensor(w1, qr, col[:, 2:3], rope[:, 1, 0:SQ], ALU.add, ALU.mult))
                    pool.after(e)
                    e = pool.run(nc.gpsimd.tensor_tensor(w0, w0, w1, ALU.add))
                    yield
                    act.after(e, q_loaded.get(b - 1))
                    a = act.run(nc.scalar.activation(hi, w0, ACT.Copy))
                    yield
                    pool.after(a)
                    r = pool.run(nc.gpsimd.tensor_tensor(w1, w0, hi, ALU.subtract))
                else:
                    act.after(e, q_loaded.get(b - 1))
                    a = act.run(nc.scalar.activation(hi, q, ACT.Identity, bias=col[:, 0:1]))
                    yield
                    dve.after(a, work_read[1])
                    free[m] = r = dve.run(nc.vector.scalar_tensor_tensor(w1, q, col[:, 0:1], hi, ALU.add, ALU.subtract))
                yield
                act.after(r)
                a = act.run(nc.scalar.activation(mid, w1, ACT.Copy))
                yield
                pool.after(a)
                q_parts[b] = work_read[1] = pool.run(nc.gpsimd.tensor_tensor(lo, w1, mid, ALU.subtract))
                yield
                stack_loads(b, "q")

            side = []

            def prep(b):
                for job in (prep_context, prep_ln, prep_k, prep_v, prep_x_transpose, prep_q):
                    yield from job(b)
                    yield

            def first_prep():
                def queries():
                    yield from prep_ln(0)
                    mask_parts()
                    yield from prep_x_transpose(0, M0)
                    yield
                    yield from prep_q(0, M0)

                def keys():
                    for job in (prep_context, prep_k, prep_v):
                        yield from job(0)
                        yield

                return [queries(), keys()]

            s_count = 0
            s_banks = [S0 + i for i in range(NS)]

            def scores_max(b, h, qt, banks=s_banks):
                nonlocal s_count
                n = banks[s_count % len(banks)]
                s_count += 1
                i = b % 3
                pe.after(k_loaded[b], q_loaded[b], free[n])
                e = pe.run(nc.tensor.matmul(bank[n], qstack[i][0:mask_rows, h, qt * P:(qt + 1) * P],
                                            kstack[i][0:mask_rows, h // 2, :], start=True, stop=True))
                dve.after(e)
                free[n] = dve.run(nc.vector.tensor_reduce(negmax[:, b % 2, h, qt:qt + 1], bank[n], AX.X, ALU.max, negate=True))
                s_last[b, h // 8] = free[n]

            def max_parts(b, half):
                hs = slice(8 * half, 8 * half + 8)
                nm = negmax[:, b % 2, hs, :].rearrange("p h q -> p q h")
                mp = mparts[:, half]
                pool.after(s_last[b, half])
                e = pool.run(nc.gpsimd.tensor_copy(mp[:, :, 0, :], nm))
                pool.after(e)
                e = pool.run(nc.gpsimd.tensor_tensor(mrest[:, :, :], nm, mp[:, :, 0, :], ALU.subtract))
                pool.after(e)
                e = pool.run(nc.gpsimd.tensor_copy(mp[:, :, 1, :], mrest[:, :, :]))
                pool.after(e)
                mT_event[b, half] = pool.run(nc.gpsimd.tensor_tensor(mp[:, :, 2, :], mrest[:, :, :], mp[:, :, 1, :], ALU.subtract))

            def max_rows(b, half, n=M0):
                m16 = bank[n].bitcast(BF16)
                pe.after(mT_event[b, half], free[n])
                for qt in range(QT):
                    e = pe.run(nc.tensor.transpose(m16[0:24, qt * P:(qt + 1) * P],
                                                   mparts[:, half, qt].rearrange("p j h -> p (j h)"), ident16[:, :]))
                if n == M0:
                    yield
                act.after(e, m_loaded.get((b - 1, half)))
                free[n] = e = act.run(nc.scalar.activation(mT[:, half, :], m16[0:24, 0:SQ], ACT.Copy))
                sp.after(e)
                m_loaded[b, half] = ld_m[half].start(sp, qstack[b % 3][MAX_ROW:MAX_ROW + 3, 8 * half:8 * half + 8, :], mT[:, half, :])

            t_count = 0

            def scores_exp(b, tick):
                nonlocal t_count
                quad, g, c = tick // 8, 2 * (tick // 8) + tick % 2, tick % 8 // 2
                i = b % 3
                turn = (KC * b + quad) % 2
                n = T0 + t_count % NT
                t_count += 1
                pe.after(m_loaded[b, quad // 2], free[n])
                stack_read[b] = e = pe.run(nc.tensor.matmul(
                    bank[n], kstack[i][0:STACK, g, c * P:(c + 1) * P],
                    qstack[i][0:STACK, 2 * g:2 * g + 2, :].rearrange("p h q -> p (h q)"), start=True, stop=True))
                act.after(e, pv_done.get(KC * b + quad - 2))
                free[n] = exp_done[b, quad, g % 2, c] = act.run(nc.scalar.activation(prob[:, turn, g % 2, c, :], bank[n], ACT.Exp))

            def values(b, quad, c):
                turn = (KC * b + quad) % 2
                pe.after(exp_done[b, quad, 0, c], exp_done[b, quad, 1, c], v_ready[b])
                if c == 0 and quad % 2 == 0:
                    pe.after(free[O])
                for j in range(4):
                    h = 4 * quad + j
                    e = nc.tensor.matmul(bank[O][32 * j:32 * j + 32, (quad % 2) * SQ:(quad % 2 + 1) * SQ],
                                         vaug[:, KC * (b % 3) + c, h * VC:h * VC + 32],
                                         prob[:, turn, j // 2, c, (j % 2) * SQ:(j % 2 + 1) * SQ],
                                         start=c == 0, stop=c == KC - 1)
                    if j == 3:
                        pv_done[KC * b + quad] = e = pe.run(e)
                if c == KC - 1 and quad % 2 == 1:
                    half = quad // 2
                    act.after(e, o_read.get((b - 2, QT - 1)))
                    free[O] = o_copied[b, half] = act.run(nc.scalar.activation(oT[:, b % 2, half, :], bank[O], ACT.Copy))

            def out_tile(b, qt, n=M0):
                pe.after(o_copied[b, 0], o_copied[b, 1], free[n])
                for k in range(4):
                    o_read[b, qt] = e = pe.run(nc.tensor.transpose(
                        bank[n][:, k * P:(k + 1) * P], oT[:, b % 2, k // 2, (k % 2) * SQ + qt * P:(k % 2) * SQ + (qt + 1) * P], ident[:, :]))
                yield
                m = bank[n].rearrange("p (h v) -> p h v", v=32)
                dve.after(e)
                e = dve.run(nc.vector.reciprocal(rsum[:, qt, :], m[:, :, HD]))
                dve.after(e, o_step.get((b - 1, qt, "transposed")))
                free[n] = e = dve.run(nc.vector.tensor_tensor(
                    o_norm[:, qt, :].rearrange("p (h v) -> p h v", v=HD), m[:, :, 0:HD],
                    rsum[:, qt, :].unsqueeze(2).to_broadcast([P, H, HD]), ALU.mult))
                yield
                yield
                pe.after(e, free[n])
                e = o_step[b, qt, "transposed"] = pe.run(nc.tensor.transpose(bank[n][:, 0:P], o_norm[:, qt, :], ident[:, :]))
                yield
                act.after(e, o_step.get((b - 1, qt, "product")))
                free[n] = e = act.run(nc.scalar.activation(o_normT[:, qt, :], bank[n][:, 0:P], ACT.Copy))
                yield
                yield
                pe.after(e, free[n])
                e = o_step[b, qt, "product"] = pe.run(nc.tensor.matmul(bank[n][:, 0:D], o_normT[:, qt, :], wo[:, :], start=True, stop=True))
                yield
                dve.after(e, x_free[b])
                free[n] = o_step[b, qt, "added"] = dve.run(nc.vector.tensor_tensor(
                    x[:, QT * b + qt, :], bank[n][:, 0:D], x[:, QT * b + qt, :], ALU.add))

            normalised = {}

            def next_ln(b):
                e = ln_statistics([QT * b, QT * b + 1], o_step[b, 1, "added"])
                yield
                yield
                normalised[b] = ln_apply(dve if b == B - 1 else pool, [QT * b, QT * b + 1], 2, e, xn_read[1])
                yield

            def next_transpose(b, n=M0):
                e = normalised[b]
                pe.after(e, free[n])
                for i in range(QT):
                    e = pe.run(nc.tensor.transpose(bank[n][:, i * P:(i + 1) * P], xn[:, 2 + i, :], ident[:, :]))
                xn_read[1] = e
                cols = slice(b * SQ, (b + 1) * SQ)
                yield
                act.after(e)
                a = act.run(nc.scalar.activation(xT[:, 0, cols], bank[n][:, 0:SQ], ACT.Copy))
                yield
                dve.after(e, a)
                free[n] = next_ready[b] = dve.run(nc.vector.tensor_tensor(
                    xT[:, 1, cols], bank[n][:, 0:SQ], xT[:, 0, cols].bitcast(FP32), ALU.subtract))

            next_ready = {}

            def wait(n):
                for _ in range(n):
                    yield

            def m0_jobs(b):
                if 0 <= b < B:
                    yield
                    yield from max_rows(b, 1)
                elif b < 0:
                    yield
                if b == B:
                    n = M1 if layer else SIDE
                    for job in (next_transpose(b - 2, n), out_tile(b - 1, 0, n), out_tile(b - 1, 1, n), next_ln(b - 1), next_transpose(b - 1, n)):
                        yield from job
                        yield
                    return
                if b >= 1:
                    if b >= 2:
                        yield from wait(TRANSPOSE_AT)
                        yield from next_transpose(b - 2)
                        yield from wait(5 - TRANSPOSE_AT)
                    else:
                        yield from wait(7)
                    yield from out_tile(b - 1, 0)
                    yield
                if b + 1 < B:
                    yield from wait(0 if b >= 1 else 16)
                    while (b + 1, 0) not in mT_event:
                        yield
                    yield
                    yield from max_rows(b + 1, 0)
                    yield
                if b >= 1:
                    yield from out_tile(b - 1, 1)
                    yield
                    yield from next_ln(b - 1)

            units = [(h, qt) for h in range(H) for qt in range(QT)]

            def before_heads():
                jobs = [prep(0)]
                while jobs or side:
                    advance(jobs)
                    advance(side)
                    yield
                jobs = [prep(1)]
                for tick in range(8):
                    advance(jobs)
                    yield
                for tick in range(32):
                    scores_max(0, *units[tick], banks=[SIDE])
                    if tick == 17:
                        max_parts(0, 0)
                    if tick == 22:
                        list(max_rows(0, 0, SIDE))
                    advance(jobs)
                    advance(side)
                    yield
                while jobs or side:
                    advance(jobs)
                    advance(side)
                    yield

            def heads():
                for b in range(-1 if layer == 0 else 0, B):
                    jobs, fast = [m0_jobs(b)], []
                    if b == -1:
                        fast = first_prep()
                        while fast or side:
                            advance(fast)
                            advance(side)
                        fast = [prep(1)]
                    elif b + 2 < B:
                        fast = [prep(b + 2)]
                    if b == B - 1:
                        prepared = [(q.sem, q.count) for q in engines if q.count]
                    if layer == 0 and b == B - 1:
                        router["parts"] = split(rt_nat[:, :], rt_w[:, 0, :], rt_w[:, 1, :], loads["weights"])
                        fast.append(itertools.chain(*(routing(blk, next_ready, S0, ACT.Exp) for blk in range(ROUTED_EARLY))))
                    if b == 0:
                        load_ffn_weights(layer)
                    for tick in range(32):
                        if b + 1 < B:
                            scores_max(b + 1, *units[tick])
                        if tick == 0 and 0 <= b < B:
                            max_parts(b, 1)
                        if 0 <= b < B:
                            scores_exp(b, tick)
                        if tick % 2:
                            if tick < 8 and b >= 1:
                                values(b - 1, 3, tick // 2)
                            elif tick >= 8 and 0 <= b < B:
                                values(b, tick // 8 - 1, tick % 8 // 2)
                        if tick == 16 and b + 1 < B:
                            max_parts(b + 1, 0)
                        advance(jobs)
                        advance(side)
                        advance(fast)
                        if tick in EXTRA_STEPS[layer]:
                            advance(side)
                            advance(fast)
                    while jobs or side or fast:
                        advance(jobs)
                        advance(fast)
                        advance(side)
                for c in range(KC):
                    values(B - 1, 3, c)
                return next_ready, m0_jobs(B), pv_done[KC * B - 1], prepared

            if layer == 1:
                yield from before_heads()
            return heads

        loads = {}

        def load_ffn_weights(layer):
            if layer == 0:
                ld_ffn.start(sp, rt_nat[:, :], A["L0_router"])
                ld_ffn.start(sp, gate_bias[:, :], A["L0_ffn_gate_bias"].partition_broadcast(P))
                ld_ffn.start(sp, e_nat[:, :, :, :], A["L0_gu"])
                loads["weights"] = ld_ffn.start(sp, down0[:, :, :], A["L0_down"])
                return
            pre = "L1_ffn_"
            ld_ffn.start(sp, rt_nat[:, 0:E1], A["L1_ffn_router_DE"])
            ld_ffn.start(sp, w_nat[:, :, :, :], A["L1_gu"])
            for c, (f0, fn) in enumerate(FC):
                ld_ffn.start(sp, down1[0:fn, 0:E1, c, :], A[pre + "w2_eFD"][:, f0:f0 + fn, :].rearrange("e f d -> f e d"))
                loads["weights"] = ld_ffn.start(sp, down1[0:fn, E1, c, :], A[pre + "ws2_FD"][f0:f0 + fn, :])
            loads["rows_in"] = ld_empty.start(sp, rows_in, A["c_rows"])

        def router_logits(n, tiles, xT_ready, experts, w_ready):
            pe.after(free[n], w_ready)
            for i, t in enumerate(tiles):
                pe.after(xT_ready[t // QT])
                tok = slice(t * P, (t + 1) * P)
                e = parts3(bank[n][:, i * experts:(i + 1) * experts], xT[:, 0, tok], xT[:, 1, tok],
                           rt_w[:, 0, 0:experts], rt_w[:, 1, 0:experts])
            return e

        class Blocks:

            def __init__(self, silu, hid, yT):
                self.silu, self.hid, self.yT = silu, hid, yT
                self.n, self.waiting, self.sums, self.y_read = 0, None, {}, None
                self.silu_read, self.hid_read = [None, None], [None] * 3

            def unit(self, blk, rows, gu, x_ready, weight, down, first, last, background=iter(())):
                i, h = self.n % 2, self.n % 3
                self.n += 1
                silu, hid = self.silu[0:rows, i, :], self.hid[0:rows, h, :]
                cols = slice(blk * BLK, (blk + 1) * BLK)
                pe.after([x_ready[b] for b in range(BLK * blk // SQ, BLK * (blk + 1) // SQ)], free[i])
                g = parts3(bank[i][0:rows, :], gu[0][0], gu[0][1], xT[:, 0, cols], xT[:, 1, cols])
                next(background, None)
                pe.after(free[2 + i])
                u = parts3(bank[2 + i][0:rows, :], gu[1][0], gu[1][1], xT[:, 0, cols], xT[:, 1, cols])
                if weight is not None:
                    pe.after(free[WEIGHT])
                    w = pe.run(nc.tensor.matmul(bank[WEIGHT], weight, wT[:, cols], start=True, stop=True))
                self.flush()
                act.after(g, self.silu_read[i])
                free[i] = s = act.run(nc.scalar.activation(silu, bank[i][0:rows, :], ACT.Silu))
                dve.after(s, u, self.hid_read[h])
                free[2 + i] = self.silu_read[i] = e = dve.run(nc.vector.tensor_tensor(hid, bank[2 + i][0:rows, :], silu, ALU.mult))
                if weight is not None:
                    dve.after(e, w)
                    free[WEIGHT] = e = dve.run(nc.vector.tensor_tensor(hid, bank[WEIGHT], hid, ALU.mult))
                self.waiting = (blk, rows, h, e, down, first, last)

            def flush(self):
                if self.waiting is None:
                    return
                blk, rows, h, ready, down, first, last = self.waiting
                self.waiting = None
                pe.after(ready)
                if first:
                    pe.after(free[SUM])
                self.hid_read[h] = e = pe.run(nc.tensor.matmul(bank[SUM], down, self.hid[0:rows, h, :], start=first, stop=last))
                if last:
                    act.after(e, self.y_read)
                    free[SUM] = self.sums[blk] = act.run(nc.scalar.activation(self.y(blk), bank[SUM], ACT.Copy))

            def y(self, blk):
                return self.yT[:, blk % self.yT.shape[1], :]

            def finish(self, blk):
                pe.after(self.sums[blk], free[SIDE])
                for k in range(BT):
                    e = pe.run(nc.tensor.transpose(bank[SIDE][:, k * P:(k + 1) * P], self.y(blk)[:, k * P:(k + 1) * P], ident[:, :]))
                self.y_read = e
                dve.after(e)
                xs = x[:, BT * blk:BT * blk + BT, :].rearrange("p t d -> p (t d)")
                free[SIDE] = dve.run(nc.vector.tensor_tensor(xs, bank[SIDE], xs, ALU.add))
                return free[SIDE]

        router, weights = {}, {}

        def routing(blk, xT_ready, n, function):
            w, r, scores, choice, masked, found = (route[:, i, :, :] for i in range(6))
            sel = found
            logits = bank[n][:, 0:BT * E0].rearrange("p (t e) -> p t e", e=E0)
            act.after(router_logits(n, range(BT * blk, BT * blk + BT), xT_ready, E0, router["parts"]), weights.get(blk - 1))
            if function == ACT.Sigmoid:
                free[n] = e = act.run(nc.scalar.activation(scores, logits, ACT.Sigmoid))
            else:
                free[n] = e = act.run(nc.scalar.activation(scores, logits, ACT.Exp, scale=-1.0))
                yield
                dve.after(e)
                e = dve.run(nc.vector.tensor_scalar(scores, scores, 1.0, None, ALU.add))
                dve.after(e)
                e = dve.run(nc.vector.reciprocal(scores, scores))
            yield
            dve.after(e)
            e = dve.run(nc.vector.tensor_tensor(choice, scores, gate_bias[:, :].unsqueeze(1).to_broadcast([P, BT, E0]), ALU.add))
            dve.after(e)
            for t in range(BT):
                for g in range(GROUPS):
                    e = dve.run(nc.vector.max(found[:, t, 8 * g:8 * g + 8], choice[:, t, 8 * g:8 * g + 8]))
                if t % 2:
                    yield
            dve.after(e)
            gs = small[:, 0, :, 0:4]
            f4 = found.rearrange("p t (g k) -> p t g k", k=8)
            e = dve.run(nc.vector.tensor_tensor(gs, f4[:, :, :, 0], f4[:, :, :, 1], ALU.add))
            dve.after(e)
            sh = [P, BT, 4, 4]
            mine = gs.unsqueeze(3).to_broadcast(sh)
            other = gs.unsqueeze(2).to_broadcast(sh)
            c4 = [small[:, i, :, :].rearrange("p t (a b) -> p t a b", b=4) for i in range(1, 4)]
            dve.run(nc.vector.tensor_tensor(c4[0], other, mine, ALU.is_gt))
            e = dve.run(nc.vector.tensor_tensor(c4[1], other, mine, ALU.is_equal))
            yield
            dve.after(e, order_ready)
            e = dve.run(nc.vector.tensor_tensor(small[:, 2, :, :], small[:, 2, :, :],
                                                order[:, COLUMNS["groups_before"]].unsqueeze(1).to_broadcast([P, BT, 16]), ALU.mult))
            dve.after(e)
            e = dve.run(nc.vector.tensor_tensor(small[:, 3, :, :], small[:, 1, :, :], small[:, 2, :, :], ALU.add))
            dve.after(e)
            e = dve.run(nc.vector.tensor_reduce(small[:, 4, :, 0:4], c4[2], AX.X, ALU.add))
            yield
            dve.after(e)
            e = dve.run(nc.vector.tensor_scalar(small[:, 5, :, 0:4], small[:, 4, :, 0:4], 2.0, None, ALU.is_lt))
            dve.after(e)
            e = dve.run(nc.vector.tensor_tensor(masked.rearrange("p t (g k) -> p t g k", k=8), choice.rearrange("p t (g k) -> p t g k", k=8),
                                                small[:, 5, :, 0:4].unsqueeze(3).to_broadcast([P, BT, 4, 8]), ALU.mult))
            dve.after(e)
            e = dve.run(nc.vector.tensor_scalar(masked, masked, 0.0, None, ALU.add))
            yield
            dve.after(e)
            for t in range(BT):
                e = dve.run(nc.vector.max(small[:, 0, t, 8:16], masked[:, t, :]))
            dve.after(e)
            for t in range(BT):
                e = dve.run(nc.vector.match_replace(sel[:, t, :], small[:, 0, t, 8:16], masked[:, t, :], -BIG))
            yield
            dve.after(e)
            e = dve.run(nc.vector.scalar_tensor_tensor(sel, sel, -BIG, scores, ALU.is_equal, ALU.mult))
            dve.after(e)
            tot = small[:, 1, :, 0]
            e = dve.run(nc.vector.tensor_reduce(tot, sel, AX.X, ALU.add))
            dve.after(e)
            e = dve.run(nc.vector.tensor_scalar(tot, tot, 1e-20, None, ALU.add))
            yield
            dve.after(e)
            e = dve.run(nc.vector.reciprocal(tot, tot))
            dve.after(e)
            e = dve.run(nc.vector.tensor_scalar(tot, tot, 2.5, None, ALU.mult))
            dve.after(e)
            e = dve.run(nc.vector.tensor_tensor(w, sel, small[:, 1, :, 0:1].to_broadcast([P, BT, E0]), ALU.mult))
            yield
            dve.after(e, weights.get(blk - 1))
            e = dve.run(nc.vector.tensor_copy(wparts[:, :, 0, :], w))
            dve.after(e)
            e = dve.run(nc.vector.tensor_tensor(r, w, wparts[:, :, 0, :], ALU.subtract))
            dve.after(e)
            e = dve.run(nc.vector.tensor_copy(wparts[:, :, 1, :], r))
            dve.after(e)
            e = dve.run(nc.vector.tensor_tensor(wparts[:, :, 2, :], r, wparts[:, :, 1, :], ALU.subtract))
            yield
            yield
            yield
            b16 = bank[n].bitcast(BF16)
            pe.after(e, free[n])
            for i in range(BT):
                e = pe.run(nc.tensor.transpose(b16[0:96, i * P:(i + 1) * P], wparts[:, i].rearrange("p j h -> p (j h)"), ident16[:, :]))
            act.after(e)
            free[n] = weights[blk] = act.run(nc.scalar.activation(wT[:, blk * BLK:(blk + 1) * BLK], b16[0:96, 0:BLK], ACT.Copy))

        def ffn_0(xT_ready, last_heads, prob_read, background, done):
            w_loaded = loads["weights"]
            for q in (act, dve, sp):
                q.after(prob_read)
            sel_loaded = ld_w.start(sp, sel0[:, :, :], A["c_sel0"].bitcast(BF16))
            w_ready = {}

            def split_weights(u):
                nat, hi = e_nat[:, u, :, :], eh[:, u, :, :]
                act.after(w_loaded)
                a = act.run(nc.scalar.activation(hi, nat, ACT.Copy))
                dve.after(w_loaded, a)
                w_ready[u] = dve.run(nc.vector.tensor_tensor(e_lo[:, u, :, :], nat, hi.bitcast(FP32), ALU.subtract))

            blocks = Blocks(silu0, hid0, yT0)
            split_weights(EP)
            jobs = [itertools.chain(last_heads, *(routing(blk, xT_ready, SIDE, ACT.Sigmoid) for blk in range(ROUTED_EARLY, NB)))]
            for blk in range(NB):
                for n, u in enumerate([EP] + list(range(EP))):
                    if blk == 0 and n < EP:
                        split_weights(n)
                    if n == 1:
                        pe.after(weights[blk], sel_loaded)
                    pe.after(w_ready[u])
                    gu = [[part[:, u, i, :] for part in (eh, e_lo)] for i in range(2)]
                    blocks.unit(blk, P, gu, xT_ready, sel0[:, u, :] if u < EP else None, down0[:, u, :], n == 0, n == EP, background)
                    if n == 2 and blk:
                        done[blk - 1] = blocks.finish(blk - 1)
                    advance(jobs)
                    if blk == 0:
                        advance(jobs)
                    next(background, None)
            blocks.flush()
            done[NB - 1] = blocks.finish(NB - 1)
            list(background)

        def ffn_1(xT_ready, last_heads, heads_done, prepared):
            w_loaded = loads["weights"]
            for q in engines:
                q.after(prepared)
            rw = split(rt_nat[:, 0:E1], rt_w[:, 0, 0:E1], rt_w[:, 1, 0:E1], w_loaded)

            def split_weights(u):
                return split(w_nat[:, u, :, :], gu1[:, u, :, 0, :], gu1[:, u, :, 1, :], w_loaded)

            shared_ready = split_weights(E1)
            blocks = Blocks(silu1, hid1, yT1)
            pe.after(w_loaded, shared_ready)
            done, last = {}, [last_heads]
            dve.after(heads_done)
            act.after(heads_done)

            def shared_unit(n):
                blk, c = n // len(FC), n % len(FC)
                f0, fn = FC[c]
                gu = [[gu1[:, E1, i, j, f0:f0 + fn] for j in range(2)] for i in range(2)]
                blocks.unit(blk, fn, gu, xT_ready, None, down1[0:fn, E1, c, :], c == 0, c == len(FC) - 1)

            for n in range(SHARED_EARLY):
                shared_unit(n)
                for _ in range(3):
                    advance(last)
            while last:
                advance(last)
            turned_logits = []
            for blk in range(NB):
                n = (WEIGHT, M1)[blk % 2]
                pe.after([xT_ready[b] for b in range(BLK * blk // SQ, BLK * (blk + 1) // SQ)], rw, free[n])
                cols = slice(blk * BLK, (blk + 1) * BLK)
                e = parts3(bank[n][0:E1, :], rt_w[:, 0, 0:E1], rt_w[:, 1, 0:E1], xT[:, 0, cols], xT[:, 1, cols])
                act.after(e)
                free[n] = lt = act.run(nc.scalar.activation(logitsT1[:, blk, :], bank[n][0:E1, :], ACT.Copy))
                turned_logits.append(lt)
            for t in range(TT):
                pe.after(turned_logits[t // BT], free[SIDE])
                e = pe.run(nc.tensor.transpose(bank[SIDE][:, t * E1:(t + 1) * E1], logitsT1[:, t // BT, t % BT * P:(t % BT + 1) * P], ident[0:E1, 0:E1]))
            act.after(e)
            scores, eq, sel = (choice1[:, i, :, :] for i in range(3))
            gates, rank = choice1[:, 3, :, :], choice1[:, 4, :, :]
            e = act.run(nc.scalar.activation(scores, bank[SIDE][:, 0:TT * E1].rearrange("p (t e) -> p t e", e=E1), ACT.Copy))
            act.after(e)
            free[SIDE] = g = act.run(nc.scalar.activation(gates, scores, ACT.Sigmoid))
            dve.after(e)
            best, gate, place = (per_token[:, i, :].unsqueeze(2) for i in range(3))

            def over_experts(out, in_, op, ready):
                dve.after(ready)
                return dve.run(nc.vector.tensor_reduce(out.rearrange("p t o -> p (t o)"), in_, AX.X, op))

            e = over_experts(best, scores, ALU.max, e)
            dve.after(e)
            e = dve.run(nc.vector.tensor_tensor(eq, scores, best.to_broadcast([P, TT, E1]), ALU.is_equal))
            dve.after(e)
            e = dve.run(nc.vector.tensor_tensor(eq, eq, order[:, COLUMNS["precedence"]].unsqueeze(1).to_broadcast([P, TT, E1]), ALU.mult))
            e = over_experts(best, eq, ALU.max, e)
            dve.after(e)
            chosen = dve.run(nc.vector.tensor_tensor(sel, eq, best.to_broadcast([P, TT, E1]), ALU.is_equal))
            dve.after(chosen, g)
            sel16_ready = dve.run(nc.vector.tensor_copy(sel16[:, :, :], sel))
            e = dve.run(nc.vector.tensor_tensor(gates, gates, sel, ALU.mult))
            e = over_experts(gate, gates, ALU.add, e)
            dve.after(e)
            gate_ready = dve.run(nc.vector.tensor_tensor(gate.rearrange("p t o -> p (t o)"), gate.rearrange("p t o -> p (t o)"), rstd[:, 2, :], ALU.mult))

            shared_unit(SHARED_EARLY)
            ranks = bank[WEIGHT][:, 0:TT * E1].rearrange("p (t e) -> p t e", e=E1)
            totals = bank[WEIGHT][:, TT * E1:(TT + 1) * E1]
            pe.after(sel16_ready, free[WEIGHT], order_ready)
            nc.tensor.matmul(ranks, before16[:, 0, :], sel16[:, :, :], start=True, stop=False)
            for k in range(1, TT):
                nc.tensor.matmul(ranks[:, k:TT, :], before16[:, 1, :], sel16[:, 0:TT - k, :], start=False, stop=k == TT - 1)
            for t in range(TT):
                e = nc.tensor.matmul(totals, before16[:, 1, :], sel16[:, t, :], start=t == 0, stop=t == TT - 1)
            counted = pe.run(e)
            steps = order[:, COLUMNS["full_tiles"]].unsqueeze(1).to_broadcast([P, E1, TT])
            before = order[:, COLUMNS["experts_before"]].rearrange("p (a b) -> p a b", b=E1)
            numbers = order[:, COLUMNS["tile"]]
            tiles_of, first_tile, end_tile = (plan[:, i, 0:E1] for i in range(3))
            grid = plan[:, 3:5, :].rearrange("p a b -> p (a b)")
            dve.after(counted)
            g3 = grid[:, 0:E1 * TT].rearrange("p (e k) -> p e k", k=TT)
            e = dve.run(nc.vector.tensor_tensor(g3, totals.unsqueeze(2).to_broadcast([P, E1, TT]), steps, ALU.is_gt))
            dve.after(e)
            e = dve.run(nc.vector.tensor_reduce(tiles_of, g3, AX.X, ALU.add))
            dve.after(e)
            g3 = grid[:, 0:E1 * E1].rearrange("p (a b) -> p a b", b=E1)
            e = dve.run(nc.vector.tensor_tensor(g3, tiles_of.unsqueeze(1).to_broadcast([P, E1, E1]), before, ALU.mult))
            dve.after(e)
            e = dve.run(nc.vector.tensor_reduce(first_tile, g3, AX.X, ALU.add))
            dve.after(e)
            free[WEIGHT] = r = dve.run(nc.vector.scalar_tensor_tensor(rank, first_tile.unsqueeze(1).to_broadcast([P, TT, E1]), float(P), ranks, ALU.mult, ALU.add))
            e = dve.run(nc.vector.tensor_tensor(end_tile, first_tile, tiles_of, ALU.add))
            dve.after(r)
            r = dve.run(nc.vector.tensor_tensor(rank, rank, sel, ALU.mult))
            r = over_experts(place, rank, ALU.add, r)
            dve.after(r)
            placed = dve.run(nc.vector.tensor_copy(row_of[:, :], place.rearrange("p t o -> p (t o)")))
            e2 = dve.run(nc.vector.tensor_copy(gx[:, :, D], order[:, COLUMNS["token"]]))
            dve.after(gate_ready)
            to_rows = transfers("sorted")
            pool.after(placed, e2, loads["rows_in"])
            for t in range(TT):
                pool.after(dve.run(nc.vector.tensor_scalar(gx[:, t, 0:D], x[:, t, :], mv[:, t, 0:1], per_token[:, 1, t:t + 1], ALU.subtract, ALU.mult)))
                sorted_ = to_rows.scatter(pool, rows_in, row_of[:, t:t + 1], gx[:, t, :])
                if t == 3:
                    dve.after(e)
                    g3 = grid[:, 0:TILES * (E1 - 1)].rearrange("p (j e) -> p j e", e=E1 - 1)
                    i = dve.run(nc.vector.tensor_tensor(g3, end_tile[:, 0:E1 - 1].unsqueeze(1).to_broadcast([P, TILES, E1 - 1]),
                                                        numbers.unsqueeze(2).to_broadcast([P, TILES, E1 - 1]), ALU.is_le))
                    dve.after(i)
                    i = dve.run(nc.vector.tensor_reduce(plan[:, 5, 0:TILES], g3, AX.X, ALU.add))
                    dve.after(i)
                    experts_known = dve.run(nc.vector.tensor_copy(expert_of[:, :], plan[:, 5, 0:TILES]))
            groups = [range(g, min(g + 4, TILES)) for g in range(0, TILES, 4)]
            sp.after(sorted_)
            loaded = []
            for i, g in enumerate(groups):
                loaded.append(ld_rows[i].start(sp, rows[:, g[0]:g[-1] + 1, :], rows_in.rearrange("(t p) d -> p t d", p=P)[:, g[0]:g[-1] + 1, :]))
            for n in range(SHARED_EARLY + 1, NB * len(FC)):
                shared_unit(n)
                for u in range(2 * (n - SHARED_EARLY - 1), min(2 * (n - SHARED_EARLY), E1)):
                    w_ready = split_weights(u)
                if len(done) in blocks.sums:
                    done[len(done)] = blocks.finish(len(done))
            blocks.flush()
            while len(done) < NB:
                done[len(done)] = blocks.finish(len(done))

            turned, numbers_known = {}, {}
            pe.after(w_ready, experts_known)

            def turn(i):
                g = groups[i]
                n = len(g) * P
                pe.after(loaded[i], free[WEIGHT])
                for k, j in enumerate(g):
                    e = pe.run(nc.tensor.transpose(bank[WEIGHT][:, k * P:(k + 1) * P], rows[:, j, 0:D], ident[:, :]))
                act.after(e, gu_done.get(groups[i - 2][-1]) if i > 1 else None)
                a = act.run(nc.scalar.activation(gxT[:, i % 2, 0, 0:n], bank[WEIGHT][:, 0:n], ACT.Copy))
                dve.after(e, a)
                free[WEIGHT] = turned[i] = dve.run(nc.vector.tensor_tensor(gxT[:, i % 2, 1, 0:n], bank[WEIGHT][:, 0:n], gxT[:, i % 2, 0, 0:n].bitcast(FP32), ALU.subtract))
                numbers_known[i] = dve.run(nc.vector.tensor_copy(token_of[:, g[0]:g[-1] + 1], rows[:, g[0]:g[-1] + 1, D]))

            gu_done, hid_ready, hidT_ready, hidT_read, hid_read, expert = {}, {}, {}, {}, {}, {}
            scattered = transfers("scattered")
            F = slice(0, F1)

            def gate_up(j):
                i, k, m = j // 4, j % 4, j % 2
                expert[j] = ev = nc.tensor.value_load(expert_of[0:1, j:j + 1], min_val=0, max_val=E1 - 1)
                pe.after(turned[i])
                xs = [gxT[:, i % 2, part, k * P:(k + 1) * P] for part in range(2)]
                for which, n in ((0, m), (1, 2 + m)):
                    w = [gu1[:, bass.ds(ev, 1), which, part, :].rearrange("p o f -> p (o f)") for part in range(2)]
                    pe.after(free[n])
                    e = parts3(bank[n][:, F], xs[0], xs[1], w[0], w[1])
                    if which == 0:
                        act.after(e, hid_ready.get(j - 2))
                        free[n] = s = act.run(nc.scalar.activation(silu1[:, m, F], bank[n][:, F], ACT.Silu))
                gu_done[j] = e
                dve.after(e, s, hid_read.get(j - 2))
                free[n] = hid_ready[j] = dve.run(nc.vector.tensor_tensor(mid[:, m, F], bank[n][:, F], silu1[:, m, F], ALU.mult))

            def turn_hidden(j):
                m = j % 2
                pe.after(hid_ready[j], free[SIDE])
                for c, (f0, fn) in enumerate(FC):
                    e = pe.run(nc.tensor.transpose(bank[SIDE][0:fn, c * P:(c + 1) * P], mid[:, m, f0:f0 + fn], ident[:, :]))
                hid_read[j] = e
                act.after(e, hidT_read.get(j - 2))
                a = act.run(nc.scalar.activation(hid1[:, m, 0:2 * P], bank[SIDE][:, 0:2 * P], ACT.Copy))
                dve.after(e, a)
                d = dve.run(nc.vector.tensor_copy(hid1[0:FC[2][1], m, 2 * P:3 * P], bank[SIDE][0:FC[2][1], 2 * P:3 * P]))
                free[SIDE] = hidT_ready[j] = d

            def down(j):
                i, k = j // 4, j % 4
                n = 6 + i % 2
                pe.after(hidT_ready[j])
                if k == 0:
                    pe.after(free[n])
                for c, (f0, fn) in enumerate(FC):
                    w2 = down1[0:fn, bass.ds(expert[j], 1), c, :].rearrange("p o f -> p (o f)")
                    e = nc.tensor.matmul(bank[n][:, k * P:(k + 1) * P], hid1[0:fn, j % 2, c * P:(c + 1) * P], w2, start=c == 0, stop=c == 2)
                hidT_read[j] = e = pe.run(e)
                if j == groups[i][-1]:
                    g = groups[i]
                    act.after(e, turned[i])
                    free[n] = a = act.run(nc.scalar.activation(rows[:, g[0]:g[-1] + 1, 0:D], bank[n][:, 0:len(g) * P].rearrange("p (t d) -> p t d", d=P), ACT.Copy))
                    pool.after(a, numbers_known[i])
                    for t in g:
                        back = scattered.scatter(pool, rows_out, token_of[:, t:t + 1], rows[:, t, 0:D])
                    return back

            turn(0)
            for j in range(TILES + 2):
                if j < TILES:
                    gate_up(j)
                if j % 4 == 1 and j // 4 + 1 < len(groups):
                    turn(j // 4 + 1)
                if 0 <= j - 1 < TILES:
                    turn_hidden(j - 1)
                if j >= 2:
                    back = down(j - 2) or back if j > 2 else down(0)
            sp.after(back)
            for blk in range(NB):
                ts = slice(4 * blk, 4 * blk + 4)
                e = ld_back[blk].start(sp, gx[:, ts, 0:D], rows_out.rearrange("(t p) d -> p t d", p=P)[:, ts, :])
                dve.after(e, done[blk])
                done[blk] = dve.run(nc.vector.tensor_tensor(x[:, ts, :], gx[:, ts, 0:D], x[:, ts, :], ALU.add))
            return done

        x_loaded, layer0_done = {"first": x0_ready}, {}
        xT_ready, last_heads, prob_read, _ = to_the_end(xattn(0, x_loaded))()
        start_1 = {}

        def layer1_start():
            yield from itertools.repeat(None, LAYER1_AT)
            attention_done = [(q.sem, q.count) for q in engines if q.count]
            sp.after(attention_done)
            pool.after(attention_done)
            start_1["heads"] = yield from xattn(1, layer0_done)

        ffn_0(xT_ready, last_heads, prob_read, layer1_start(), layer0_done)
        everybody()
        done = ffn_1(*start_1["heads"]())
        st = transfers("store")
        for blk in range(NB):
            sp.after(done[blk])
            stored = st.start(sp, out[:, 4 * blk:4 * blk + 4, :], x[:, 4 * blk:4 * blk + 4, :])
        sp.after(stored)


def constants():
    import numpy as np
    ident = np.eye(P, dtype=np.float32)
    experts = np.arange(E1)
    order = [(np.arange(GROUPS)[None, :] < np.arange(GROUPS)[:, None]).reshape(-1),
             E1 - experts,
             P * np.arange(TT),
             (experts[None, :] < experts[:, None]).reshape(-1),
             np.arange(TILES)]
    order = np.concatenate([np.tile(np.concatenate(order), (P, 1)),
                            np.arange(P)[:, None] + P * np.arange(TT)[None, :]], 1).astype(np.float32)
    rows = np.zeros((TILES * P, D + 1), np.float32)
    rows[:, D] = T + np.arange(TILES * P)
    before = np.stack([np.arange(P)[:, None] < np.arange(P)[None, :], np.ones((P, P), bool)], 1) * np.uint16(0x3F80)
    sel0 = np.zeros((96, EP, P), np.uint16)
    for part in range(3):
        for e in range(E0):
            sel0[32 * part + e, e // 2, 64 * (e % 2):64 * (e % 2) + 64] = 0x3F80
    half = np.arange(0, HD, 2, dtype=np.float32) / np.float32(HD)
    inv = (np.float32(1.0) / np.power(np.float32(10000.0), half)).astype(np.float32)
    angle = (np.arange(SK, dtype=np.float32)[:, None] * inv[None, :]).astype(np.float32)
    rope = np.zeros((P, 2, SK), np.float32)
    for row in range(P):
        d = row % 64 // PAIRS
        a = angle[:, d % (HD // 2)].astype(np.float64)
        rope[row, 0] = np.cos(a)
        rope[row, 1] = np.sin(a) * (-1.0 if d < HD // 2 else 1.0)
    return {"c_ones": np.full((STACK - MASK_ROW, H * SQ), 0x3F80, np.uint16), "c_ident": ident, "c_order": order, "c_sel0": sel0, "c_before": before, "c_rows": rows, "c_rope": rope}


def laid_out(a):
    import numpy as np
    a = {k: np.asarray(v) for k, v in a.items()}

    def tiles(v):
        return v.reshape(TT, P, D).transpose(1, 0, 2)

    def stacked(w):
        return w.reshape(*w.shape[:-1], PAIRS, 2, HD).swapaxes(-3, -2).swapaxes(-2, -1).reshape(w.shape)

    def half(w):
        return np.roll(w.reshape(*w.shape[:-1], H, HD), HD // 2, axis=-1).reshape(w.shape)

    r = {"x": tiles(a["x"]), "ctxT": a["ctx_1024"].reshape(-1, D).T, "mask": a["mask_Bx1x1xS2_ff0"].reshape(B, SK)}
    for layer, names in ((0, ["wq", "wk", "wv", "wo"]), (1, ["Wq", "Wk", "Wv", "Wo"])):
        pre = f"L{layer}_xattn_"
        wq, wk, wv, wo = (a[pre + n] if layer == 0 else a[pre + n].T for n in names)
        bq, bk = a[pre + "bq"], a[pre + "bk"]
        r[f"L{layer}_w"] = np.stack([stacked(wq), stacked(wk), stacked(half(wq)), stacked(half(wk)), wv], 1)
        r[f"L{layer}_b"] = np.stack([stacked(bq), stacked(bk), stacked(half(bq)), stacked(half(bk))], 1)
        r[f"L{layer}_wo"], r[f"L{layer}_bv"], r[f"L{layer}_bo"] = wo, a[pre + "bv"], a[pre + "bo"]
    pre = "L0_ffn_"
    gu = [np.concatenate([a[pre + "expert_" + n].reshape(EP, P, D), a[pre + "shared_" + n][None]]) for n in ("gate", "up")]
    r["L0_gu"] = np.stack(gu, 1).transpose(3, 0, 1, 2)
    down = a[pre + "expert_down"].transpose(0, 2, 1).reshape(EP, P, D)
    r["L0_down"] = np.concatenate([down, a[pre + "shared_down"].T[None]]).transpose(1, 0, 2)
    r["L0_router"], r[pre + "gate_bias"] = a[pre + "gate_w"].T, a[pre + "gate_bias"]
    pre = "L1_ffn_"
    gu = [np.concatenate([a[pre + f"w{n}_eDF"], a[pre + f"ws{n}_DF"][None]]) for n in (1, 3)]
    r["L1_gu"] = np.stack(gu, 1).transpose(2, 0, 1, 3)
    for n in ("w2_eFD", "ws2_FD", "router_DE"):
        r[pre + n] = a[pre + n]
    return r


def kernel(**inputs):
    import numpy as np
    import concourse.bacc as bacc
    from concourse.bass_utils import run_bass_kernel_spmd

    nc = bacc.Bacc("TRN2", target_bir_lowering=False, num_devices=1)
    arrays, aps = {}, {}
    for name, value in {**laid_out(inputs), **constants()}.items():
        a = np.ascontiguousarray(value)
        arrays[f"in_{name}"] = a
        aps[name] = nc.dram_tensor(f"in_{name}", a.shape, mybir.dt.from_np(a.dtype), kind="ExternalInput").ap()
    out = nc.dram_tensor("out_x", (P, TT, D), FP32, kind="ExternalOutput").ap()
    build(nc, aps, out)
    r = run_bass_kernel_spmd(nc, [arrays], core_ids=[0])
    return r.results[0]["out_x"].transpose(1, 0, 2).reshape(B, SQ, D)
```
